# Optimizing a Trainium2 kernel written in Bass

```python
import numpy as np
import jax
import jax.numpy as jnp

def _softmax(x, axis=-1):
    return jax.nn.softmax(x, axis=axis)

def _gelu(x):
    return jax.nn.gelu(x, approximate=True)

def _silu(x):
    return jax.nn.silu(x)

def _sigmoid(x):
    return jax.nn.sigmoid(x)

def _layernorm(x, axis=-1, eps=1e-05):
    m = jnp.mean(x, axis=axis, keepdims=True)
    v = jnp.var(x, axis=axis, keepdims=True)
    return (x - m) / jnp.sqrt(v + eps)

def _scatter_add(tgt, idx, src, axis=0):
    return tgt.at[idx].add(src)

def _segment_sum(src, seg, n):
    return jax.ops.segment_sum(src, seg, n)
kernel_name = 'mk_adaln_d1_jaxref_r8_5e3a0b'

def setup_inputs(seed: int=0):
    np.random.seed(seed)
    _w = jnp.asarray

    def _L0_attn_setup():
        import jax, jax.numpy as jnp
        import numpy as np
        D_MODEL = 128
        N_HEADS = 16
        D_K = D_MODEL // N_HEADS
        THETA = 10000.0
        MAX_SEQ = 256

        def _trunc_normal(key, shape, std):
            return jnp.clip(jax.random.normal(key, shape) * std, -3 * std, 3 * std).astype(jnp.float32)

        def _rope(x, positions):
            d = x.shape[-1]
            inv_freq = THETA ** (-2.0 * jnp.arange(0, d // 2, dtype=jnp.float32) / d)
            angles = positions.astype(jnp.float32)[:, None] * inv_freq[None, :]
            cos, sin = (jnp.cos(angles), jnp.sin(angles))
            xp = x.reshape(x.shape[:-1] + (d // 2, 2))
            x_even, x_odd = (xp[..., 0], xp[..., 1])
            out_even = x_even * cos - x_odd * sin
            out_odd = x_even * sin + x_odd * cos
            return jnp.stack((out_even, out_odd), axis=-1).reshape(x.shape)
        key = jax.random.key(seed)
        kx, kq, kk, kv, ko = jax.random.split(key, 5)
        std = np.sqrt(2.0 / (D_MODEL + D_MODEL))
        x = jax.random.normal(kx, (2, 256, D_MODEL), dtype=jnp.float32)
        W_q = _trunc_normal(kq, (D_MODEL, D_MODEL), std)
        W_k = _trunc_normal(kk, (D_MODEL, D_MODEL), std)
        W_v = _trunc_normal(kv, (D_MODEL, D_MODEL), std)
        W_o = _trunc_normal(ko, (D_MODEL, D_MODEL), std)
        return {'x': x, 'W_q': W_q, 'W_k': W_k, 'W_v': W_v, 'W_o': W_o}
    _L0_attn_in = _L0_attn_setup()

    def _L0_ffn_setup():
        import jax, jax.numpy as jnp
        import numpy as np
        H, I, E_ROUTED, TOP_K = (128, 352, 7, 2)
        B, S = (4, 256)

        def _expert(h, g, u, d):
            return jnp.einsum('...i,hi->...h', jax.nn.silu(h @ g.T) * (h @ u.T), d)
        key = jax.random.key(seed)
        ks = jax.random.split(key, 10)
        sc = 0.02
        return {'x': jax.random.normal(ks[0], (B, S, H), dtype=jnp.float32), 'sg': jax.random.normal(ks[1], (I, H), dtype=jnp.float32) * sc, 'su': jax.random.normal(ks[2], (I, H), dtype=jnp.float32) * sc, 'sd': jax.random.normal(ks[3], (H, I), dtype=jnp.float32) * sc, 'rg': jax.random.normal(ks[4], (E_ROUTED, I, H), dtype=jnp.float32) * sc, 'ru': jax.random.normal(ks[5], (E_ROUTED, I, H), dtype=jnp.float32) * sc, 'rd': jax.random.normal(ks[6], (E_ROUTED, H, I), dtype=jnp.float32) * sc, 'wr': jax.random.normal(ks[7], (E_ROUTED, H), dtype=jnp.float32) * sc, 'rb': jnp.zeros((E_ROUTED,), dtype=jnp.float32)}
    _L0_ffn_in = _L0_ffn_setup()
    _L0_c = _w((lambda *s: np.random.randn(*s).astype(np.float32) * 0.05)(4, 128))
    _L0_wmod = _w((lambda *s: np.random.randn(*s).astype(np.float32) * 0.05)(128, 6 * 128) * 128 ** (-0.5))
    _d = {'L0_attn_x': _L0_attn_in['x'], 'L0_attn_W_q': _L0_attn_in['W_q'], 'L0_attn_W_k': _L0_attn_in['W_k'], 'L0_attn_W_v': _L0_attn_in['W_v'], 'L0_attn_W_o': _L0_attn_in['W_o'], 'L0_ffn_sg': _L0_ffn_in['sg'], 'L0_ffn_su': _L0_ffn_in['su'], 'L0_ffn_sd': _L0_ffn_in['sd'], 'L0_ffn_rg': _L0_ffn_in['rg'], 'L0_ffn_ru': _L0_ffn_in['ru'], 'L0_ffn_rd': _L0_ffn_in['rd'], 'L0_ffn_wr': _L0_ffn_in['wr'], 'L0_ffn_rb': _L0_ffn_in['rb'], 'L0_c': _L0_c, 'L0_wmod': _L0_wmod}
    _x0 = _d['L0_attn_x']
    _d['L0_attn_x'] = jax.random.normal(jax.random.fold_in(jax.random.key(seed), 1), (4, 1024, 128), dtype=_x0.dtype)
    del _x0
    return _d

def reference(L0_attn_x, L0_attn_W_q, L0_attn_W_k, L0_attn_W_v, L0_attn_W_o, L0_ffn_sg, L0_ffn_su, L0_ffn_sd, L0_ffn_rg, L0_ffn_ru, L0_ffn_rd, L0_ffn_wr, L0_ffn_rb, L0_c, L0_wmod):

    def _L0_attn_ref(x, W_q, W_k, W_v, W_o):
        import jax, jax.numpy as jnp
        import numpy as np
        D_MODEL = 128
        N_HEADS = 16
        D_K = D_MODEL // N_HEADS
        THETA = 10000.0
        MAX_SEQ = 256

        def _trunc_normal(key, shape, std):
            return jnp.clip(jax.random.normal(key, shape) * std, -3 * std, 3 * std).astype(jnp.float32)

        def _rope(x, positions):
            d = x.shape[-1]
            inv_freq = THETA ** (-2.0 * jnp.arange(0, d // 2, dtype=jnp.float32) / d)
            angles = positions.astype(jnp.float32)[:, None] * inv_freq[None, :]
            cos, sin = (jnp.cos(angles), jnp.sin(angles))
            xp = x.reshape(x.shape[:-1] + (d // 2, 2))
            x_even, x_odd = (xp[..., 0], xp[..., 1])
            out_even = x_even * cos - x_odd * sin
            out_odd = x_even * sin + x_odd * cos
            return jnp.stack((out_even, out_odd), axis=-1).reshape(x.shape)
        b, s, _ = x.shape

        def split_heads(t):
            return t.reshape(b, s, N_HEADS, D_K).transpose(0, 2, 1, 3)
        Q = split_heads(x @ W_q.T)
        K = split_heads(x @ W_k.T)
        V = split_heads(x @ W_v.T)
        pos = jnp.arange(s)
        Q = _rope(Q, pos)
        K = _rope(K, pos)
        score = jnp.einsum('bnqd,bnkd->bnqk', Q, K) / jnp.sqrt(jnp.float32(D_K))
        causal = jnp.triu(jnp.ones((s, s), dtype=bool), k=1)
        score = jnp.where(causal[None, None], -jnp.inf, score)
        attn = jax.nn.softmax(score, axis=-1)
        out = jnp.einsum('bnqk,bnkd->bnqd', attn, V)
        out = out.transpose(0, 2, 1, 3).reshape(b, s, D_MODEL)
        return out @ W_o.T

    def _L0_ffn_ref(x, sg, su, sd, rg, ru, rd, wr, rb):
        import jax, jax.numpy as jnp
        import numpy as np
        H, I, E_ROUTED, TOP_K = (128, 352, 7, 2)
        B, S = (4, 256)

        def _expert(h, g, u, d):
            return jnp.einsum('...i,hi->...h', jax.nn.silu(h @ g.T) * (h @ u.T), d)
        shared_out = _expert(x, sg, su, sd)
        logits = x @ wr.T + rb
        probs = jax.nn.softmax(logits, axis=-1)
        scores, idx = jax.lax.top_k(probs, TOP_K)
        scores = scores / scores.sum(axis=-1, keepdims=True)
        w = jnp.sum(scores[..., None] * jax.nn.one_hot(idx, E_ROUTED, dtype=x.dtype), axis=-2)
        out = shared_out
        for e in range(E_ROUTED):
            out = out + w[..., e:e + 1] * _expert(x, rg[e], ru[e], rd[e])
        return out
    x = L0_attn_x
    mod = (_silu(L0_c) @ L0_wmod).reshape(L0_c.shape[0], 6, 1, -1)
    sa, ca, ga, sb, cb, gb = (mod[:, 0], mod[:, 1], mod[:, 2], mod[:, 3], mod[:, 4], mod[:, 5])
    ga = (2 * (ga >= 0) - 1) * jnp.maximum(jnp.abs(ga), 0.25)
    gb = (2 * (gb >= 0) - 1) * jnp.maximum(jnp.abs(gb), 0.25)
    h = _layernorm(x, axis=-1) * (1 + ca) + sa
    x = x + ga * _L0_attn_ref(h, L0_attn_W_q, L0_attn_W_k, L0_attn_W_v, L0_attn_W_o)
    h = _layernorm(x, axis=-1) * (1 + cb) + sb
    x = x + gb * _L0_ffn_ref(h, L0_ffn_sg, L0_ffn_su, L0_ffn_sd, L0_ffn_rg, L0_ffn_ru, L0_ffn_rd, L0_ffn_wr, L0_ffn_rb)
    return x

_drawn_inputs = setup_inputs


def setup_inputs(seed=0):
    import zlib

    import numpy as np

    out = dict(_drawn_inputs(seed))
    spreads = {'L0_ffn_rb': (0.0, 0.8)}
    factors = {'L0_ffn_sg': 8.0,
     'L0_ffn_su': 8.0,
     'L0_ffn_sd': 8.0,
     'L0_ffn_rg': 8.0,
     'L0_ffn_ru': 8.0,
     'L0_ffn_rd': 8.0,
     'L0_ffn_wr': 8.0}
    for name, (base, spread) in spreads.items():
        noise = np.random.default_rng([zlib.crc32(name.encode()), seed]).standard_normal(out[name].shape)
        drawn = base * np.exp(spread * noise) if base else spread * noise
        out[name] = jnp.asarray(drawn.astype(out[name].dtype))
    for name, factor in factors.items():
        out[name] = (out[name] * factor).astype(out[name].dtype)
    return out
```

```python
from contextlib import ExitStack

import numpy as np

import concourse.bass as bass
from concourse import mybir

F32 = mybir.dt.float32
BF16 = mybir.dt.bfloat16
F32R = mybir.dt.float32r
ALU = mybir.AluOpType
ACT = mybir.ActivationFunctionType
AX = mybir.AxisListType

B, S, D = 4, 1024, 128
NH, DK = 16, 8
HQ = 4
NG = NH // HQ
NQ = B * NG
T = 128
TB = S // T
NT = B * TB
CH = 512
NP = 3
KR = NP * NP * DK
KM = KR + NP
VW = 32
NE, NI = 7, 352
EX = NE + 1
IC = [(0, 128), (128, 128), (256, 96)]
EPS = 1e-5
SCALE = float(DK) ** -0.5
LOW = -3.0e38
CG = CH // T

STEPS = [(c, k, max(0, k - CG * c) * T) for c in range(S // CH) for k in range(CG * (c + 1))]
NS = len(STEPS)
PIECES = []
for _h in range(HQ):
    for _q in range(TB):
        _n = (_q + 1) * T
        if _n > CH:
            PIECES.append((_h, _q, 0, CH, False))
            PIECES.append((_h, _q, CH, _n - CH, True))
        else:
            PIECES.append((_h, _q, 0, _n, True))
NM = len(PIECES)
EARLY = NM // HQ
SLOTS = 3
STEP_COST, PIECE_COST = 60, 120
SHIFT_SLOT = (NS - 3) * SLOTS
RING = 3


def ring_plan(back, ahead1, ahead2):
    pieces = [("max", 1, p) for p in range(EARLY, NM)] if ahead1 else []
    late = [("max", 2, p) for p in range(EARLY)] if ahead2 else []
    if ahead1:
        late.insert(min(3, len(late)), ("shift", 1, None))
    slots, total = [], 0
    for s, (_, _, q0) in enumerate(STEPS):
        for j in range(SLOTS):
            total += STEP_COST + CH - q0
            slots.append((total, s * SLOTS + j))
    scale = total / sum(PIECE_COST + x[3] for x in PIECES)
    plan, at = [], 0
    for kind, off, p in pieces + late:
        slot = next((s for end, s in slots if at < end), NS * SLOTS - 1)
        if not ahead2 and kind == "shift":
            slot = SHIFT_SLOT
        plan.append((slot, kind, off, p))
        at += (PIECES[p][3] + PIECE_COST) * scale if kind == "max" else 0
    out = []
    for s in range(NS * SLOTS):
        if s == 3 * SLOTS and back:
            out.append((s, "norm", -1, 1))
        if s == 7 * SLOTS:
            out.append((s, "norm", 0, 0))
        out += [x for x in plan if x[0] == s]
    return out


def adaln_block(nc, x_d, wq_d, wk_d, wv_d, wo_d, sw_g_d, sw_u_d, sw_d_d, wr_d, rb_d, c_d, wmod_d,
                cos_d, sin_d, eye_d, tri_d, out_d):
    KPART = [0, 1, 2, 0, 1]
    qs_d = nc.dram_tensor("q_parts_scratch", [NQ, NP, DK * HQ, S], BF16, kind="Internal").ap()
    ks_d = nc.dram_tensor("k_parts_scratch", [NQ, len(KPART), DK * HQ, S], BF16, kind="Internal").ap()

    ctx = ExitStack()
    with ctx:
        def sb(name, shape, dt=F32, at=None):
            return (at or ctx).enter_context(nc.sbuf_tensor(name, shape, dt))

        def sem(name):
            return ctx.enter_context(nc.semaphore(name))

        xs = sb("xs", [T, NT, D])
        eye = sb("eye", [128, 128])
        wo = sb("wo", [D, D])
        gate_a = sb("gate_a", [128, B, D])
        gate_b = sb("gate_b", [128, B, D])
        mod1 = sb("mod1", [D, 2, B])
        mod2 = sb("mod2", [D, 2, B])
        o_all = sb("o_all", [T, NQ, TB, HQ * DK])
        stats = sb("stats", [T, NT, 6])
        mean = sb("mean", [T, NT])
        part_a = sb("part_a", [T, NT])
        part_b = sb("part_b", [T, NT])
        rstd = sb("rstd", [T, NT])
        rb = sb("rb", [128, NE])
        wr = sb("wr", [D, NE])
        xn = sb("xn", [T, 2, CG, D])
        hT = sb("hT", [D, 2, CH])

        att = ExitStack()
        v_all = sb("v_all", [T, NQ, TB, HQ * DK], at=att)
        qa = [sb(f"qa{m}", [KM, HQ * S], BF16, at=att) for m in range(3)]
        ka = [sb(f"ka{m}", [KM, HQ * S], BF16, at=att) for m in range(3)]
        v4 = [sb(f"v4_{m}", [T, TB, HQ, VW], at=att) for m in range(3)]
        tri = sb("tri", [T, CH], at=att)
        rowmax = [sb(f"rowmax{m}", [T, HQ, TB], at=att) for m in range(3)]
        leftmax = [sb(f"leftmax{m}", [T, HQ, TB - CG], at=att) for m in range(3)]
        mparts = [sb(f"mparts{m}", [HQ * TB, NP, T], BF16, at=att) for m in range(3)]
        mrest = sb("mrest", [HQ * TB, T], at=att)
        junk = sb("junk", [T, RING, CH], at=att)
        outT = sb("outT", [128, 2, CH], at=att)
        recip = sb("recip", [T, CG, HQ], at=att)
        pre = ExitStack()
        wq = sb("wq", [D, 2, D], at=pre)
        wk = sb("wk", [D, 2, D], at=pre)
        wv = sb("wv", [D, D], at=pre)
        c_t = sb("c_t", [D, B], at=pre)
        c_s = sb("c_s", [D, B], at=pre)
        c_b = sb("c_b", [D, B, 128], at=pre)
        wmod = sb("wmod", [D, 6, D], at=pre)
        mag = sb("mag", [128, 2, B * D], at=pre)
        cos = sb("cos", [128, S], at=pre)
        sin = sb("sin", [128, S], at=pre)
        rot = sb("rot", [128, 3, CH], at=pre)
        qk_parts = sb("qk_parts", [128, 2, 2, NP, CH], BF16, at=pre)
        pre.close()
        probs = [sb(f"probs{m}", [T, HQ, CH], at=att) for m in range(4)]
        att.close()

        moe = ctx
        h2_hi = sb("h2_hi", [D, NT * T], F32R, at=moe)
        h2_lo = sb("h2_lo", [D, NT * T], F32R, at=moe)
        w_raw = sb("w_raw", [D, 2, 2, NI], at=moe)
        w_hi = sb("w_hi", [D, EX, 2, NI], F32R, at=moe)
        w_lo = sb("w_lo", [D, EX, 2, NI], F32R, at=moe)
        wd = sb("wd", [128, EX, len(IC), D], at=moe)
        o_tile = sb("o_tile", [T, 2, CG, D], at=moe)
        oT = sb("oT", [D, 2, CH], at=moe)
        att_o = sb("att_o", [T, 2, CH], at=moe)
        logit = sb("logit", [T, NT, NE], at=moe)
        prob = sb("prob", [T, NT, NE], at=moe)
        rank = sb("rank", [T, NT, NE], at=moe)
        beats = sb("beats", [T, NT, NE], at=moe)
        rsum = sb("rsum", [T, NT], at=moe)
        route = sb("route", [T, NT, NE], at=moe)
        sg = sb("sg", [128, 3, CH], at=moe)
        hid = sb("hid", [128, 2, len(IC), CH], at=moe)
        acc = sb("acc", [T, 2, CG, D], at=moe)

        ps = ctx.enter_context(nc.psum_tensor("ps", [128, 8, CH], F32))

        s_in0 = sem("s_in0")
        s_in = sem("s_in")
        s_x = sem("s_x")
        s_link = sem("s_link")
        s_glink = sem("s_glink")
        s_csilu = sem("s_csilu")
        s_cb = sem("s_cb")
        s_modps = sem("s_modps")
        s_mod = sem("s_mod")
        s_var = sem("s_var")
        s_std = sem("s_std")
        s_seen_act, s_seen_pool, s_seen_dve = sem("s_seen_act"), sem("s_seen_pool"), sem("s_seen_dve")
        s_xn = sem("s_xn")
        s_tp = sem("s_tp")
        s_hT = sem("s_hT")
        s_qk = sem("s_qk")
        s_qk_free = sem("s_qk_free")
        s_v = sem("s_v")
        s_v_free = sem("s_v_free")
        s_xn_free = sem("s_xn_free")
        s_hT_free = sem("s_hT_free")
        s_parts = sem("s_parts")
        s_spill = [sem(f"s_spill{m}") for m in range(2)]
        s_fill = sem("s_fill")
        s_qk_in = [sem(f"s_qk_in{m}") for m in range(3)]
        s_ring = sem("s_ring")
        s_ring_free = sem("s_ring_free")
        s_rowmax = sem("s_rowmax")
        s_mparts = sem("s_mparts")
        s_m_in = [sem(f"s_m_in{m}") for m in range(3)]
        s_scores = sem("s_scores")
        s_exp = sem("s_exp")
        s_mask = sem("s_mask")
        s_pv = sem("s_pv")
        s_outT = sem("s_outT")
        s_v4 = sem("s_v4")
        s_otile = sem("s_otile")
        s_ot = sem("s_ot")
        s_oT = sem("s_oT")
        s_proj = sem("s_proj")
        s_x2 = sem("s_x2")
        s_var2 = sem("s_var2")
        s_std2 = sem("s_std2")
        s_xn2 = sem("s_xn2")
        s_tp2 = sem("s_tp2")
        s_hT2 = sem("s_hT2")
        s_lg = sem("s_lg")
        s_lg_free = sem("s_lg_free")
        s_split2 = sem("s_split2")
        s_max7 = sem("s_max7")
        s_exp7 = sem("s_exp7")
        s_wraw = [sem(f"s_wraw{m}") for m in range(2)]
        s_wsplit = sem("s_wsplit")
        s_wd = sem("s_wd")
        s_gu = sem("s_gu")
        s_silu = sem("s_silu")
        s_hid = sem("s_hid")
        s_dn = sem("s_dn")
        s_dn_free = sem("s_dn_free")
        s_res = sem("s_res")
        s_out = sem("s_out")

        block = ctx.enter_context(nc.Block())

        def quad(i, r):
            return 3 * i + r

        def third(i, r):
            return i + r // 3

        FULL = ring_plan(True, True, True)
        FIRST = ring_plan(False, True, True)
        PRE = [("max", 0, p) for p in range(NM)] + [("shift", 0, None)] + [("max", 1, p) for p in range(EARLY)]
        LAST1 = ring_plan(True, True, False)
        LAST0 = ring_plan(True, False, False)
        R1 = len(PRE) + len(FIRST)
        RL = len(FULL)
        assert RL % RING == 0

        def ring_base(i, r):
            if isinstance(i, int):
                n = quad(i, r)
                if n == 0:
                    return len(PRE)
                return R1 + RL * (min(n, NQ - 2 + 0) - 1) + (len(LAST1) if n >= NQ - 1 else 0) \
                    + (len(LAST0) if n >= NQ else 0)
            return quad(i, r) * RL + (R1 - RL)

        def ring_bank(i, r, k):
            if isinstance(i, int):
                return (ring_base(i, r) + k) % RING
            return (R1 + k) % RING

        def plan_of(i, r):
            if isinstance(i, int):
                n = quad(i, r)
                return {0: FIRST, NQ - 2: LAST1, NQ - 1: LAST0}.get(n, FULL)
            return FULL

        def quads(eng, body):
            body(0, 0)
            with eng.Fori(0, 4) as i:
                for r in (1, 2, 3):
                    body(i, r)
            for r in (1, 2, 3):
                body(4, r)

        @block.sync
        def _(sp):
            for dst, src in ((c_t[:], c_d), (wmod[:], wmod_d.rearrange("k (j f) -> k j f", j=6)),
                             (eye[:], eye_d)):
                sp.dma_start(dst, src).then_inc(s_in0, 16)
            xv = x_d.rearrange("(t p) d -> p t d", p=T)
            for b in range(B):
                sp.dma_start(xs[:, b * TB:(b + 1) * TB, :], xv[:, b * TB:(b + 1) * TB, :]).then_inc(s_x, 16)
            for dst, src in ((wq[:], wq_d.rearrange("j k m -> k j m")), (wk[:], wk_d.rearrange("j k m -> k j m")),
                             (wv[:], wv_d), (cos[:], cos_d), (sin[:], sin_d), (wo[:], wo_d), (tri[:], tri_d),
                             (wr[:], wr_d), (rb[:], rb_d[0:1, :].to_broadcast((128, NE)))):
                sp.dma_start(dst, src).then_inc(s_in, 16)

            with sp.Fori(0, B) as b:
                for u in range(2):
                    for w, (scr, kept) in enumerate(((qs_d, range(NP)), (ks_d, KPART))):
                        sp.wait_ge(s_parts, (b * 2 + u) * 2 + w + 1)
                        for slot, p in enumerate(kept):
                            dst = scr[bass.ds(b * NG, NG), slot, :, u * CH:(u + 1) * CH]
                            sp.dma_start(dst, qk_parts[:, u, w, p, :]).then_inc(s_spill[u], 16)

            def load_quad(i, r):
                n, m = quad(i, r), r % 3
                q = qs_d[bass.ds(n, 1), :, :, :].rearrange("n p (d h) s -> (n p d) (h s)", h=HQ)
                k = ks_d[bass.ds(n, 1), :, :, :].rearrange("n p (d h) s -> (n p d) (h s)", h=HQ)
                w = NP * DK
                for j in range(NP):
                    sp.dma_start(qa[m][j * w:(j + 1) * w, :], q[0:w, :]).then_inc(s_qk_in[m], 16)
                    sp.dma_start(ka[m][j * w:(j + 1) * w, :], k[j * DK:j * DK + w, :]).then_inc(s_qk_in[m], 16)

            def load_shift(i, r):
                m = r % 3
                sp.wait_ge(s_mparts, quad(i, r) + 1)
                for p in range(NP):
                    sp.dma_start(qa[m][KR + p:KR + p + 1, :].rearrange("o (a t) -> o a t", t=T),
                                 mparts[m][:, p, :]).then_inc(s_m_in[m], 16)

            for u in range(2):
                sp.wait_ge(s_spill[u], B * 16 * (NP + len(KPART)) + 16)
            sp.wait_ge(s_fill, 1)
            for r in range(2):
                load_quad(0, r)
            load_shift(0, 0)

            def body(i, r):
                n = quad(i, r)
                if not (isinstance(i, int) and n + 2 >= NQ):
                    if not (isinstance(i, int) and n == 0):
                        sp.wait_ge(s_scores, n * (2 * NS))
                    load_quad(i, r + 2)
                if not (isinstance(i, int) and n + 1 >= NQ):
                    load_shift(i, r + 1)
            quads(sp, body)

            sp.wait_ge(s_ring_free, ring_base(0, NQ) + 1)
            for c, (i0, w) in enumerate(IC):
                sp.dma_start(wd[0:w, :, c, :], sw_d_d[:, i0:i0 + w, :].rearrange("e p h -> p e h")).then_inc(s_wd, 16)
            for e in range(EX):
                if e >= 2:
                    sp.wait_ge(s_wsplit, 2 * (e - 1))
                sp.dma_start(w_raw[:, e % 2, 0, :], sw_g_d[e, :, :]).then_inc(s_wraw[e % 2], 16)
                sp.dma_start(w_raw[:, e % 2, 1, :], sw_u_d[e, :, :]).then_inc(s_wraw[e % 2], 16)

            ov = out_d.rearrange("(t p) d -> p t d", p=T)
            with sp.Fori(0, B) as b:
                for u in range(2):
                    sp.wait_ge(s_res, b * 2 + u + 1)
                    sp.dma_start(ov[:, bass.ds(b * TB + u * CG, CG), :],
                                 xs[:, bass.ds(b * TB + u * CG, CG), :]).then_inc(s_out, 16)
            sp.wait_ge(s_out, 16 * 2 * B)

        @block.gpsimd
        def _(pool):
            for m in range(3):
                nc.gpsimd.memset(ka[m][64:KM, :], 1.0)
                last = nc.gpsimd.memset(qa[m][64:KM, :], 0.0)
            last.then_inc(s_fill, 1)
            pool.wait_ge(s_fill, 1)
            for m in range(3):
                nc.gpsimd.memset(v4[m][:], 0.0).then_inc(s_glink, 1)
            pool.wait_ge(s_glink, 3)
            for m in range(3):
                nc.gpsimd.memset(v4[m][:, :, :, DK:DK + 1], 1.0).then_inc(s_glink, 1)
            pool.wait_ge(s_glink, 6)

            def values(i, r):
                m = r % 3
                nc.gpsimd.tensor_copy(v4[m][:, :, :, 0:DK],
                                      v_all[:, bass.ds(quad(i, r), 1), :, :].rearrange("p n k (h d) -> p (n k) h d", h=HQ)
                                      ).then_inc(s_v4, 1)

            pool.wait_ge(s_v_free, 2 * B)
            values(0, 0)

            def body(i, r):
                n = quad(i, r)
                if not (isinstance(i, int) and n + 1 >= NQ):
                    if not (isinstance(i, int) and n == 0):
                        pool.wait_ge(s_pv, n * NS - (NS - 1))
                    values(i, r + 1)
                for s, (c, k, q0) in enumerate(STEPS):
                    if k < CG * c:
                        continue
                    pool.wait_ge(s_exp, n * (2 * NS) + 2 * (s + 1))
                    pool.sem_inc(s_seen_pool, 1)
                    p = probs[s % 4][:, :, 0:T]
                    nc.gpsimd.affine_select(out=p, in_=p, compare_op=ALU.is_ge, fill=0.0, base=0,
                                            pattern=[[0, HQ], [1, T]], channel_multiplier=-1).then_inc(s_mask, 1)
            quads(pool, body)

        @block.scalar
        def _(act):
            act.wait_ge(s_in0, 48)
            nc.scalar.activation(c_s[:], c_t[:], ACT.Silu).then_inc(s_csilu, 1)
            act.wait_ge(s_var, 1)
            nc.scalar.activation(rstd[:], rstd[:], ACT.Sqrt).then_inc(s_std, 1)
            act.wait_ge(s_mod, 1)

            with act.Fori(0, B) as b:
                for u in range(2):
                    n = b * 2 + u
                    act.wait_ge(s_tp, n + 1)
                    act.wait_ge(s_hT_free, n + 1)
                    act.sem_inc(s_seen_act, 1)
                    nc.scalar.activation(hT[:, u, :], ps[:, u, :], ACT.Identity, scale=mod1[:, 0, bass.ds(b, 1)],
                                         bias=mod1[:, 1, bass.ds(b, 1)]).then_inc(s_hT, 1)
                    act.wait_ge(s_v, n + 1)
                    act.sem_inc(s_seen_act, 1)
                    nc.scalar.activation(
                        v_all[:, bass.ds(b * NG, NG), u * CG:(u + 1) * CG, :].rearrange("p g j e -> p j g e"),
                        ps[:, 6 + u, :].rearrange("p (j g e) -> p j g e", j=CG, g=NG), ACT.Copy).then_inc(s_v_free, 1)

            def copy_out(i, r, c, k):
                n = quad(i, r)
                act.wait_ge(s_pv, n * NS + CG + c * 2 * CG)
                if not (isinstance(i, int) and n == 0):
                    j, q = (i, r) if c else (i, r - 1)
                    if isinstance(i, int):
                        j, q = 0, quad(i, q)
                    at = [x[1:] for x in plan_of(j, q)].index(("norm", -1, 1) if c else ("norm", 0, 0))
                    act.wait_ge(s_ring, ring_base(j, q) + (at + 1))
                nc.scalar.activation(outT[:, c, :], ps[:, 4, :], ACT.Copy).then_inc(s_outT, 1)

            def body(i, r):
                n = quad(i, r)
                first = isinstance(i, int) and n == 0
                for s, (c, k, q0) in enumerate(STEPS):
                    if not (first and s < 4):
                        act.wait_ge(s_pv, n * NS + s - 3)
                    for h in range(2):
                        act.wait_ge(s_scores, n * (2 * NS) + 2 * s + h + 1)
                        nc.scalar.activation(probs[s % 4][:, 2 * h:2 * h + 2, 0:CH - q0], ps[:, 2 * h:2 * h + 2, q0:CH],
                                             ACT.Exp, scale=SCALE).then_inc(s_exp, 1)
                    if s == 1 and not first:
                        copy_out(i, r - 1, 1, None)
                    if s == 5:
                        copy_out(i, r, 0, None)
            quads(act, body)
            copy_out(5, 0, 1, None)

            with act.Fori(0, B) as b:
                for u in range(2):
                    n = b * 2 + u
                    act.wait_ge(s_ot, n + 1)
                    nc.scalar.activation(oT[:, u, :], ps[:, u, :], ACT.Copy).then_inc(s_oT, 1)
            act.wait_ge(s_var2, 1)
            nc.scalar.activation(rstd[:], rstd[:], ACT.Sqrt).then_inc(s_std2, 1)
            with act.Fori(0, B) as b:
                for u in range(2):
                    n = b * 2 + u
                    act.wait_ge(s_tp2, n + 1)
                    act.wait_ge(s_lg_free, n + 1)
                    act.sem_inc(s_seen_act, 1)
                    nc.scalar.activation(hT[:, u, :], ps[:, 4 + u, :], ACT.Identity, scale=mod2[:, 0, bass.ds(b, 1)],
                                         bias=mod2[:, 1, bass.ds(b, 1)]).then_inc(s_hT2, 1)
            act.wait_ge(s_max7, 1)
            nc.scalar.activation(prob[:], logit[:], ACT.Exp).then_inc(s_exp7, 1)

            with act.Fori(0, B) as b:
                for u in range(2):
                    for e in range(EX):
                        for c, (i0, w) in enumerate(IC):
                            g = (b * 2 + u) * (EX * len(IC)) + e * len(IC) + c
                            act.wait_ge(s_gu, g + 1)
                            act.wait_ge(s_hid, g + 1)
                            nc.scalar.activation(sg[0:w, c, :], ps[0:w, 2 * c, :], ACT.Silu).then_inc(s_silu, 1)

        @block.vector
        def _(dve):
            chain = [0]

            def link(ins):
                chain[0] += 1
                ins.then_inc(s_link, 1)
                dve.wait_ge(s_link, chain[0])

            V = nc.vector
            dve.sem_inc(s_qk_free, 2)
            dve.sem_inc(s_xn_free, 2)
            dve.sem_inc(s_hT_free, 2)
            dve.sem_inc(s_lg_free, 2)
            dve.sem_inc(s_hid, len(IC))
            dve.sem_inc(s_dn_free, 2)
            for u in range(2):
                dve.sem_inc(s_spill[u], 16)

            def layernorm_stats(done, std):
                def tiles(t0):
                    for j in range(TB):
                        V.bn_stats(stats[:, bass.ds(t0 + j, 1), :].rearrange("p o s -> p (o s)"),
                                   xs[:, bass.ds(t0 + j, 1), :].rearrange("p o s -> p (o s)"))
                with dve.Fori(0, B) as b:
                    tiles(b * TB)
                m0, q0, m1, q1 = stats[:, :, 1], stats[:, :, 2], stats[:, :, 4], stats[:, :, 5]
                link(V.drain())
                link(V.tensor_tensor(mean[:], m0, m1, ALU.add))
                link(V.tensor_tensor(part_a[:], m0, m1, ALU.subtract))
                link(V.tensor_tensor(part_b[:], q0, q1, ALU.add))
                link(V.tensor_scalar(mean[:], mean[:], 0.5, None, ALU.mult))
                link(V.tensor_tensor(part_a[:], part_a[:], part_a[:], ALU.mult))
                link(V.tensor_scalar(part_b[:], part_b[:], 1.0 / D, EPS, ALU.mult, ALU.add))
                V.scalar_tensor_tensor(rstd[:], part_a[:], 0.25, part_b[:], ALU.mult, ALU.add).then_inc(done, 1)
                dve.wait_ge(std, 1)
                link(V.reciprocal(rstd[:], rstd[:]))

            dve.wait_ge(s_x, 16 * B)
            layernorm_stats(s_var, s_std)
            link(V.tensor_copy(c_b[:], c_s[:].unsqueeze(2).to_broadcast((D, B, 128))))
            dve.sem_inc(s_cb, 1)
            dve.wait_ge(s_modps, 1)
            mps = ps[:, 0, 0:4 * B].rearrange("p (j b) -> p j b", b=B)
            for m, j in ((mod1, 0), (mod2, 2)):
                link(V.tensor_scalar(m[:, 0, :], mps[:, j + 1, :], 1.0, None, ALU.add))
                link(V.tensor_copy(m[:, 1, :], mps[:, j, :]))
            for g, bank in ((gate_a, 1), (gate_b, 2)):
                link(V.tensor_scalar(mag[:, 0, :], ps[:, bank, :], 0.0, 2.0, ALU.is_ge, ALU.mult))
                link(V.tensor_scalar(mag[:, 1, :], ps[:, bank, :], -1.0, 0.25, ALU.mult, ALU.max))
                link(V.tensor_tensor(mag[:, 1, :], ps[:, bank, :], mag[:, 1, :], ALU.max))
                link(V.scalar_tensor_tensor(g[:].rearrange("p b d -> p (b d)"), mag[:, 0, :], -1.0, mag[:, 1, :],
                                            ALU.add, ALU.mult))
            dve.sem_inc(s_mod, 1)
            dve.wait_ge(s_in, 16 * 9)

            base = chain[0]
            PER = 16
            with dve.Fori(0, B) as b:
                for u in range(2):
                    n = b * 2 + u
                    step = [0]

                    def ulink(ins):
                        step[0] += 1
                        ins.then_inc(s_link, 1)
                        dve.wait_ge(s_link, n * PER + (base + step[0]))
                    dve.wait_ge(s_xn_free, n + 1)
                    for j in range(CG):
                        t = b * TB + (u * CG + j)
                        last = V.tensor_scalar(xn[:, u, j, :], xs[:, bass.ds(t, 1), :].rearrange("p o d -> p (o d)"),
                                               mean[:, bass.ds(t, 1)], rstd[:, bass.ds(t, 1)],
                                               ALU.subtract, ALU.mult)
                    last.then_inc(s_xn, 1)
                    for w in range(2):
                        dve.wait_ge(s_qk, n * 2 + w + 1)
                        if w == 0:
                            dve.wait_ge(s_spill[u], b * (16 * (NP + len(KPART))) + 16)
                        part = [qk_parts[:, u, w, p, :] for p in range(NP)]
                        pb = 2 + 2 * w
                        V.tensor_tensor(rot[:, 0, :], ps[:, pb, :], cos[:, u * CH:(u + 1) * CH], ALU.mult)
                        ulink(V.tensor_tensor(rot[:, 1, :], ps[:, pb + 1, :], sin[:, u * CH:(u + 1) * CH], ALU.mult))
                        dve.sem_inc(s_qk_free, 1)
                        ulink(V.tensor_tensor(rot[:, 0, :], rot[:, 0, :], rot[:, 1, :], ALU.add))
                        ulink(V.tensor_copy(part[0], rot[:, 0, :]))
                        ulink(V.tensor_tensor(rot[:, 1, :], rot[:, 0, :], part[0], ALU.subtract))
                        ulink(V.tensor_copy(part[1], rot[:, 1, :]))
                        V.tensor_tensor(part[2], rot[:, 1, :], part[1], ALU.subtract).then_inc(s_parts, 1)
                        ulink(V.tensor_copy(rot[:, 2, 0:8], rot[:, 1, 0:8]))
                    while step[0] < PER:
                        step[0] += 1
                        dve.sem_inc(s_link, 1)
            chain[0] = base + PER * 2 * B

            def shift_parts(m, bank):
                part = [mparts[m][:, p, :] for p in range(NP)]
                neg = ps[0:HQ * TB, bank, 0:T]
                return [lambda: V.tensor_scalar(part[0], neg, -1.0, None, ALU.mult),
                        lambda: V.scalar_tensor_tensor(mrest[:], neg, -1.0, part[0], ALU.mult, ALU.subtract),
                        lambda: V.tensor_copy(part[1], mrest[:]),
                        lambda: V.tensor_tensor(part[2], mrest[:], part[1], ALU.subtract)]

            aux = chain[0]
            AUX = 7

            def ring_item(i, r, k, kind, off, what, links):
                lbase, lk = links
                bank = 5 + ring_bank(i, r, k) if k is not None else None
                m = (r + off) % 3
                if kind == "max":
                    h, q, k0, w, diag = PIECES[what]
                    src = ps[:, bank, 0:w]
                    if diag:
                        dve.sem_inc(s_seen_dve, 1)
                        dst = rowmax[m][:, h, q:q + 1]
                        V.tensor_tensor_reduce(out=junk[:, bank - 5, 0:w], in0=src, in1=tri[:, CH - w:CH], scale=1.0,
                                               scalar=LOW, op0=ALU.add, op1=ALU.max, accum_out=dst).then_inc(s_ring_free, 1)
                    else:
                        V.reduce_max(leftmax[m][:, h, q - CG:q - CG + 1], src, AX.X).then_inc(s_ring_free, 1)
                elif kind == "shift":
                    ops = shift_parts(m, bank)
                    for j, op in enumerate(ops):
                        ins = op()
                        if j < 3:
                            ins.then_inc(s_link, 1)
                            lk[0] += 1
                            dve.wait_ge(s_link, lbase + lk[0])
                            if j == 1:
                                dve.sem_inc(s_ring_free, 1)
                        else:
                            ins.then_inc(s_mparts, 1)
                else:
                    c = what
                    src = ps[:, bank, :].rearrange("p (j h w) -> p j h w", j=CG, h=HQ)
                    V.reciprocal(recip[:], src[:, :, :, DK]).then_inc(s_link, 1)
                    lk[0] += 1
                    dve.wait_ge(s_link, lbase + lk[0])
                    dst = o_all[:, bass.ds(quad(i, r + off), 1), c * CG:(c + 1) * CG, :]
                    V.tensor_tensor(dst.rearrange("p n j (h d) -> p (n j) h d", h=HQ), src[:, :, :, 0:DK],
                                    recip[:].unsqueeze(3).to_broadcast((T, CG, HQ, DK)), ALU.mult).then_inc(s_ring_free, 1)
                    lk[0] += 1
                    dve.sem_inc(s_link, 1)

            def full_max(m):
                V.tensor_tensor(rowmax[m][:, :, CG:TB], rowmax[m][:, :, CG:TB], leftmax[m][:], ALU.max).then_inc(s_rowmax, 1)

            lk = [0]
            for k, (kind, off, what) in enumerate(PRE):
                dve.wait_ge(s_ring, k + 1)
                if kind == "shift":
                    pass
                bank_k = k % RING
                ring_pre = (5 + bank_k)
                m = off % 3
                if kind == "max":
                    h, q, k0, w, diag = PIECES[what]
                    src = ps[:, ring_pre, 0:w]
                    if diag:
                        V.tensor_tensor_reduce(out=junk[:, bank_k, 0:w], in0=src, in1=tri[:, CH - w:CH], scale=1.0,
                                               scalar=LOW, op0=ALU.add, op1=ALU.max,
                                               accum_out=rowmax[m][:, h, q:q + 1]).then_inc(s_ring_free, 1)
                    else:
                        V.reduce_max(leftmax[m][:, h, q - CG:q - CG + 1], src, AX.X).then_inc(s_ring_free, 1)
                    if what == NM - 1:
                        dve.wait_ge(s_ring_free, k + 1)
                        full_max(m)
                else:
                    for j, op in enumerate(shift_parts(m, ring_pre)):
                        ins = op()
                        if j < 3:
                            ins.then_inc(s_link, 1)
                            lk[0] += 1
                            dve.wait_ge(s_link, aux + lk[0])
                            if j == 1:
                                dve.sem_inc(s_ring_free, 1)
                        else:
                            ins.then_inc(s_mparts, 1)
            l0 = aux + lk[0]

            def body(i, r):
                n = quad(i, r)
                plan = plan_of(i, r)
                lk = [0]
                first = isinstance(i, int) and n == 0
                lbase = l0 if first else n * AUX + (l0 - 2)
                rbase = ring_base(i, r)
                for k, (s, kind, off, what) in enumerate(plan):
                    if k and kind == "norm" and plan[k - 1][1] == "norm":
                        dve.wait_ge(s_ring_free, rbase + k)
                    dve.wait_ge(s_ring, rbase + (k + 1))
                    ring_item(i, r, k, kind, off, what, (lbase, lk))
                    if kind == "max" and what == NM - 1:
                        dve.wait_ge(s_ring_free, rbase + (k + 1))
                        full_max((r + off) % 3)
            quads(dve, body)
            endbase = ring_base(5, 1)
            dve.wait_ge(s_ring_free, endbase)
            dve.wait_ge(s_ring, endbase + 1)
            lend = l0 - 2 + NQ * AUX - 3
            lk = [0]
            ring_item(5, 1, 0, "norm", -1, 1, (lend, lk))
            chain[0] = lend + 2

            def tile_pair(b, u):
                return b * TB + u * CG
            base2 = chain[0]

            def by_tile(n, b, u):
                V.tensor_copy(o_tile[:, u, :, :].rearrange("p j (g e) -> p j g e", g=NG),
                              o_all[:, bass.ds(b * NG, NG), u * CG:(u + 1) * CG, :].rearrange("p g j e -> p j g e")
                              ).then_inc(s_otile, 1)

            dve.wait_ge(s_ring_free, ring_base(0, NQ) + 1)
            with dve.Fori(0, B) as b:
                for u in range(2):
                    n = b * 2 + u
                    by_tile(n, b, u)
                    dve.wait_ge(s_proj, n + 1)
                    V.tensor_tensor(att_o[:, u, :].rearrange("p (j d) -> p j d", j=CG),
                                    ps[:, 2 + u, :].rearrange("p (j d) -> p j d", j=CG),
                                    gate_a[:, bass.ds(b, 1), :].to_broadcast((T, CG, D)), ALU.mult).then_inc(s_link, 1)
                    dve.wait_ge(s_link, n + (base2 + 1))
                    xt = xs[:, bass.ds(tile_pair(b, u), CG), :]
                    V.tensor_tensor(xt, xt, att_o[:, u, :].rearrange("p (j d) -> p j d", j=CG),
                                    ALU.add).then_inc(s_x2, 1)
            chain[0] = base2 + 2 * B
            dve.wait_ge(s_x2, 2 * B)
            layernorm_stats(s_var2, s_std2)

            base3 = chain[0]
            with dve.Fori(0, B) as b:
                for u in range(2):
                    n = b * 2 + u
                    for j in range(CG):
                        t = b * TB + (u * CG + j)
                        if j == 0:
                            dve.wait_ge(s_lg_free, n + 1)
                        last = V.tensor_scalar(xn[:, u, j, :], xs[:, bass.ds(t, 1), :].rearrange("p o d -> p (o d)"),
                                               mean[:, bass.ds(t, 1)], rstd[:, bass.ds(t, 1)],
                                               ALU.subtract, ALU.mult)
                    last.then_inc(s_xn2, 1)
                    dve.wait_ge(s_hT2, n + 1)
                    cols = bass.ds(n * CH, CH)
                    V.tensor_copy(h2_hi[:, cols], hT[:, u, :]).then_inc(s_link, 1)
                    dve.wait_ge(s_link, n + (base3 + 1))
                    V.tensor_tensor(h2_lo[:, cols], hT[:, u, :], h2_hi[:, cols].bitcast(F32), ALU.subtract).then_inc(s_split2, 1)
                    dve.wait_ge(s_lg, n + 1)
                    V.tensor_tensor(logit[:, bass.ds(tile_pair(b, u), CG), :],
                                    ps[:, 6 + u, 0:CG * NE].rearrange("p (j e) -> p j e", j=CG),
                                    rb[:].unsqueeze(1).to_broadcast((T, CG, NE)), ALU.add).then_inc(s_lg_free, 1)
            chain[0] = base3 + 2 * B

            for e in range(EX):
                dve.wait_ge(s_wraw[e % 2], 32 * (e // 2 + 1))
                V.tensor_copy(w_hi[:, e, :, :], w_raw[:, e % 2, :, :]).then_inc(s_wsplit, 1)
                dve.wait_ge(s_wsplit, 2 * e + 1)
                V.tensor_tensor(w_lo[:, e, :, :], w_raw[:, e % 2, :, :], w_hi[:, e, :, :].bitcast(F32),
                                ALU.subtract).then_inc(s_wsplit, 1)

            dve.wait_ge(s_lg_free, 2 + 2 * B)
            link(V.tensor_reduce(rsum[:], logit[:], AX.X, ALU.max))
            V.tensor_tensor(logit[:], logit[:], rsum[:].unsqueeze(2).to_broadcast((T, NT, NE)), ALU.subtract).then_inc(s_max7, 1)
            dve.wait_ge(s_exp7, 1)
            link(V.reduce_sum(rsum[:], prob[:], AX.X))
            link(V.reciprocal(rsum[:], rsum[:]))
            link(V.tensor_tensor(prob[:], prob[:], rsum[:].unsqueeze(2).to_broadcast((T, NT, NE)), ALU.mult))
            link(V.memset(rank[:], 0.0))
            for j in range(NE):
                pj = prob[:, :, j:j + 1]
                if j:
                    V.tensor_tensor(beats[:, :, 0:j], pj.to_broadcast((T, NT, j)), prob[:, :, 0:j], ALU.is_gt)
                if j < NE - 1:
                    V.tensor_tensor(beats[:, :, j + 1:NE], pj.to_broadcast((T, NT, NE - 1 - j)), prob[:, :, j + 1:NE], ALU.is_ge)
                link(V.memset(beats[:, :, j:j + 1], 0.0))
                link(V.tensor_tensor(rank[:], rank[:], beats[:], ALU.add))
            link(V.tensor_scalar(rank[:], rank[:], 1.5, None, ALU.is_lt))
            link(V.tensor_tensor(prob[:], prob[:], rank[:], ALU.mult))
            link(V.reduce_sum(rsum[:], prob[:], AX.X))
            link(V.reciprocal(rsum[:], rsum[:]))
            link(V.tensor_tensor(route[:], prob[:], rsum[:].unsqueeze(2).to_broadcast((T, NT, NE)), ALU.mult))

            base4 = chain[0]

            def gather(b, u, e):
                d = (b * 2 + u) * EX + e
                dve.wait_ge(s_dn, d + 1)
                src = ps[:, 6 + e % 2, :].rearrange("p (j d) -> p j d", j=CG)
                if e == 0:
                    V.tensor_copy(acc[:, u, :, :], src).then_inc(s_dn_free, 1)
                else:
                    dve.wait_ge(s_dn_free, d + 2)
                    for j in range(CG):
                        w = route[:, bass.ds(b * TB + (u * CG + j), 1), e - 1]
                        last = V.scalar_tensor_tensor(acc[:, u, j, :], src[:, j, :], w, acc[:, u, j, :],
                                                      ALU.mult, ALU.add)
                    last.then_inc(s_dn_free, 1)

            def finish(b, u):
                n = b * 2 + u
                dve.wait_ge(s_dn_free, (n + 1) * EX + 2)
                V.tensor_tensor(acc[:, u, :, :], acc[:, u, :, :], gate_b[:, bass.ds(b, 1), :].to_broadcast((T, CG, D)),
                                ALU.mult).then_inc(s_link, 1)
                dve.wait_ge(s_link, n + (base4 + 1))
                xt = xs[:, bass.ds(tile_pair(b, u), CG), :]
                V.tensor_tensor(xt, xt, acc[:, u, :, :], ALU.add).then_inc(s_res, 1)

            with dve.Fori(0, B) as b:
                for u in range(2):
                    for e in range(EX):
                        for c, (i0, w) in enumerate(IC):
                            g = (b * 2 + u) * (EX * len(IC)) + e * len(IC) + c
                            dve.wait_ge(s_silu, g + 1)
                            V.tensor_tensor(hid[0:w, e % 2, c, :], sg[0:w, c, :], ps[0:w, 2 * c + 1, :],
                                            ALU.mult).then_inc(s_hid, 1)
                        if e:
                            gather(b, u, e - 1)
                    gather(b, u, EX - 1)
                    finish(b, u)

        @block.tensor
        def _(pe):
            MM = nc.tensor.matmul
            pe.wait_ge(s_in0, 48)
            pe.wait_ge(s_csilu, 1)
            for k, j in enumerate((0, 1, 3, 4)):
                MM(ps[:, 0, k * B:(k + 1) * B], wmod[:, j, :], c_s[:], start=True, stop=True)
            pe.wait_ge(s_cb, 1)
            for bank, j in ((1, 2), (2, 5)):
                for b in range(B):
                    last = MM(ps[:, bank, b * D:(b + 1) * D], c_b[:, b, :], wmod[:, j, :], start=True, stop=True)
            last.then_inc(s_modps, 1)
            pe.wait_ge(s_mod, 1)
            pe.wait_ge(s_in, 16 * 9)

            with pe.Fori(0, B) as b:
                for u in range(2):
                    n = b * 2 + u
                    pe.wait_ge(s_xn, n + 1)
                    pe.wait_ge(s_hT_free, n + 1)
                    for j in range(CG):
                        last = nc.tensor.transpose(ps[:, u, j * T:(j + 1) * T], xn[:, u, j, :], eye[:])
                    last.then_inc(s_tp, 1)
                    pe.wait_ge(s_hT, n + 1)
                    pe.sem_inc(s_xn_free, 1)
                    for w, mat in enumerate((wq, wk)):
                        pe.wait_ge(s_qk_free, n * 2 + w + 1)
                        for j in range(2):
                            last = MM(ps[:, 2 + 2 * w + j, :], mat[:, j, :], hT[:, u, :], start=True, stop=True)
                        last.then_inc(s_qk, 1)
                    for j in range(CG):
                        last = MM(ps[:, 6 + u, j * D:(j + 1) * D], hT[:, u, j * T:(j + 1) * T], wv[:], start=True, stop=True)
                    last.then_inc(s_v, 1)
                    pe.wait_ge(s_v_free, n + 1)
                    pe.sem_inc(s_hT_free, 1)

            def piece(m, bank, what):
                h, q, k0, w, diag = PIECES[what]
                return MM(ps[:, bank, 0:w], qa[m][0:KR, h * S + q * T:h * S + (q + 1) * T],
                          ka[m][0:KR, h * S + k0:h * S + k0 + w], start=True, stop=True)

            def ring_write(i, r, bank, kind, off, what):
                m = (r + off) % 3
                if kind == "max":
                    if what == 0:
                        pe.wait_ge(s_qk_in[m], (third(i, r + off) + 1) * (2 * NP * 16))
                    last = piece(m, bank, what)
                elif kind == "shift":
                    pe.wait_ge(s_rowmax, quad(i, r + off) + 1)
                    last = nc.tensor.transpose(ps[0:HQ * TB, bank, 0:T],
                                               rowmax[m][:].rearrange("p h q -> p (h q)"), eye[:])
                else:
                    pe.wait_ge(s_outT, 2 * quad(i, r + off) + what + 1)
                    for j in range(CG):
                        last = nc.tensor.transpose(ps[:, bank, j * T:(j + 1) * T], outT[:, what, j * T:(j + 1) * T], eye[:])
                last.then_inc(s_ring, 1)

            for k, (kind, off, what) in enumerate(PRE):
                if k >= RING:
                    pe.wait_ge(s_ring_free, k - RING + 1)
                ring_write(0, 0, 5 + k % RING, kind, off, what)

            def values_product(i, r, s):
                c, k, q0 = STEPS[s]
                n, m = quad(i, r), r % 3
                pe.wait_ge(s_exp, n * (2 * NS) + 2 * s + 2)
                if k >= CG * c:
                    diag = s if c == 0 else s - NS + 2 * CG
                    pe.wait_ge(s_mask, n * (2 * CG) + diag + 1)
                if s == 0:
                    pe.wait_ge(s_v4, n + 1)
                if k == 0 and not (isinstance(i, int) and n == 0 and c == 0):
                    pe.wait_ge(s_outT, 2 * n + c)
                for h in range(HQ):
                    last = MM(ps[VW * h:VW * (h + 1), 4, q0:CH], v4[m][:, k, h, :], probs[s % 4][:, h, 0:CH - q0],
                              start=(k == 0), stop=(k == CG * (c + 1) - 1))
                last.then_inc(s_pv, 1)

            def body(i, r):
                n, m = quad(i, r), r % 3
                first = isinstance(i, int) and n == 0
                plan = plan_of(i, r)
                rbase = ring_base(i, r)
                pe.wait_ge(s_m_in[m], (third(i, r) + 1) * (16 * NP))
                ks = [0]

                def ring_entries(slot):
                    while ks[0] < len(plan) and plan[ks[0]][0] <= slot:
                        k = ks[0]
                        _, kind, off, what = plan[k]
                        pe.wait_ge(s_ring_free, rbase + (k + 1 - RING))
                        ring_write(i, r, 5 + ring_bank(i, r, k), kind, off, what)
                        ks[0] += 1

                for s, (c, kb, q0) in enumerate(STEPS):
                    for h in range(HQ):
                        if h % 2 == 0 and not (first and s == 0):
                            pe.wait_ge(s_exp, n * (2 * NS) + 2 * s + h // 2 - 1)
                        last = MM(ps[:, h, q0:CH], ka[m][0:KM, h * S + kb * T:h * S + (kb + 1) * T],
                                  qa[m][0:KM, h * S + c * CH + q0:h * S + (c + 1) * CH], start=True, stop=True)
                        if h % 2:
                            last.then_inc(s_scores, 1)
                            ring_entries(s * SLOTS + h // 2)
                    if s >= 2:
                        values_product(i, r, s - 2)
                    elif not first:
                        values_product(i, r - 1, NS - 2 + s)
                    ring_entries(s * SLOTS + 2)
            quads(pe, body)
            values_product(5, 0, NS - 2)
            values_product(5, 0, NS - 1)
            endbase = ring_base(5, 1)
            pe.wait_ge(s_ring_free, endbase + 1 - RING)
            ring_write(5, 1, 5 + endbase % RING, "norm", -1, 1)
            pe.wait_ge(s_ring_free, ring_base(0, NQ) + 1)

            with pe.Fori(0, B) as b:
                for u in range(2):
                    n = b * 2 + u
                    pe.wait_ge(s_otile, n + 1)
                    for j in range(CG):
                        last = nc.tensor.transpose(ps[:, u, j * T:(j + 1) * T], o_tile[:, u, j, :], eye[:])
                    last.then_inc(s_ot, 1)
                    pe.wait_ge(s_oT, n + 1)
                    for j in range(CG):
                        last = MM(ps[:, 2 + u, j * D:(j + 1) * D], oT[:, u, j * T:(j + 1) * T], wo[:], start=True, stop=True)
                    last.then_inc(s_proj, 1)
                    pe.wait_ge(s_x2, n + 1)

            with pe.Fori(0, B) as b:
                for u in range(2):
                    n = b * 2 + u
                    pe.wait_ge(s_xn2, n + 1)
                    for j in range(CG):
                        last = nc.tensor.transpose(ps[:, 4 + u, j * T:(j + 1) * T], xn[:, u, j, :], eye[:])
                    last.then_inc(s_tp2, 1)
                    pe.wait_ge(s_hT2, n + 1)
                    for j in range(CG):
                        last = MM(ps[:, 6 + u, j * NE:(j + 1) * NE], hT[:, u, j * T:(j + 1) * T], wr[:], start=True, stop=True)
                    last.then_inc(s_lg, 1)

            pe.wait_ge(s_lg_free, 2 + 2 * B)
            pe.wait_ge(s_split2, 2 * B)
            pe.wait_ge(s_wsplit, 2 * EX)
            pe.wait_ge(s_wd, 16 * len(IC))

            def down(b, u, e):
                d = (b * 2 + u) * EX + e
                pe.wait_ge(s_hid, (d + 2) * len(IC))
                pe.wait_ge(s_dn_free, d + 1)
                for j in range(CG):
                    for c, (i0, w) in enumerate(IC):
                        last = MM(ps[:, 6 + e % 2, j * D:(j + 1) * D], hid[0:w, e % 2, c, j * T:(j + 1) * T],
                                  wd[0:w, e, c, :], start=(c == 0), stop=(c == len(IC) - 1))
                last.then_inc(s_dn, 1)

            with pe.Fori(0, B) as b:
                for u in range(2):
                    cols = bass.ds((b * 2 + u) * CH, CH)
                    for e in range(EX):
                        d = (b * 2 + u) * EX + e
                        for c, (i0, w) in enumerate(IC):
                            pe.wait_ge(s_hid, d * len(IC) + c + 1)
                            for g in range(2):
                                trio = ((w_hi, h2_hi), (w_lo, h2_hi), (w_hi, h2_lo))
                                for k, (wt, ht) in enumerate(trio):
                                    last = MM(ps[0:w, 2 * c + g, :], wt[:, e, g, i0:i0 + w], ht[:, cols],
                                              start=(k == 0), stop=(k == 2))
                            last.then_inc(s_gu, 1)
                        if e:
                            down(b, u, e - 1)
                    down(b, u, EX - 1)


_INS = ["x", "wq", "wk", "wv", "wo", "gate", "up", "down", "wr", "rb", "c", "wmod", "cos", "sin", "eye", "tri"]


def kernel(L0_attn_x, L0_attn_W_q, L0_attn_W_k, L0_attn_W_v, L0_attn_W_o, L0_ffn_sg, L0_ffn_su, L0_ffn_sd,
           L0_ffn_rg, L0_ffn_ru, L0_ffn_rd, L0_ffn_wr, L0_ffn_rb, L0_c, L0_wmod):
    import concourse.bacc as bacc
    from concourse.bass_utils import run_bass_kernel_spmd

    def rows(w, swap):
        w = np.asarray(w).reshape(NG, HQ, DK, D)
        if swap:
            w = w[:, :, [d ^ 1 for d in range(DK)], :]
        return w.transpose(0, 2, 1, 3).reshape(D, D).T

    def both(w):
        return np.stack([rows(w, False), rows(w, True)])

    freq = np.float32(10000.0) ** (np.float32(-2.0) * np.arange(DK // 2, dtype=np.float32) / np.float32(DK))
    ang = np.arange(S, dtype=np.float32)[:, None] * freq[None, :].astype(np.float32)
    dim = (np.arange(D) // HQ) % DK
    cos = np.cos(ang)[:, dim // 2].T
    sin = np.sin(ang)[:, dim // 2].T * np.where(dim % 2 == 0, -1.0, 1.0)[:, None]
    tri = np.zeros((T, CH), np.float32)
    tri[:, CH - T:] = np.where(np.arange(T)[None, :] > np.arange(T)[:, None], LOW, 0.0)

    def experts(shared, routed):
        return np.concatenate([np.asarray(shared)[None], np.asarray(routed)])

    vals = [
        np.asarray(L0_attn_x).reshape(B * S, D), both(L0_attn_W_q), both(L0_attn_W_k),
        np.asarray(L0_attn_W_v).T, np.asarray(L0_attn_W_o).T,
        experts(L0_ffn_sg, L0_ffn_rg).transpose(0, 2, 1), experts(L0_ffn_su, L0_ffn_ru).transpose(0, 2, 1),
        experts(L0_ffn_sd, L0_ffn_rd).transpose(0, 2, 1), np.asarray(L0_ffn_wr).T,
        np.asarray(L0_ffn_rb).reshape(1, NE), np.asarray(L0_c).T, np.asarray(L0_wmod),
        cos.astype(np.float32), sin.astype(np.float32), np.eye(128, dtype=np.float32), tri,
    ]
    nc = bacc.Bacc("TRN2", target_bir_lowering=False, num_devices=1)
    arrays, args = {}, []
    for name, a in zip(_INS, vals):
        a = np.ascontiguousarray(a)
        arrays[f"in_{name}"] = a
        args.append(nc.dram_tensor(f"in_{name}", a.shape, mybir.dt.from_np(a.dtype), kind="ExternalInput").ap())
    out = nc.dram_tensor("out", (B * S, D), F32, kind="ExternalOutput").ap()
    adaln_block(nc, *args, out)
    r = run_bass_kernel_spmd(nc, [arrays], core_ids=[0])
    return r.results[0]["out"].reshape(B, S, D)
```

```python
from contextlib import ExitStack

import numpy as np

import concourse.bass as bass
from concourse import mybir

F32 = mybir.dt.float32
BF16 = mybir.dt.bfloat16
I32 = mybir.dt.int32
F32R = mybir.dt.float32r
ALU = mybir.AluOpType
ACT = mybir.ActivationFunctionType
AX = mybir.AxisListType

B, S, D = 4, 1024, 128
NH, DK = 16, 8
HQ = 4
NG = NH // HQ
NQ = B * NG
T = 128
TB = S // T
NT = B * TB
CH = 512
NP = 3
KR = NP * NP * DK
KM = KR + NP
VW = 32
NE, NI = 7, 352
EX = NE + 1
IC = [(0, 128), (128, 128), (256, 96)]
EPS = 1e-5
SCALE = float(DK) ** -0.5
LOW = -3.0e38
CG = CH // T
TOP = 2
ST = (TOP * B * S + NE * (T - 1)) // T
RW = D + 2 * NE
SB = 4
SU = 2 * SB
CST, _at = {}, 0
for _name, _w in (("before", T), ("ones", T), ("steps", NT), ("tiles", ST), ("token", NT), ("pad", RW), ("spare", ST)):
    CST[_name] = (_at, _w)
    _at += _w
CSTW = _at

STEPS = [(c, k, max(0, k - CG * c) * T) for c in range(S // CH) for k in range(CG * (c + 1))]
NS = len(STEPS)
HEAD_BANKS = [
    [(0, 0, T, True), (2, 0, 3 * T, True)],
    [(1, 0, 2 * T, True), (5, CH, 2 * T, True)],
    [(3, 0, CH, True)],
    [(4, CH, T, True), (6, CH, 3 * T, True)],
    [(7, CH, CH, True)],
] + [[(q, 0, CH, False)] for q in range(CG, TB)]
assert TB == 2 * CG == 8 and sum(w for bank in HEAD_BANKS for _, _, w, _ in bank) == T * TB * (TB + 1) // 2
PIECES = [(h, bank) for h in range(HQ) for bank in HEAD_BANKS]
NM = len(PIECES)
EARLY = NM // HQ
SLOTS = 3
STEP_COST = 60
SHIFT_SLOT = (NS - 3) * SLOTS
RING = 3


def ring_plan(back, ahead1, ahead2):
    pieces = [("max", 1, p) for p in range(EARLY, NM)] if ahead1 else []
    late = [("max", 2, p) for p in range(EARLY)] if ahead2 else []
    if ahead1:
        late.insert(min(3, len(late)), ("shift", 1, None))
    slots, total = [], 0
    for s, (_, _, q0) in enumerate(STEPS):
        for j in range(SLOTS):
            total += STEP_COST + CH - q0
            slots.append((total, s * SLOTS + j))
    scale = total / len(PIECES)
    plan, at = [], 0
    for kind, off, p in pieces + late:
        slot = next((s for end, s in slots if at < end), NS * SLOTS - 1)
        if not ahead2 and kind == "shift":
            slot = SHIFT_SLOT
        plan.append((slot, kind, off, p))
        at += scale if kind == "max" else 0
    out = []
    for s in range(NS * SLOTS):
        if s == 3 * SLOTS and back:
            out.append((s, "norm", -1, 1))
        if s == 7 * SLOTS:
            out.append((s, "norm", 0, 0))
        out += [x for x in plan if x[0] == s]
    return out


def adaln_block(nc, x_d, wq_d, wk_d, wv_d, wo_d, sw_g_d, sw_u_d, sw_d_d, wr_d, rb_d, c_d, wmod_d,
                cos_d, sin_d, eye_d, tri_d, cst_d, out_d):
    KPART = [0, 1, 2, 0, 1]
    qs_d = nc.dram_tensor("q_parts_scratch", [NQ, NP, DK * HQ, S], BF16, kind="Internal").ap()
    ks_d = nc.dram_tensor("k_parts_scratch", [NQ, len(KPART), DK * HQ, S], BF16, kind="Internal").ap()

    slot_d = nc.dram_tensor("slot_rows_scratch", [ST * T, RW], F32, kind="Internal").ap()
    y_d = nc.dram_tensor("routed_results_scratch", [TOP * B * S + ST * T, D], F32, kind="Internal").ap()

    ctx = ExitStack()
    with ctx:
        def sb(name, shape, dt=F32, at=None):
            return (at or ctx).enter_context(nc.sbuf_tensor(name, shape, dt))

        def sem(name):
            return ctx.enter_context(nc.semaphore(name))

        xs = sb("xs", [T, NT, D])
        eye = sb("eye", [128, 128])
        wo = sb("wo", [D, D])
        gate_a = sb("gate_a", [128, B, D])
        gate_b = sb("gate_b", [128, B, D])
        mod2_rows = sb("mod2_rows", [128, 2, B, D])
        cst = sb("cst", [128, CSTW])
        mod1 = sb("mod1", [D, 2, B])
        mod2 = sb("mod2", [D, 2, B])
        xn = sb("xn", [T, NT, D])
        o_quads = xn[:].rearrange("p t d -> p (t d)").rearrange("p (k n e) -> p k n e", k=TB, n=NQ)
        o_rows = xn[:].rearrange("p t d -> p (t d)").rearrange("p (k b d) -> p k b d", k=TB, b=B)
        stats = sb("stats", [T, NT, 6])
        mean = sb("mean", [T, NT])
        part_a = sb("part_a", [T, NT])
        part_b = sb("part_b", [T, NT])
        rstd = sb("rstd", [T, NT])
        rb = sb("rb", [128, NE])
        wr = sb("wr", [D, NE])
        hT = sb("hT", [D, 2, CH])

        att = ExitStack()
        v_all = sb("v_all", [T, NQ, TB, HQ * DK], at=att)
        qa = [sb(f"qa{m}", [KM, HQ * S], BF16, at=att) for m in range(3)]
        ka = [sb(f"ka{m}", [KM, HQ * S], BF16, at=att) for m in range(3)]
        v4 = [sb(f"v4_{m}", [T, TB, HQ, VW], at=att) for m in range(3)]
        tri = sb("tri", [T, CH], at=att)
        rowmax = [sb(f"rowmax{m}", [T, HQ, TB], at=att) for m in range(3)]
        leftmax = [sb(f"leftmax{m}", [T, HQ, TB - CG], at=att) for m in range(3)]
        mparts = [sb(f"mparts{m}", [HQ * TB, NP, T], BF16, at=att) for m in range(3)]
        mrest = sb("mrest", [HQ * TB, T], at=att)
        junk = sb("junk", [T, RING, CH], at=att)
        outT = sb("outT", [128, 2, CH], at=att)
        recip = sb("recip", [T, CG, HQ], at=att)
        pre = ExitStack()
        wq = sb("wq", [D, 2, D], at=pre)
        wk = sb("wk", [D, 2, D], at=pre)
        wv = sb("wv", [D, D], at=pre)
        c_t = sb("c_t", [D, B], at=pre)
        c_s = sb("c_s", [D, B], at=pre)
        c_b = sb("c_b", [D, B, 128], at=pre)
        wmod = sb("wmod", [D, 6, D], at=pre)
        cos = sb("cos", [128, S], at=pre)
        sin = sb("sin", [128, S], at=pre)
        rot = sb("rot", [128, 2, 2, 2, CH], at=pre)
        qk_parts = sb("qk_parts", [128, 2, 2, NP, CH], BF16, at=pre)
        pre.close()
        probs = [sb(f"probs{m}", [T, HQ, CH], at=att) for m in range(4)]
        att.close()

        moe = ctx
        h2_hi = sb("h2_hi", [D, NT * T], F32R, at=moe)
        h2_lo = sb("h2_lo", [D, NT * T], F32R, at=moe)
        w_raw = sb("w_raw", [D, 2, 2, NI], at=moe)
        w_hi = sb("w_hi", [D, EX, 2, NI], F32R, at=moe)
        w_lo = sb("w_lo", [D, EX, 2, NI], F32R, at=moe)
        wd = sb("wd", [128, EX, len(IC), D], at=moe)
        rows = sb("rows", [T, NT, RW], at=moe)
        oT = sb("oT", [D, 2, CH], at=moe)
        att_o = sb("att_o", [T, 2, CH], at=moe)
        logit = sb("logit", [T, NT, NE], at=moe)
        prob = sb("prob", [T, NT, NE], at=moe)
        rank = sb("rank", [T, NT, NE], at=moe)
        beats = sb("beats", [T, NT, NE], at=moe)
        rsum = sb("rsum", [T, NT], at=moe)
        sel = sb("sel", [T, NT, NE], at=moe)
        tot = sb("tot", [T, NT, NE], at=moe)
        scan = sb("scan", [T, 2, NT, NE], at=moe)
        reached = sb("reached", [T, NE, NT], at=moe)
        tcount = sb("tcount", [T, NE], at=moe)
        tend = sb("tend", [T, 2, NE], at=moe)
        tbase = sb("tbase", [T, NE], at=moe)
        passed = sb("passed", [1, ST, NE], at=moe)
        expert_f = sb("expert_f", [1, ST], at=moe)
        expert = sb("expert", [1, ST], I32, at=moe)
        slot_f = sb("slot_f", [T, TOP, NT], at=moe)
        slot = sb("slot", [T, TOP, NT], I32, at=moe)
        acc = sb("acc", [T, 2, CG, D], at=moe)
        sg = sb("sg", [128, 2, NI], at=moe)
        srow = sb("srow", [T, SB, RW], at=moe)
        s_weight = sb("s_weight", [T, ST], at=moe)
        s_dest_f = sb("s_dest_f", [T, ST], at=moe)
        s_dest = sb("s_dest", [T, SB], I32, at=moe)
        shared_only = ExitStack()
        sgs = sb("sgs", [128, 3, CH], at=shared_only)
        hid = sb("hid", [128, 2, len(IC), CH], at=shared_only)
        shared_only.close()
        h_hi = sb("h_hi", [D, 2, T], F32R, at=moe)
        h_lo = sb("h_lo", [D, 2, T], F32R, at=moe)
        hid_s = sb("hid_s", [T, 2, NI], at=moe)
        hidT = sb("hidT", [128, 2, len(IC), T], at=moe)
        y_s = sb("y_s", [T, SB, D], at=moe)
        y_in = [h2_hi[:].bitcast(F32).rearrange("p (t d) -> p t d", t=NT),
                h2_lo[:].bitcast(F32).rearrange("p (t d) -> p t d", t=NT)]

        ps = ctx.enter_context(nc.psum_tensor("ps", [128, 8, CH], F32))

        s_in0 = sem("s_in0")
        s_in = sem("s_in")
        s_x = [sem(f"s_x_row{b}") for b in range(B)]
        s_link = sem("s_link")
        s_glink = sem("s_glink")
        s_csilu = sem("s_csilu")
        s_cb = sem("s_cb")
        s_modps = sem("s_modps")
        s_mod = sem("s_mod")
        s_raw = sem("s_raw")
        s_var = sem("s_var")
        s_std = sem("s_std")
        s_seen_act, s_seen_pool, s_seen_dve = sem("s_seen_act"), sem("s_seen_pool"), sem("s_seen_dve")
        s_xn = sem("s_xn")
        s_tp = sem("s_tp")
        s_hT = sem("s_hT")
        s_qk = sem("s_qk")
        s_prod = sem("s_prod")
        s_sum = sem("s_sum")
        s_hi = sem("s_hi")
        s_rest = sem("s_rest")
        s_mid = sem("s_mid")
        s_v = sem("s_v")
        s_v_free = sem("s_v_free")
        s_parts = sem("s_parts")
        s_spill = [sem(f"s_spill{m}") for m in range(2)]
        s_fill = sem("s_fill")
        s_qk_in = [sem(f"s_qk_in{m}") for m in range(3)]
        s_ring = sem("s_ring")
        s_ring_free = sem("s_ring_free")
        s_rowmax = sem("s_rowmax")
        s_mparts = sem("s_mparts")
        s_m_in = [sem(f"s_m_in{m}") for m in range(3)]
        s_scores = sem("s_scores")
        s_exp = sem("s_exp")
        s_mask = sem("s_mask")
        s_pv = sem("s_pv")
        s_outT = sem("s_outT")
        s_v4 = sem("s_v4")
        s_ot = sem("s_ot")
        s_oT = sem("s_oT")
        s_proj = sem("s_proj")
        s_gated = sem("s_gated")
        s_x2 = sem("s_x2")
        s_var2 = sem("s_var2")
        s_std2 = sem("s_std2")
        s_xn2 = sem("s_xn2")
        s_tp2 = sem("s_tp2")
        s_hT2 = sem("s_hT2")
        s_lg = sem("s_lg")
        s_lg_free = sem("s_lg_free")
        s_h2_hi = sem("s_h2_hi")
        s_split2 = sem("s_split2")
        s_max7 = sem("s_max7")
        s_exp7 = sem("s_exp7")
        s_wraw = [sem(f"s_wraw{m}") for m in range(2)]
        s_whi = sem("s_whi")
        s_wlo = sem("s_wlo")
        s_wd = sem("s_wd")
        s_gu = sem("s_gu")
        s_silu = sem("s_silu")
        s_hid = sem("s_hid")
        s_dn = sem("s_dn")
        s_dn_free = sem("s_dn_free")
        s_shared = sem("s_shared")
        s_rows = sem("s_rows")
        s_sel = sem("s_sel")
        s_prefix = sem("s_prefix")
        s_slot = sem("s_slot")
        s_pad_out = sem("s_pad_out")
        s_scatter = sem("s_scatter")
        s_srow = [sem(f"s_srow{j}") for j in range(SB)]
        s_rowT = sem("s_rowT")
        s_meta = sem("s_meta")
        s_h_hi = sem("s_h_hi")
        s_h_lo = sem("s_h_lo")
        s_sgu = sem("s_sgu")
        s_ssilu = sem("s_ssilu")
        s_shid = sem("s_shid")
        s_shidT = sem("s_shidT")
        s_hidT = sem("s_hidT")
        s_sdn = sem("s_sdn")
        s_y = sem("s_y")
        s_dest_i = sem("s_dest_i")
        s_y_out = [sem(f"s_y_out{j}") for j in range(SB)]
        s_y_in = [sem(f"s_y_in{b}") for b in range(B)]
        s_res = sem("s_res")
        s_out = sem("s_out")

        block = ctx.enter_context(nc.Block())

        def quad(i, r):
            return 3 * i + r

        def third(i, r):
            return i + r // 3

        FULL = ring_plan(True, True, True)
        FIRST = ring_plan(False, True, True)
        PRE = [("max", 0, p) for p in range(NM)] + [("shift", 0, None)] + [("max", 1, p) for p in range(EARLY)]
        LAST1 = ring_plan(True, True, False)
        LAST0 = ring_plan(True, False, False)
        R1 = len(PRE) + len(FIRST)
        RL = len(FULL)
        assert RL % RING == 0

        def ring_base(i, r):
            if isinstance(i, int):
                n = quad(i, r)
                if n == 0:
                    return len(PRE)
                return R1 + RL * (min(n, NQ - 2 + 0) - 1) + (len(LAST1) if n >= NQ - 1 else 0) \
                    + (len(LAST0) if n >= NQ else 0)
            return quad(i, r) * RL + (R1 - RL)

        def ring_bank(i, r, k):
            if isinstance(i, int):
                return (ring_base(i, r) + k) % RING
            return (R1 + k) % RING

        def plan_of(i, r):
            if isinstance(i, int):
                n = quad(i, r)
                return {0: FIRST, NQ - 2: LAST1, NQ - 1: LAST0}.get(n, FULL)
            return FULL

        def quads(eng, body):
            body(0, 0)
            with eng.Fori(0, 4) as i:
                for r in (1, 2, 3):
                    body(i, r)
            for r in (1, 2, 3):
                body(4, r)

        def slot_steps(eng, first, last, body):
            stop = (ST - SB - 1) // SU
            for s in range(first, SU):
                body(0, s)
            with eng.Fori(1, stop) as i:
                for r in range(SU):
                    body(i, r)
            for s in range(stop * SU, last + 1):
                body(0, s)

        def tile(i, r, lag):
            t = SU * i + (r - lag)
            if isinstance(t, int) and not 0 <= t < ST:
                return None
            return t, (r - lag) % SB, SU // SB * i + (r - lag) // SB

        def needs(eng, semaphore, value):
            if not (isinstance(value, int) and value <= 0):
                eng.wait_ge(semaphore, value)

        @block.sync
        def _(sp):
            for dst, src in ((c_t[:], c_d), (wmod[:], wmod_d.rearrange("k (j f) -> k j f", j=6)),
                             (eye[:], eye_d)):
                sp.dma_start(dst, src).then_inc(s_in0, 16)
            xv = x_d.rearrange("(t p) d -> p t d", p=T)
            for b in range(B):
                sp.dma_start(xs[:, b * TB:(b + 1) * TB, :], xv[:, b * TB:(b + 1) * TB, :]).then_inc(s_x[b], 16)
            for dst, src in ((wq[:], wq_d.rearrange("j k m -> k j m")), (wk[:], wk_d.rearrange("j k m -> k j m")),
                             (wv[:], wv_d), (cos[:], cos_d), (sin[:], sin_d), (wo[:], wo_d), (tri[:], tri_d),
                             (wr[:], wr_d), (rb[:], rb_d[0:1, :].to_broadcast((128, NE))), (cst[:], cst_d)):
                sp.dma_start(dst, src).then_inc(s_in, 16)

            def spill(b, u):
                for w, (scr, kept) in enumerate(((qs_d, range(NP)), (ks_d, KPART))):
                    sp.wait_ge(s_parts, (b * 2 + u) * 2 + w + 1)
                    for slot, p in enumerate(kept):
                        dst = scr[bass.ds(b * NG, NG), slot, :, u * CH:(u + 1) * CH]
                        sp.dma_start(dst, qk_parts[:, u, w, p, :]).then_inc(s_spill[u], 16)

            def load_quad(i, r):
                n, m = quad(i, r), r % 3
                q = qs_d[bass.ds(n, 1), :, :, :].rearrange("n p (d h) s -> (n p d) (h s)", h=HQ)
                k = ks_d[bass.ds(n, 1), :, :, :].rearrange("n p (d h) s -> (n p d) (h s)", h=HQ)
                w = NP * DK
                for j in range(NP):
                    sp.dma_start(qa[m][j * w:(j + 1) * w, :], q[0:w, :]).then_inc(s_qk_in[m], 16)
                    sp.dma_start(ka[m][j * w:(j + 1) * w, :], k[j * DK:j * DK + w, :]).then_inc(s_qk_in[m], 16)

            def load_shift(i, r):
                m = r % 3
                sp.wait_ge(s_mparts, quad(i, r) + 1)
                for p in range(NP):
                    sp.dma_start(qa[m][KR + p:KR + p + 1, :].rearrange("o (a t) -> o a t", t=T),
                                 mparts[m][:, p, :]).then_inc(s_m_in[m], 16)

            UNIT = 16 * (NP + len(KPART))
            for u in range(2):
                spill(0, u)
            for u in range(2):
                sp.wait_ge(s_spill[u], UNIT + 16)
            sp.wait_ge(s_fill, 1)
            for r in range(2):
                load_quad(0, r)
            with sp.Fori(1, B) as b:
                for u in range(2):
                    spill(b, u)
            for u in range(2):
                sp.wait_ge(s_spill[u], B * UNIT + 16)
            load_shift(0, 0)

            pad0, _ = CST["pad"]
            sp.wait_ge(s_in, 16 * 10)
            sp.dma_start(slot_d.rearrange("(t p) c -> p t c", p=T),
                         cst[:, pad0:pad0 + RW].unsqueeze(1).to_broadcast((T, ST, RW))).then_inc(s_pad_out, 16)

            def body(i, r):
                n = quad(i, r)
                if not (isinstance(i, int) and n + 2 >= NQ):
                    if not (isinstance(i, int) and n == 0):
                        sp.wait_ge(s_scores, n * (2 * NS))
                    load_quad(i, r + 2)
                if not (isinstance(i, int) and n + 1 >= NQ):
                    load_shift(i, r + 1)
            quads(sp, body)

            sp.wait_ge(s_ring_free, ring_base(0, NQ) + 1)
            for c, (i0, w) in enumerate(IC):
                sp.dma_start(wd[0:w, :, c, :], sw_d_d[:, i0:i0 + w, :].rearrange("e p h -> p e h")).then_inc(s_wd, 16)
            for e in range(EX):
                if e >= 2:
                    sp.wait_ge(s_wlo, e - 1)
                sp.dma_start(w_raw[:, e % 2, 0, :], sw_g_d[e, :, :]).then_inc(s_wraw[e % 2], 16)
                sp.dma_start(w_raw[:, e % 2, 1, :], sw_u_d[e, :, :]).then_inc(s_wraw[e % 2], 16)

            sp.wait_ge(s_scatter, 16 * TOP * NT)

            def load_rows(i, r):
                at = tile(i, r, -SB - 1)
                if at:
                    t, j, times = at
                    needs(sp, s_rowT, t - SB + 1)
                    needs(sp, s_meta, t - SB + 1)
                    sp.dma_start(srow[:, j, :], slot_d[bass.ds(t * T, T), :]).then_inc(s_srow[j], 16)
            slot_steps(sp, -SB - 1, ST - SB - 2, load_rows)

            yv = y_d[0:TOP * B * S, :].rearrange("(k t p) d -> k p t d", k=TOP, p=T)
            for j in range(SB):
                sp.wait_ge(s_y_out[j], 16 * ((ST + SB - 1 - j) // SB))
            for b in range(B):
                for k in range(TOP):
                    sp.dma_start(y_in[k][:, b * TB:(b + 1) * TB, :], yv[k, :, b * TB:(b + 1) * TB, :]).then_inc(s_y_in[b], 16)
            ov = out_d.rearrange("(t p) d -> p t d", p=T)
            for n in range(2 * B):
                sp.wait_ge(s_res, n + 1)
                sp.dma_start(ov[:, n * CG:(n + 1) * CG, :], xs[:, n * CG:(n + 1) * CG, :]).then_inc(s_out, 16)
            sp.wait_ge(s_out, 16 * 2 * B)

        @block.gpsimd
        def _(pool):
            for m in range(3):
                nc.gpsimd.memset(ka[m][64:KM, :], 1.0)
                last = nc.gpsimd.memset(qa[m][64:KM, :], 0.0)
            last.then_inc(s_fill, 1)
            pool.wait_ge(s_fill, 1)
            for m in range(3):
                nc.gpsimd.memset(v4[m][:], 0.0).then_inc(s_glink, 1)
            pool.wait_ge(s_glink, 3)
            for m in range(3):
                nc.gpsimd.memset(v4[m][:, :, :, DK:DK + 1], 1.0).then_inc(s_glink, 1)
            pool.wait_ge(s_glink, 6)

            def values(i, r):
                m = r % 3
                nc.gpsimd.tensor_copy(v4[m][:, :, :, 0:DK],
                                      v_all[:, bass.ds(quad(i, r), 1), :, :].rearrange("p n k (h d) -> p (n k) h d", h=HQ)
                                      ).then_inc(s_v4, 1)

            with pool.Fori(0, B) as b:
                for u in range(2):
                    for w in range(2):
                        pool.wait_ge(s_mid, (b * 2 + u) * 2 + w + 1)
                        pool.sem_inc(s_seen_pool, 1)
                        nc.gpsimd.tensor_tensor(qk_parts[:, u, w, 2, :], rot[:, u, w, 1, :], qk_parts[:, u, w, 1, :],
                                                ALU.subtract).then_inc(s_parts, 1)

            pool.wait_ge(s_v_free, 2 * B)
            values(0, 0)

            def body(i, r):
                n = quad(i, r)
                if not (isinstance(i, int) and n + 1 >= NQ):
                    if not (isinstance(i, int) and n == 0):
                        pool.wait_ge(s_pv, n * NS - (NS - 1))
                    values(i, r + 1)
                for s, (c, k, q0) in enumerate(STEPS):
                    if k < CG * c:
                        continue
                    pool.wait_ge(s_exp, n * (2 * NS) + 2 * (s + 1))
                    pool.sem_inc(s_seen_pool, 1)
                    p = probs[s % 4][:, :, 0:T]
                    nc.gpsimd.affine_select(out=p, in_=p, compare_op=ALU.is_ge, fill=0.0, base=0,
                                            pattern=[[0, HQ], [1, T]], channel_multiplier=-1).then_inc(s_mask, 1)
            quads(pool, body)

            for e in range(EX):
                pool.wait_ge(s_whi, e + 1)
                nc.gpsimd.tensor_tensor(w_lo[:, e, :, :], w_raw[:, e % 2, :, :], w_hi[:, e, :, :].bitcast(F32),
                                        ALU.subtract).then_inc(s_wlo, 1)

            pool.wait_ge(s_pad_out, 16)
            pool.wait_ge(s_slot, 1)
            for t in range(NT):
                for k in range(TOP):
                    nc.gpsimd.indirect_dma_start(slot_d, bass.IndirectOffsetOnAxis(ap=slot[:, k, t:t + 1], axis=0),
                                                 rows[:, t, :], None).then_inc(s_scatter, 16)

            def slot_step(i, r):
                at = tile(i, r, -2)
                if at:
                    t, j, times = at
                    t2 = j % 2
                    pool.wait_ge(s_srow[j], 16 * times + 16)
                    e = pool.value_load(expert[0:1, bass.ds(t, 1)], min_val=1, max_val=NE)
                    nc.gpsimd.tensor_copy(s_weight[:, bass.ds(t, 1)], srow[:, j, bass.ds(D - 1 + e, 1)])
                    nc.gpsimd.tensor_tensor(s_dest_f[:, bass.ds(t, 1)], srow[:, j, bass.ds(D + NE - 1 + e, 1)],
                                            cst[:, bass.ds(CST["spare"][0] + t, 1)], ALU.add).then_inc(s_meta, 1)
                at = tile(i, r, 3)
                if at:
                    t, j, times = at
                    t2 = j % 2
                    needs(pool, s_y_out[j], 16 * times)
                    pool.sem_inc(s_seen_pool, 1)
                    nc.gpsimd.tensor_copy(s_dest[:, j:j + 1], s_dest_f[:, bass.ds(t, 1)]).then_inc(s_dest_i, 1)
                    pool.wait_ge(s_dest_i, t + 1)
                    pool.wait_ge(s_y, t + 1)
                    pool.sem_inc(s_seen_pool, 1)
                    nc.gpsimd.indirect_dma_start(y_d, bass.IndirectOffsetOnAxis(ap=s_dest[:, j:j + 1], axis=0),
                                                 y_s[:, j, :], None).then_inc(s_y_out[j], 16)
            slot_steps(pool, -2, ST + 2, slot_step)

        @block.scalar
        def _(act):
            act.wait_ge(s_in0, 48)
            nc.scalar.activation(c_s[:], c_t[:], ACT.Silu).then_inc(s_csilu, 1)
            act.wait_ge(s_modps, 1)
            for bank, dst in ((1, gate_a[:]), (2, gate_b[:]), (3, mod2_rows[:, 0, :, :]), (4, mod2_rows[:, 1, :, :])):
                nc.scalar.activation(dst, ps[:, bank, :].rearrange("p (b d) -> p b d", b=B), ACT.Copy).then_inc(s_raw, 1)
            act.wait_ge(s_var, 1)
            nc.scalar.activation(rstd[:], rstd[:], ACT.Sqrt).then_inc(s_std, 1)
            act.wait_ge(s_mod, 1)

            with act.Fori(0, B) as b:
                for u in range(2):
                    n = b * 2 + u
                    act.wait_ge(s_tp, n + 1)
                    act.sem_inc(s_seen_act, 1)
                    nc.scalar.activation(hT[:, u, :], ps[:, u, :], ACT.Identity, scale=mod1[:, 0, bass.ds(b, 1)],
                                         bias=mod1[:, 1, bass.ds(b, 1)]).then_inc(s_hT, 1)
                for u in range(2):
                    n = b * 2 + u
                    for w in range(2):
                        act.wait_ge(s_sum, n * 2 + w + 1)
                        nc.scalar.activation(qk_parts[:, u, w, 0, :], rot[:, u, w, 0, :], ACT.Copy).then_inc(s_hi, 1)
                    for w in range(2):
                        act.wait_ge(s_rest, n * 2 + w + 1)
                        nc.scalar.activation(qk_parts[:, u, w, 1, :], rot[:, u, w, 1, :], ACT.Copy).then_inc(s_mid, 1)
                    act.wait_ge(s_v, n + 1)
                    act.sem_inc(s_seen_act, 1)
                    nc.scalar.activation(
                        v_all[:, bass.ds(b * NG, NG), u * CG:(u + 1) * CG, :].rearrange("p g j e -> p j g e"),
                        ps[:, 6 + u, :].rearrange("p (j g e) -> p j g e", j=CG, g=NG), ACT.Copy).then_inc(s_v_free, 1)

            def copy_out(i, r, c, k):
                n = quad(i, r)
                act.wait_ge(s_pv, n * NS + CG + c * 2 * CG)
                if not (isinstance(i, int) and n == 0):
                    j, q = (i, r) if c else (i, r - 1)
                    if isinstance(i, int):
                        j, q = 0, quad(i, q)
                    at = [x[1:] for x in plan_of(j, q)].index(("norm", -1, 1) if c else ("norm", 0, 0))
                    act.wait_ge(s_ring, ring_base(j, q) + (at + 1))
                nc.scalar.activation(outT[:, c, :], ps[:, 4, :], ACT.Copy).then_inc(s_outT, 1)

            def body(i, r):
                n = quad(i, r)
                first = isinstance(i, int) and n == 0
                for s, (c, k, q0) in enumerate(STEPS):
                    if not (first and s < 4):
                        act.wait_ge(s_pv, n * NS + s - 3)
                    for h in range(2):
                        act.wait_ge(s_scores, n * (2 * NS) + 2 * s + h + 1)
                        nc.scalar.activation(probs[s % 4][:, 2 * h:2 * h + 2, 0:CH - q0], ps[:, 2 * h:2 * h + 2, q0:CH],
                                             ACT.Exp, scale=SCALE).then_inc(s_exp, 1)
                    if s == 1 and not first:
                        copy_out(i, r - 1, 1, None)
                    if s == 5:
                        copy_out(i, r, 0, None)
            quads(act, body)
            copy_out(5, 0, 1, None)

            with act.Fori(0, B) as b:
                for u in range(2):
                    n = b * 2 + u
                    act.wait_ge(s_ot, n + 1)
                    act.wait_ge(s_gated, n + 1)
                    nc.scalar.activation(oT[:, u, :], ps[:, u, :], ACT.Copy).then_inc(s_oT, 1)

            def first_part(e):
                act.wait_ge(s_wraw[e % 2], 32 * (e // 2 + 1))
                nc.scalar.activation(w_hi[:, e, :, :], w_raw[:, e % 2, :, :], ACT.Copy).then_inc(s_whi, 1)
            for e in range(EX // 2):
                first_part(e)
            act.wait_ge(s_var2, 1)
            nc.scalar.activation(rstd[:], rstd[:], ACT.Sqrt).then_inc(s_std2, 1)
            with act.Fori(0, B) as b:
                for u in range(2):
                    n = b * 2 + u
                    act.wait_ge(s_tp2, n + 1)
                    act.wait_ge(s_lg_free, n + 1)
                    act.sem_inc(s_seen_act, 1)
                    nc.scalar.activation(hT[:, u, :], ps[:, 4 + u, :], ACT.Identity, scale=mod2[:, 0, bass.ds(b, 1)],
                                         bias=mod2[:, 1, bass.ds(b, 1)]).then_inc(s_hT2, 1)
                    nc.scalar.activation(h2_hi[:, bass.ds(n * CH, CH)], ps[:, 4 + u, :], ACT.Identity,
                                         scale=mod2[:, 0, bass.ds(b, 1)], bias=mod2[:, 1, bass.ds(b, 1)]).then_inc(s_h2_hi, 1)
            for e in range(EX // 2, EX):
                first_part(e)
            act.wait_ge(s_max7, 1)
            nc.scalar.activation(prob[:], logit[:], ACT.Exp).then_inc(s_exp7, 1)

            with act.Fori(0, B) as b:
                for u in range(2):
                    for c, (i0, w) in enumerate(IC):
                        g = (b * 2 + u) * len(IC) + c
                        act.wait_ge(s_gu, g + 1)
                        act.wait_ge(s_hid, g + 1)
                        nc.scalar.activation(sgs[0:w, c, :], ps[0:w, 2 * c, :], ACT.Silu).then_inc(s_silu, 1)

            def slot_step(i, r):
                at = tile(i, r, -1)
                if at:
                    t, j, _ = at
                    t2 = j % 2
                    act.wait_ge(s_rowT, t + 1)
                    needs(act, s_sgu, t - 1)
                    nc.scalar.activation(h_hi[:, t2, :], ps[:, 0, 0:T], ACT.Copy).then_inc(s_h_hi, 1)
                at = tile(i, r, 0)
                if at:
                    t, j, _ = at
                    t2 = j % 2
                    act.wait_ge(s_sgu, t + 1)
                    needs(act, s_shid, t - 1)
                    nc.scalar.activation(sg[:, t2, :], ps[:, 1 + 2 * t2, 0:NI], ACT.Silu).then_inc(s_ssilu, 1)
                at = tile(i, r, 2)
                if at:
                    t, j, times = at
                    t2 = j % 2
                    act.wait_ge(s_sdn, t + 1)
                    act.wait_ge(s_meta, t + 1)
                    needs(act, s_y_out[j], 16 * times)
                    act.sem_inc(s_seen_act, 1)
                    nc.scalar.activation(y_s[:, j, :], ps[:, 6, 0:D], ACT.Copy, scale=s_weight[:, bass.ds(t, 1)]).then_inc(s_y, 1)
                at = tile(i, r, 1)
                if at:
                    t, j, _ = at
                    t2 = j % 2
                    act.wait_ge(s_shidT, t + 1)
                    needs(act, s_sdn, t - 1)
                    nc.scalar.activation(hidT[:, t2, 0:2, :], ps[:, 5, 0:2 * T].rearrange("p (c t) -> p c t", c=2), ACT.Copy)
                    w = IC[2][1]
                    nc.scalar.activation(hidT[0:w, t2, 2, :], ps[0:w, 5, 2 * T:3 * T], ACT.Copy).then_inc(s_hidT, 1)
            slot_steps(act, -1, ST + 1, slot_step)

        @block.vector
        def _(dve):
            chain = [0]

            def link(ins):
                chain[0] += 1
                ins.then_inc(s_link, 1)
                dve.wait_ge(s_link, chain[0])

            V = nc.vector
            dve.sem_inc(s_prod, 2)
            dve.sem_inc(s_hT, 2)
            dve.sem_inc(s_oT, 2)
            dve.sem_inc(s_gated, 2)
            dve.sem_inc(s_lg_free, 2)
            dve.sem_inc(s_hid, len(IC))
            dve.sem_inc(s_dn_free, 1)
            for u in range(2):
                dve.sem_inc(s_spill[u], 16)

            def tile_stats(t0, count):
                for j in range(count):
                    V.bn_stats(stats[:, bass.ds(t0 + j, 1), :].rearrange("p o s -> p (o s)"),
                               xs[:, bass.ds(t0 + j, 1), :].rearrange("p o s -> p (o s)"))

            def layernorm_scale(done, std):
                m0, q0, m1, q1 = stats[:, :, 1], stats[:, :, 2], stats[:, :, 4], stats[:, :, 5]
                link(V.drain())
                link(V.tensor_tensor(mean[:], m0, m1, ALU.add))
                link(V.tensor_tensor(part_a[:], m0, m1, ALU.subtract))
                link(V.tensor_tensor(part_b[:], q0, q1, ALU.add))
                link(V.tensor_scalar(mean[:], mean[:], 0.5, None, ALU.mult))
                link(V.tensor_tensor(part_a[:], part_a[:], part_a[:], ALU.mult))
                link(V.tensor_scalar(part_b[:], part_b[:], 1.0 / D, EPS, ALU.mult, ALU.add))
                V.scalar_tensor_tensor(rstd[:], part_a[:], 0.25, part_b[:], ALU.mult, ALU.add).then_inc(done, 1)
                dve.wait_ge(std, 1)
                link(V.reciprocal(rstd[:], rstd[:]))

            dve.wait_ge(s_csilu, 1)
            V.tensor_copy(c_b[:], c_s[:].unsqueeze(2).to_broadcast((D, B, 128))).then_inc(s_cb, 1)
            for b in range(B):
                dve.wait_ge(s_x[b], 16)
                tile_stats(b * TB, TB)
            layernorm_scale(s_var, s_std)
            dve.wait_ge(s_modps, 1)
            mps = ps[:, 0, 0:4 * B].rearrange("p (j b) -> p j b", b=B)
            for m, j in ((mod1, 0), (mod2, 2)):
                link(V.tensor_scalar(m[:, 0, :], mps[:, j + 1, :], 1.0, None, ALU.add))
                link(V.tensor_copy(m[:, 1, :], mps[:, j, :]))
            dve.sem_inc(s_mod, 1)

            def normalise(done):
                with dve.Fori(0, B) as b:
                    for j in range(TB):
                        t = b * TB + j
                        last = V.tensor_scalar(xn[:, bass.ds(t, 1), :].rearrange("p o d -> p (o d)"),
                                               xs[:, bass.ds(t, 1), :].rearrange("p o d -> p (o d)"),
                                               mean[:, bass.ds(t, 1)], rstd[:, bass.ds(t, 1)],
                                               ALU.subtract, ALU.mult)
                        if j % CG == CG - 1:
                            last.then_inc(done, 1)
            normalise(s_xn)
            dve.wait_ge(s_in, 16 * 10)

            with dve.Fori(0, B) as b:
                for u in range(2):
                    n = b * 2 + u
                    dve.wait_ge(s_spill[u], b * (16 * (NP + len(KPART))) + 16)
                    part = [[qk_parts[:, u, w, p, :] for p in range(NP)] for w in range(2)]
                    ra = [rot[:, u, w, 0, :] for w in range(2)]
                    rb_ = [rot[:, u, w, 1, :] for w in range(2)]

                    def products(w):
                        dve.wait_ge(s_qk, n * 2 + w + 1)
                        V.tensor_tensor(ra[w], ps[:, 2 + 2 * w, :], cos[:, u * CH:(u + 1) * CH], ALU.mult)
                        V.tensor_tensor(rb_[w], ps[:, 3 + 2 * w, :], sin[:, u * CH:(u + 1) * CH],
                                        ALU.mult).then_inc(s_prod, 1)

                    def rotated(w):
                        dve.wait_ge(s_prod, n * 2 + w + 3)
                        V.tensor_tensor(ra[w], ra[w], rb_[w], ALU.add).then_inc(s_sum, 1)

                    def rest(w):
                        dve.wait_ge(s_hi, n * 2 + w + 1)
                        V.tensor_tensor(rb_[w], ra[w], part[w][0], ALU.subtract).then_inc(s_rest, 1)

                    products(0)
                    products(1)
                    rotated(0)
                    rotated(1)
                    rest(0)
                    rest(1)

            dve.wait_ge(s_raw, 4)
            for g in (gate_a, gate_b):
                row = g[:].rearrange("p b d -> p (b d)")
                link(V.tensor_scalar(junk[:, 0, :], row, 0.0, 2.0, ALU.is_ge, ALU.mult))
                link(V.tensor_scalar(junk[:, 1, :], row, -1.0, 0.25, ALU.mult, ALU.max))
                link(V.tensor_tensor(junk[:, 1, :], row, junk[:, 1, :], ALU.max))
                link(V.scalar_tensor_tensor(row, junk[:, 0, :], -1.0, junk[:, 1, :], ALU.add, ALU.mult))
            link(V.tensor_scalar(mod2_rows[:, 1, :, :], mod2_rows[:, 1, :, :], 1.0, None, ALU.add))

            def shift_parts(m, bank):
                part = [mparts[m][:, p, :] for p in range(NP)]
                neg = ps[0:HQ * TB, bank, 0:T]
                return [lambda: V.tensor_scalar(part[0], neg, -1.0, None, ALU.mult),
                        lambda: V.scalar_tensor_tensor(mrest[:], neg, -1.0, part[0], ALU.mult, ALU.subtract),
                        lambda: V.tensor_copy(part[1], mrest[:]),
                        lambda: V.tensor_tensor(part[2], mrest[:], part[1], ALU.subtract)]

            def bank_maxima(m, bank, what):
                h, parts = PIECES[what]
                at = 0
                for q, k0, w, diag in parts:
                    src = ps[:, bank, at:at + w]
                    if diag:
                        last = V.tensor_tensor_reduce(out=junk[:, bank - 5, at:at + w], in0=src, in1=tri[:, CH - w:CH],
                                                      scale=1.0, scalar=LOW, op0=ALU.add, op1=ALU.max,
                                                      accum_out=rowmax[m][:, h, q:q + 1])
                    else:
                        last = V.reduce_max(leftmax[m][:, h, q - CG:q - CG + 1], src, AX.X)
                    at += w
                return last

            aux = chain[0]
            AUX = 7

            def ring_item(i, r, k, kind, off, what, links):
                lbase, lk = links
                bank = 5 + ring_bank(i, r, k) if k is not None else None
                m = (r + off) % 3
                if kind == "max":
                    dve.sem_inc(s_seen_dve, 1)
                    bank_maxima(m, bank, what).then_inc(s_ring_free, 1)
                elif kind == "shift":
                    ops = shift_parts(m, bank)
                    for j, op in enumerate(ops):
                        ins = op()
                        if j < 3:
                            ins.then_inc(s_link, 1)
                            lk[0] += 1
                            dve.wait_ge(s_link, lbase + lk[0])
                            if j == 1:
                                dve.sem_inc(s_ring_free, 1)
                        else:
                            ins.then_inc(s_mparts, 1)
                else:
                    c = what
                    src = ps[:, bank, :].rearrange("p (j h w) -> p j h w", j=CG, h=HQ)
                    V.reciprocal(recip[:], src[:, :, :, DK]).then_inc(s_link, 1)
                    lk[0] += 1
                    dve.wait_ge(s_link, lbase + lk[0])
                    dst = o_quads[:, c * CG:(c + 1) * CG, bass.ds(quad(i, r + off), 1), :]
                    V.tensor_tensor(dst.rearrange("p j n (h d) -> p (j n) h d", h=HQ), src[:, :, :, 0:DK],
                                    recip[:].unsqueeze(3).to_broadcast((T, CG, HQ, DK)), ALU.mult).then_inc(s_ring_free, 1)
                    lk[0] += 1
                    dve.sem_inc(s_link, 1)

            def full_max(m):
                V.tensor_tensor(rowmax[m][:, :, CG:TB], rowmax[m][:, :, CG:TB], leftmax[m][:], ALU.max).then_inc(s_rowmax, 1)

            lk = [0]
            for k, (kind, off, what) in enumerate(PRE):
                dve.wait_ge(s_ring, k + 1)
                if kind == "shift":
                    pass
                bank_k = k % RING
                ring_pre = (5 + bank_k)
                m = off % 3
                if kind == "max":
                    bank_maxima(m, ring_pre, what).then_inc(s_ring_free, 1)
                    if what == NM - 1:
                        dve.wait_ge(s_ring_free, k + 1)
                        full_max(m)
                else:
                    for j, op in enumerate(shift_parts(m, ring_pre)):
                        ins = op()
                        if j < 3:
                            ins.then_inc(s_link, 1)
                            lk[0] += 1
                            dve.wait_ge(s_link, aux + lk[0])
                            if j == 1:
                                dve.sem_inc(s_ring_free, 1)
                        else:
                            ins.then_inc(s_mparts, 1)
            l0 = aux + lk[0]

            def body(i, r):
                n = quad(i, r)
                plan = plan_of(i, r)
                lk = [0]
                first = isinstance(i, int) and n == 0
                lbase = l0 if first else n * AUX + (l0 - 2)
                rbase = ring_base(i, r)
                for k, (s, kind, off, what) in enumerate(plan):
                    if k and kind == "norm" and plan[k - 1][1] == "norm":
                        dve.wait_ge(s_ring_free, rbase + k)
                    dve.wait_ge(s_ring, rbase + (k + 1))
                    ring_item(i, r, k, kind, off, what, (lbase, lk))
                    if kind == "max" and what == NM - 1:
                        dve.wait_ge(s_ring_free, rbase + (k + 1))
                        full_max((r + off) % 3)
            quads(dve, body)
            endbase = ring_base(5, 1)
            dve.wait_ge(s_ring_free, endbase)
            dve.wait_ge(s_ring, endbase + 1)
            lend = l0 - 2 + NQ * AUX - 3
            lk = [0]
            ring_item(5, 1, 0, "norm", -1, 1, (lend, lk))
            chain[0] = lend + 2

            def tile_pair(b, u):
                return b * TB + u * CG

            dve.wait_ge(s_ring_free, ring_base(0, NQ) + 1)
            with dve.Fori(0, B) as b:
                for u in range(2):
                    n = b * 2 + u
                    dve.wait_ge(s_proj, n + 1)
                    V.tensor_tensor(att_o[:, u, :].rearrange("p (j d) -> p j d", j=CG),
                                    ps[:, 2 + u, :].rearrange("p (j d) -> p j d", j=CG),
                                    gate_a[:, bass.ds(b, 1), :].to_broadcast((T, CG, D)), ALU.mult).then_inc(s_gated, 1)
                    dve.wait_ge(s_gated, n + 3)
                    xt = xs[:, bass.ds(tile_pair(b, u), CG), :]
                    V.tensor_tensor(xt, xt, att_o[:, u, :].rearrange("p (j d) -> p j d", j=CG),
                                    ALU.add).then_inc(s_x2, 1)
                    dve.wait_ge(s_x2, n + 1)
                    tile_stats(tile_pair(b, u), CG)
            layernorm_scale(s_var2, s_std2)
            normalise(s_xn2)

            base3 = chain[0]
            with dve.Fori(0, B) as b:
                for u in range(2):
                    n = b * 2 + u
                    row = rows[:, bass.ds(tile_pair(b, u), CG), 0:D]
                    dve.wait_ge(s_xn2, n + 1)
                    V.tensor_tensor(row, xn[:, bass.ds(tile_pair(b, u), CG), :],
                                    mod2_rows[:, 1, bass.ds(b, 1), :].to_broadcast((T, CG, D)), ALU.mult).then_inc(s_link, 1)
                    dve.wait_ge(s_h2_hi, n + 1)
                    cols = bass.ds(n * CH, CH)
                    V.tensor_tensor(h2_lo[:, cols], hT[:, u, :], h2_hi[:, cols].bitcast(F32), ALU.subtract).then_inc(s_split2, 1)
                    dve.wait_ge(s_link, n + (base3 + 1))
                    V.tensor_tensor(row, row, mod2_rows[:, 0, bass.ds(b, 1), :].to_broadcast((T, CG, D)),
                                    ALU.add).then_inc(s_rows, 1)
                    dve.wait_ge(s_lg, n + 1)
                    V.tensor_tensor(logit[:, bass.ds(tile_pair(b, u), CG), :],
                                    ps[:, 6 + u, 0:CG * NE].rearrange("p (j e) -> p j e", j=CG),
                                    rb[:].unsqueeze(1).to_broadcast((T, CG, NE)), ALU.add).then_inc(s_lg_free, 1)
            chain[0] = base3 + 2 * B

            dve.wait_ge(s_lg_free, 2 + 2 * B)
            link(V.tensor_reduce(rsum[:], logit[:], AX.X, ALU.max))
            V.tensor_tensor(logit[:], logit[:], rsum[:].unsqueeze(2).to_broadcast((T, NT, NE)), ALU.subtract).then_inc(s_max7, 1)
            dve.wait_ge(s_exp7, 1)
            link(V.reduce_sum(rsum[:], prob[:], AX.X))
            link(V.reciprocal(rsum[:], rsum[:]))
            link(V.tensor_tensor(prob[:], prob[:], rsum[:].unsqueeze(2).to_broadcast((T, NT, NE)), ALU.mult))
            link(V.memset(rank[:], 0.0))
            for j in range(NE):
                pj = prob[:, :, j:j + 1]
                if j:
                    V.tensor_tensor(beats[:, :, 0:j], pj.to_broadcast((T, NT, j)), prob[:, :, 0:j], ALU.is_gt)
                if j < NE - 1:
                    V.tensor_tensor(beats[:, :, j + 1:NE], pj.to_broadcast((T, NT, NE - 1 - j)), prob[:, :, j + 1:NE], ALU.is_ge)
                link(V.memset(beats[:, :, j:j + 1], 0.0))
                link(V.tensor_tensor(rank[:], rank[:], beats[:], ALU.add))
            V.tensor_scalar(sel[:], rank[:], TOP - 0.5, None, ALU.is_lt).then_inc(s_sel, 1)

            dve.wait_ge(s_sel, 1)
            link(V.tensor_tensor(prob[:], prob[:], sel[:], ALU.mult))
            link(V.reduce_sum(rsum[:], prob[:], AX.X))
            link(V.reciprocal(rsum[:], rsum[:]))
            V.tensor_tensor(rows[:, :, D:D + NE], prob[:], rsum[:].unsqueeze(2).to_broadcast((T, NT, NE)), ALU.mult)

            def table(name, p=128):
                at, w = CST[name]
                return cst[0:p, at:at + w]
            V.scalar_tensor_tensor(rows[:, :, D + NE:RW], rank[:], float(B * S),
                                   table("token").unsqueeze(2).to_broadcast((T, NT, NE)), ALU.mult, ALU.add)

            dve.wait_ge(s_prefix, 1)
            before = ps[:, 2, 0:NT * NE].rearrange("p (t e) -> p t e", t=NT)
            total = ps[:, 2, NT * NE:2 * NT * NE].rearrange("p (t e) -> p t e", t=NT)
            V.tensor_copy(tot[:], total)
            link(V.tensor_copy(scan[:, 0, :, :], total))
            cur, step = 0, 1
            while step < NT:
                V.tensor_copy(scan[:, 1 - cur, 0:step, :], scan[:, cur, 0:step, :])
                link(V.tensor_tensor(scan[:, 1 - cur, step:NT, :], scan[:, cur, step:NT, :],
                                     scan[:, cur, 0:NT - step, :], ALU.add))
                cur, step = 1 - cur, 2 * step
            incl = scan[:, cur, :, :]
            link(V.tensor_tensor(reached[:], incl[:, NT - 1, :].unsqueeze(2).to_broadcast((T, NE, NT)),
                                 table("steps").unsqueeze(1).to_broadcast((T, NE, NT)), ALU.is_gt))
            link(V.reduce_sum(tcount[:], reached[:], AX.X))
            link(V.tensor_copy(tend[:, 0, :], tcount[:]))
            cur_e, step = 0, 1
            while step < NE:
                V.tensor_copy(tend[:, 1 - cur_e, 0:step], tend[:, cur_e, 0:step])
                link(V.tensor_tensor(tend[:, 1 - cur_e, step:NE], tend[:, cur_e, step:NE],
                                     tend[:, cur_e, 0:NE - step], ALU.add))
                cur_e, step = 1 - cur_e, 2 * step
            end = tend[:, cur_e, :]
            link(V.tensor_tensor(tbase[:], end, tcount[:], ALU.subtract))
            link(V.tensor_scalar(tbase[:], tbase[:], float(T), None, ALU.mult))
            link(V.tensor_tensor(tot[:], incl, tot[:], ALU.subtract))
            link(V.tensor_tensor(tot[:], tot[:], before, ALU.add))
            link(V.tensor_tensor(tot[:], tot[:], tbase[:].unsqueeze(1).to_broadcast((T, NT, NE)), ALU.add))
            link(V.tensor_tensor(rows[:, :, D + NE:RW], rows[:, :, D + NE:RW], tot[:], ALU.subtract))
            for k in range(TOP):
                link(V.tensor_scalar(sel[:], rank[:], float(k), None, ALU.is_equal))
                link(V.tensor_tensor(beats[:], sel[:], tot[:], ALU.mult))
                link(V.reduce_sum(slot_f[:, k, :], beats[:], AX.X))
            V.tensor_copy(slot[:], slot_f[:])
            link(V.tensor_tensor(passed[:], table("tiles", 1).unsqueeze(2).to_broadcast((1, ST, NE)),
                                 end[0:1, :].unsqueeze(1).to_broadcast((1, ST, NE)), ALU.is_ge))
            link(V.reduce_sum(expert_f[:], passed[:], AX.X))
            V.tensor_scalar(expert[:], expert_f[:], float(NE - 1), 1.0, ALU.min, ALU.add).then_inc(s_slot, 1)

            base4 = chain[0]
            with dve.Fori(0, B) as b:
                for u in range(2):
                    n = b * 2 + u
                    for c, (i0, w) in enumerate(IC):
                        dve.wait_ge(s_silu, n * len(IC) + c + 1)
                        V.tensor_tensor(hid[0:w, u, c, :], sgs[0:w, c, :], ps[0:w, 2 * c + 1, :], ALU.mult).then_inc(s_hid, 1)
                    dve.wait_ge(s_dn, n + 1)
                    V.tensor_tensor(acc[:, u, :, :], ps[:, 6, :].rearrange("p (j d) -> p j d", j=CG),
                                    gate_b[:, bass.ds(b, 1), :].to_broadcast((T, CG, D)), ALU.mult).then_inc(s_dn_free, 1)
                    dve.wait_ge(s_dn_free, n + 2)
                    xt = xs[:, bass.ds(tile_pair(b, u), CG), :]
                    V.tensor_tensor(xt, xt, acc[:, u, :, :], ALU.add).then_inc(s_shared, 1)

            def slot_step(i, r):
                at = tile(i, r, -1)
                if at:
                    t, j, _ = at
                    t2 = j % 2
                    dve.wait_ge(s_h_hi, t + 1)
                    V.tensor_tensor(h_lo[:, t2, :], ps[:, 0, 0:T], h_hi[:, t2, :].bitcast(F32), ALU.subtract).then_inc(s_h_lo, 1)
                at = tile(i, r, 0)
                if at:
                    t, j, _ = at
                    t2 = j % 2
                    dve.wait_ge(s_ssilu, t + 1)
                    needs(dve, s_shidT, t - 1)
                    V.tensor_tensor(hid_s[:, t2, :], sg[:, t2, :], ps[:, 2 + 2 * t2, 0:NI], ALU.mult).then_inc(s_shid, 1)
            slot_steps(dve, -1, ST + 1, slot_step)

            dve.wait_ge(s_shared, 2 * B)
            for n in range(2 * B):
                b, ts = n // 2, slice(n * CG, (n + 1) * CG)
                if n % 2 == 0:
                    dve.wait_ge(s_y_in[b], 16 * TOP)
                link(V.tensor_tensor(acc[:, n % 2, :, :], y_in[0][:, ts, :], y_in[1][:, ts, :], ALU.add))
                link(V.tensor_tensor(acc[:, n % 2, :, :], acc[:, n % 2, :, :], gate_b[:, b:b + 1, :].to_broadcast((T, CG, D)),
                                     ALU.mult))
                V.tensor_tensor(xs[:, ts, :], xs[:, ts, :], acc[:, n % 2, :, :], ALU.add).then_inc(s_res, 1)

        @block.tensor
        def _(pe):
            MM = nc.tensor.matmul
            pe.wait_ge(s_in0, 48)
            pe.wait_ge(s_csilu, 1)
            for k, j in enumerate((0, 1, 3, 4)):
                MM(ps[:, 0, k * B:(k + 1) * B], wmod[:, j, :], c_s[:], start=True, stop=True)
            pe.wait_ge(s_cb, 1)
            for bank, j in ((1, 2), (2, 5), (3, 3), (4, 4)):
                for b in range(B):
                    last = MM(ps[:, bank, b * D:(b + 1) * D], c_b[:, b, :], wmod[:, j, :], start=True, stop=True)
            last.then_inc(s_modps, 1)
            pe.wait_ge(s_mod, 1)
            pe.wait_ge(s_raw, 4)
            pe.wait_ge(s_in, 16 * 10)

            for b in range(B):
                for u in range(2):
                    n = b * 2 + u
                    pe.wait_ge(s_xn, n + 1)
                    pe.wait_ge(s_hT, n + 1)
                    for j in range(CG):
                        last = nc.tensor.transpose(ps[:, u, j * T:(j + 1) * T],
                                                   xn[:, b * TB + u * CG + j, :], eye[:])
                    last.then_inc(s_tp, 1)
                for u in range(2):
                    n = b * 2 + u
                    pe.wait_ge(s_hT, n + 3)
                    for w, mat in enumerate((wq, wk)):
                        pe.wait_ge(s_prod, n * 2 + w + 1)
                        for j in range(2):
                            last = MM(ps[:, 2 + 2 * w + j, :], mat[:, j, :], hT[:, u, :], start=True, stop=True)
                        last.then_inc(s_qk, 1)
                    for j in range(CG):
                        last = MM(ps[:, 6 + u, j * D:(j + 1) * D], hT[:, u, j * T:(j + 1) * T], wv[:], start=True, stop=True)
                    last.then_inc(s_v, 1)

            def row_scores(m, bank, what):
                h, parts = PIECES[what]
                at = 0
                for q, k0, w, diag in parts:
                    last = MM(ps[:, bank, at:at + w], qa[m][0:KR, h * S + q * T:h * S + (q + 1) * T],
                              ka[m][0:KR, h * S + k0:h * S + k0 + w], start=True, stop=True)
                    at += w
                return last

            def ring_write(i, r, bank, kind, off, what):
                m = (r + off) % 3
                if kind == "max":
                    if what == 0:
                        pe.wait_ge(s_qk_in[m], (third(i, r + off) + 1) * (2 * NP * 16))
                    last = row_scores(m, bank, what)
                elif kind == "shift":
                    pe.wait_ge(s_rowmax, quad(i, r + off) + 1)
                    last = nc.tensor.transpose(ps[0:HQ * TB, bank, 0:T],
                                               rowmax[m][:].rearrange("p h q -> p (h q)"), eye[:])
                else:
                    pe.wait_ge(s_outT, 2 * quad(i, r + off) + what + 1)
                    for j in range(CG):
                        last = nc.tensor.transpose(ps[:, bank, j * T:(j + 1) * T], outT[:, what, j * T:(j + 1) * T], eye[:])
                last.then_inc(s_ring, 1)

            pe.wait_ge(s_v_free, 2 * B)
            for k, (kind, off, what) in enumerate(PRE):
                if k >= RING:
                    pe.wait_ge(s_ring_free, k - RING + 1)
                ring_write(0, 0, 5 + k % RING, kind, off, what)

            def values_product(i, r, s):
                c, k, q0 = STEPS[s]
                n, m = quad(i, r), r % 3
                pe.wait_ge(s_exp, n * (2 * NS) + 2 * s + 2)
                if k >= CG * c:
                    diag = s if c == 0 else s - NS + 2 * CG
                    pe.wait_ge(s_mask, n * (2 * CG) + diag + 1)
                if s == 0:
                    pe.wait_ge(s_v4, n + 1)
                if k == 0 and not (isinstance(i, int) and n == 0 and c == 0):
                    pe.wait_ge(s_outT, 2 * n + c)
                for h in range(HQ):
                    last = MM(ps[VW * h:VW * (h + 1), 4, q0:CH], v4[m][:, k, h, :], probs[s % 4][:, h, 0:CH - q0],
                              start=(k == 0), stop=(k == CG * (c + 1) - 1))
                last.then_inc(s_pv, 1)

            def body(i, r):
                n, m = quad(i, r), r % 3
                first = isinstance(i, int) and n == 0
                plan = plan_of(i, r)
                rbase = ring_base(i, r)
                pe.wait_ge(s_m_in[m], (third(i, r) + 1) * (16 * NP))
                ks = [0]

                def ring_entries(slot):
                    while ks[0] < len(plan) and plan[ks[0]][0] <= slot:
                        k = ks[0]
                        _, kind, off, what = plan[k]
                        pe.wait_ge(s_ring_free, rbase + (k + 1 - RING))
                        ring_write(i, r, 5 + ring_bank(i, r, k), kind, off, what)
                        ks[0] += 1

                for s, (c, kb, q0) in enumerate(STEPS):
                    for h in range(HQ):
                        if h % 2 == 0 and not (first and s == 0):
                            pe.wait_ge(s_exp, n * (2 * NS) + 2 * s + h // 2 - 1)
                        last = MM(ps[:, h, q0:CH], ka[m][0:KM, h * S + kb * T:h * S + (kb + 1) * T],
                                  qa[m][0:KM, h * S + c * CH + q0:h * S + (c + 1) * CH], start=True, stop=True)
                        if h % 2:
                            last.then_inc(s_scores, 1)
                            ring_entries(s * SLOTS + h // 2)
                    if s >= 2:
                        values_product(i, r, s - 2)
                    elif not first:
                        values_product(i, r - 1, NS - 2 + s)
                    ring_entries(s * SLOTS + 2)
            quads(pe, body)
            values_product(5, 0, NS - 2)
            values_product(5, 0, NS - 1)
            endbase = ring_base(5, 1)
            pe.wait_ge(s_ring_free, endbase + 1 - RING)
            ring_write(5, 1, 5 + endbase % RING, "norm", -1, 1)
            pe.wait_ge(s_ring_free, ring_base(0, NQ) + 1)

            for b in range(B):
                for u in range(2):
                    n = b * 2 + u
                    pe.wait_ge(s_oT, n + 1)
                    for j in range(CG):
                        last = nc.tensor.transpose(ps[:, u, j * T:(j + 1) * T],
                                                   o_rows[:, u * CG + j, b, :], eye[:])
                    last.then_inc(s_ot, 1)
                for u in range(2):
                    n = b * 2 + u
                    pe.wait_ge(s_oT, n + 3)
                    pe.wait_ge(s_gated, n + 1)
                    for j in range(CG):
                        last = MM(ps[:, 2 + u, j * D:(j + 1) * D], oT[:, u, j * T:(j + 1) * T], wo[:], start=True, stop=True)
                    last.then_inc(s_proj, 1)

            for b in range(B):
                for u in range(2):
                    n = b * 2 + u
                    pe.wait_ge(s_xn2, n + 1)
                    pe.wait_ge(s_lg_free, n + 1)
                    for j in range(CG):
                        last = nc.tensor.transpose(ps[:, 4 + u, j * T:(j + 1) * T],
                                                   xn[:, b * TB + u * CG + j, :], eye[:])
                    last.then_inc(s_tp2, 1)
                for u in range(2):
                    n = b * 2 + u
                    pe.wait_ge(s_hT2, n + 1)
                    for j in range(CG):
                        last = MM(ps[:, 6 + u, j * NE:(j + 1) * NE], hT[:, u, j * T:(j + 1) * T], wr[:], start=True, stop=True)
                    last.then_inc(s_lg, 1)

            pe.wait_ge(s_sel, 1)
            for name, at in (("before", 0), ("ones", 1)):
                c0, w = CST[name]
                last = MM(ps[:, 2, at * NT * NE:(at + 1) * NT * NE], cst[:, c0:c0 + w],
                          sel[:].rearrange("p t e -> p (t e)"), start=True, stop=True)
            last.then_inc(s_prefix, 1)

            pe.wait_ge(s_slot, 1)
            pe.wait_ge(s_split2, 2 * B)
            pe.wait_ge(s_wlo, 1)
            pe.wait_ge(s_wd, 16 * len(IC))

            def gate_up(b, u):
                n = b * 2 + u
                cols = bass.ds(n * CH, CH)
                for c, (i0, w) in enumerate(IC):
                    pe.wait_ge(s_hid, n * len(IC) + c + 1)
                    for g in range(2):
                        trio = ((w_hi, h2_hi), (w_lo, h2_hi), (w_hi, h2_lo))
                        for k, (wt, ht) in enumerate(trio):
                            last = MM(ps[0:w, 2 * c + g, :], wt[:, 0, g, i0:i0 + w], ht[:, cols],
                                      start=(k == 0), stop=(k == 2))
                    last.then_inc(s_gu, 1)

            def down(n, u):
                pe.wait_ge(s_hid, (n + 2) * len(IC))
                pe.wait_ge(s_dn_free, n + 1)
                for j in range(CG):
                    for c, (i0, w) in enumerate(IC):
                        last = MM(ps[:, 6, j * D:(j + 1) * D], hid[0:w, u, c, j * T:(j + 1) * T],
                                  wd[0:w, 0, c, :], start=(c == 0), stop=(c == len(IC) - 1))
                last.then_inc(s_dn, 1)

            with pe.Fori(0, B) as b:
                for u in range(2):
                    gate_up(b, u)
                    down(b * 2 + u, u)

            pe.wait_ge(s_shared, 2 * B)
            pe.wait_ge(s_wlo, EX)

            known = {}

            def expert_of(i, t, r):
                if r in known and r >= 0 and known[r][0] is i:
                    return known[r][1]
                known[r] = i, load_expert(t)
                return known[r][1]

            def load_expert(t):
                return pe.value_load(expert[0:1, bass.ds(t, 1)], min_val=1, max_val=NE)

            def slot_step(i, r):
                at = tile(i, r, -1)
                if at:
                    t, j, times = at
                    t2 = j % 2
                    pe.wait_ge(s_srow[j], 16 * times + 16)
                    needs(pe, s_h_lo, t)
                    nc.tensor.transpose(ps[:, 0, 0:T], srow[:, j, 0:D], eye[:]).then_inc(s_rowT, 1)
                at = tile(i, r, 0)
                if at:
                    t, j, _ = at
                    t2 = j % 2
                    e = expert_of(i, t, r)
                    if isinstance(t, int) and t == ST - 1:
                        pe.wait_ge(s_h_lo, t + 1)
                    for k, (ht, wt) in enumerate(((h_hi, w_hi), (h_hi, w_lo), (h_lo, w_hi))):
                        for g in range(2):
                            last = MM(ps[:, 1 + 2 * t2 + g, 0:NI], ht[:, t2, :], wt[:, bass.ds(e, 1), g, :],
                                      start=(k == 0), stop=(k == 2))
                    last.then_inc(s_sgu, 1)
                at = tile(i, r, 2)
                if at:
                    t, j, _ = at
                    t2 = j % 2
                    e = expert_of(i, t, r - 2)
                    pe.wait_ge(s_hidT, t + 1)
                    needs(pe, s_y, t)
                    for c, (i0, w) in enumerate(IC):
                        last = MM(ps[:, 6, 0:D], hidT[0:w, t2, c, :], wd[0:w, bass.ds(e, 1), c, :],
                                  start=(c == 0), stop=(c == len(IC) - 1))
                    last.then_inc(s_sdn, 1)
                at = tile(i, r, 1)
                if at:
                    t, j, _ = at
                    t2 = j % 2
                    pe.wait_ge(s_shid, t + 1)
                    for c, (i0, w) in enumerate(IC):
                        last = nc.tensor.transpose(ps[0:w, 5, c * T:(c + 1) * T], hid_s[:, t2, i0:i0 + w], eye[:])
                    last.then_inc(s_shidT, 1)
            slot_steps(pe, -1, ST + 1, slot_step)


_INS = ["x", "wq", "wk", "wv", "wo", "gate", "up", "down", "wr", "rb", "c", "wmod", "cos", "sin", "eye", "tri", "cst"]


def kernel(L0_attn_x, L0_attn_W_q, L0_attn_W_k, L0_attn_W_v, L0_attn_W_o, L0_ffn_sg, L0_ffn_su, L0_ffn_sd,
           L0_ffn_rg, L0_ffn_ru, L0_ffn_rd, L0_ffn_wr, L0_ffn_rb, L0_c, L0_wmod):
    import concourse.bacc as bacc
    from concourse.bass_utils import run_bass_kernel_spmd

    def rows(w, swap):
        w = np.asarray(w).reshape(NG, HQ, DK, D)
        if swap:
            w = w[:, :, [d ^ 1 for d in range(DK)], :]
        return w.transpose(0, 2, 1, 3).reshape(D, D).T

    def both(w):
        return np.stack([rows(w, False), rows(w, True)])

    freq = np.float32(10000.0) ** (np.float32(-2.0) * np.arange(DK // 2, dtype=np.float32) / np.float32(DK))
    ang = np.arange(S, dtype=np.float32)[:, None] * freq[None, :].astype(np.float32)
    dim = (np.arange(D) // HQ) % DK
    cos = np.cos(ang)[:, dim // 2].T
    sin = np.sin(ang)[:, dim // 2].T * np.where(dim % 2 == 0, -1.0, 1.0)[:, None]
    tri = np.zeros((T, CH), np.float32)
    tri[:, CH - T:] = np.where(np.arange(T)[None, :] > np.arange(T)[:, None], LOW, 0.0)

    cst = {"before": np.arange(T)[:, None] < np.arange(T)[None, :], "ones": np.ones((T, T)),
           "steps": np.tile(T * np.arange(NT), (T, 1)), "tiles": np.tile(np.arange(ST), (T, 1)),
           "token": np.arange(T)[:, None] + T * np.arange(NT)[None, :] - TOP * B * S,
           "pad": np.zeros((T, RW)),
           "spare": TOP * B * S + np.arange(T)[:, None] + T * np.arange(ST)[None, :]}
    cst = np.concatenate([cst[name] for name in CST], axis=1).astype(np.float32)

    def experts(shared, routed):
        return np.concatenate([np.asarray(shared)[None], np.asarray(routed)])

    vals = [
        np.asarray(L0_attn_x).reshape(B * S, D), both(L0_attn_W_q), both(L0_attn_W_k),
        np.asarray(L0_attn_W_v).T, np.asarray(L0_attn_W_o).T,
        experts(L0_ffn_sg, L0_ffn_rg).transpose(0, 2, 1), experts(L0_ffn_su, L0_ffn_ru).transpose(0, 2, 1),
        experts(L0_ffn_sd, L0_ffn_rd).transpose(0, 2, 1), np.asarray(L0_ffn_wr).T,
        np.asarray(L0_ffn_rb).reshape(1, NE), np.asarray(L0_c).T, np.asarray(L0_wmod),
        cos.astype(np.float32), sin.astype(np.float32), np.eye(128, dtype=np.float32), tri, cst,
    ]
    nc = bacc.Bacc("TRN2", target_bir_lowering=False, num_devices=1)
    arrays, args = {}, []
    for name, a in zip(_INS, vals):
        a = np.ascontiguousarray(a)
        arrays[f"in_{name}"] = a
        args.append(nc.dram_tensor(f"in_{name}", a.shape, mybir.dt.from_np(a.dtype), kind="ExternalInput").ap())
    out = nc.dram_tensor("out", (B * S, D), F32, kind="ExternalOutput").ap()
    adaln_block(nc, *args, out)
    r = run_bass_kernel_spmd(nc, [arrays], core_ids=[0])
    return r.results[0]["out"].reshape(B, S, D)
```

```python
from contextlib import ExitStack

import numpy as np

import concourse.bass as bass
from concourse import mybir

F32 = mybir.dt.float32
BF16 = mybir.dt.bfloat16
I32 = mybir.dt.int32
F32R = mybir.dt.float32r
ALU = mybir.AluOpType
ACT = mybir.ActivationFunctionType
AX = mybir.AxisListType

B, S, D = 4, 1024, 128
NH, DK = 16, 8
HQ = 4
NG = NH // HQ
NQ = B * NG
T = 128
TB = S // T
NT = B * TB
CH = 512
NP = 3
KR = NP * NP * DK
KM = KR + NP
VW = 32
NE, NI = 7, 352
EX = NE + 1
IC = [(0, 128), (128, 128), (256, 96)]
EPS = 1e-5
SCALE = float(DK) ** -0.5
LOW = -3.0e38
CG = CH // T
TOP = 2
ST = (TOP * B * S + NE * (T - 1)) // T
RW = D + 2 * NE
SB = 4
SU = 3 * SB
CST, _at = {}, 0
for _name, _w in (("before", T), ("ones", T), ("steps", NT), ("tiles", ST), ("token", NT), ("pad", RW), ("spare", ST)):
    CST[_name] = (_at, _w)
    _at += _w
CSTW = _at

STEPS = [(c, k, max(0, k - CG * c) * T) for c in range(S // CH) for k in range(CG * (c + 1))]
NS = len(STEPS)
HEAD_BANKS = [
    [(0, 0, T, True), (2, 0, 3 * T, True)],
    [(1, 0, 2 * T, True), (5, CH, 2 * T, True)],
    [(3, 0, CH, True)],
    [(4, CH, T, True), (6, CH, 3 * T, True)],
    [(7, CH, CH, True)],
] + [[(q, 0, CH, False)] for q in range(CG, TB)]
assert TB == 2 * CG == 8 and sum(w for bank in HEAD_BANKS for _, _, w, _ in bank) == T * TB * (TB + 1) // 2
PIECES = [(h, bank) for h in range(HQ) for bank in HEAD_BANKS]
NM = len(PIECES)
EARLY = NM // HQ
SLOTS = 3
STEP_COST = 60
SHIFT_SLOT = (NS - 3) * SLOTS
RING = 3


def ring_plan(back, ahead1, ahead2):
    pieces = [("max", 1, p) for p in range(EARLY, NM)] if ahead1 else []
    late = [("max", 2, p) for p in range(EARLY)] if ahead2 else []
    if ahead1:
        late.insert(min(3, len(late)), ("shift", 1, None))
    slots, total = [], 0
    for s, (_, _, q0) in enumerate(STEPS):
        for j in range(SLOTS):
            total += STEP_COST + CH - q0
            slots.append((total, s * SLOTS + j))
    scale = total / len(PIECES)
    plan, at = [], 0
    for kind, off, p in pieces + late:
        slot = next((s for end, s in slots if at < end), NS * SLOTS - 1)
        if not ahead2 and kind == "shift":
            slot = SHIFT_SLOT
        plan.append((slot, kind, off, p))
        at += scale if kind == "max" else 0
    if not ahead1:
        units = 2 * (B - 1)
        order = [("turn", 0)]
        for n in range(1, units):
            order += [("turn", n), ("project", n - 1)]
        order.append(("project", units - 1))
        plan += [(2 + k * (NS * SLOTS - 4) // len(order), kind, 0, n) for k, (kind, n) in enumerate(order)]
    out = []
    for s in range(NS * SLOTS):
        if s == 3 * SLOTS and back:
            out.append((s, "norm", -1, 1))
        if s == 7 * SLOTS:
            out.append((s, "norm", 0, 0))
        out += [x for x in plan if x[0] == s]
    return out


def adaln_block(nc, x_d, wq_d, wk_d, wv_d, wo_d, sw_g_d, sw_u_d, sw_d_d, wr_d, rb_d, c_d, wmod_d,
                cos_d, sin_d, eye_d, tri_d, cst_d, out_d):
    qs_d = nc.dram_tensor("q_parts_scratch", [NQ, NP, DK * HQ, S], BF16, kind="Internal").ap()
    ks_d = nc.dram_tensor("k_parts_scratch", [NQ, NP, DK * HQ, S], BF16, kind="Internal").ap()

    slot_d = nc.dram_tensor("slot_rows_scratch", [ST * T, RW], F32, kind="Internal").ap()
    y_d = nc.dram_tensor("routed_results_scratch", [TOP * B * S + ST * T, D], F32, kind="Internal").ap()

    ctx = ExitStack()
    with ctx:
        def sb(name, shape, dt=F32, at=None):
            return (at or ctx).enter_context(nc.sbuf_tensor(name, shape, dt))

        def sem(name):
            return ctx.enter_context(nc.semaphore(name))

        xs = sb("xs", [T, NT, D])
        eye = sb("eye", [128, 128])
        wo = sb("wo", [D, D])
        gate_a = sb("gate_a", [128, B, D])
        wo_gated = sb("wo_gated", [D, B, D])
        gate_b = sb("gate_b", [128, B, D])
        mod2_rows = sb("mod2_rows", [128, 2, B, D])
        cst = sb("cst", [128, CSTW])
        mod1 = sb("mod1", [D, 2, B])
        mod2 = sb("mod2", [D, 2, B])
        xn = sb("xn", [T, NT, D])
        o_quads = xn[:].rearrange("p t d -> p (t d)").rearrange("p (k n e) -> p k n e", k=TB, n=NQ)
        o_rows = xn[:].rearrange("p t d -> p (t d)").rearrange("p (k b d) -> p k b d", k=TB, b=B)
        stats = sb("stats", [T, NT, 6])
        mean = sb("mean", [T, NT])
        part_a = sb("part_a", [T, NT])
        part_b = sb("part_b", [T, NT])
        rstd = sb("rstd", [T, NT])
        rb = sb("rb", [128, NE])
        oT = sb("oT", [D, 2, CH])
        wr = sb("wr", [D, NE])
        hT = sb("hT", [D, 2, CH])

        att = ExitStack()
        v_all = sb("v_all", [T, NQ, TB, HQ * DK], at=att)
        qa = [sb(f"qa{m}", [KM, HQ * S], BF16, at=att) for m in range(3)]
        ka = [sb(f"ka{m}", [KM, HQ * S], BF16, at=att) for m in range(3)]
        v4 = [sb(f"v4_{m}", [T, TB, HQ, VW], at=att) for m in range(3)]
        tri = sb("tri", [T, CH], at=att)
        rowmax = [sb(f"rowmax{m}", [T, HQ, TB], at=att) for m in range(3)]
        leftmax = [sb(f"leftmax{m}", [T, HQ, TB - CG], at=att) for m in range(3)]
        mparts = [sb(f"mparts{m}", [HQ * TB, NP, T], BF16, at=att) for m in range(3)]
        mrest = sb("mrest", [HQ * TB, T], at=att)
        junk = sb("junk", [T, RING, CH], at=att)
        outT = sb("outT", [128, 2, CH], at=att)
        recip = sb("recip", [T, CG, HQ], at=att)
        pre = ExitStack()
        wq = sb("wq", [D, 2, D], at=pre)
        wk = sb("wk", [D, 2, D], at=pre)
        wv = sb("wv", [D, D], at=pre)
        c_t = sb("c_t", [D, B], at=pre)
        c_s = sb("c_s", [D, B], at=pre)
        c_b = sb("c_b", [D, B, 128], at=pre)
        wmod = sb("wmod", [D, 6, D], at=pre)
        cos = sb("cos", [128, S], at=pre)
        sin = sb("sin", [128, S], at=pre)
        rot = sb("rot", [128, 2, 2, 2, CH], at=pre)
        qk_parts = sb("qk_parts", [128, 2, 2, NP, CH], BF16, at=pre)
        pre.close()
        probs = [sb(f"probs{m}", [T, HQ, CH], at=att) for m in range(4)]
        att.close()

        moe = ctx
        h2_hi = sb("h2_hi", [D, NT * T], F32R, at=moe)
        h2_lo = sb("h2_lo", [D, NT * T], F32R, at=moe)
        w_raw = sb("w_raw", [D, 2, 2, NI], at=moe)
        w_hi = sb("w_hi", [D, EX, 2, NI], F32R, at=moe)
        w_lo = sb("w_lo", [D, EX, 2, NI], F32R, at=moe)
        wd = sb("wd", [128, EX, len(IC), D], at=moe)
        rows = sb("rows", [T, NT, RW], at=moe)
        logit = sb("logit", [T, NT, NE], at=moe)
        prob = sb("prob", [T, NT, NE], at=moe)
        rank = sb("rank", [T, NT, NE], at=moe)
        chosen = sb("chosen", [T, NT, NE], at=moe)
        rsum = sb("rsum", [T, NT], at=moe)
        sel = sb("sel", [T, NT, NE], at=moe)
        tot = sb("tot", [T, NT, NE], at=moe)
        scan = sb("scan", [T, 2, NT, NE], at=moe)
        reached = sb("reached", [T, NE, NT], at=moe)
        tcount = sb("tcount", [T, NE], at=moe)
        tend = sb("tend", [T, 2, NE], at=moe)
        tbase = sb("tbase", [T, NE], at=moe)
        passed = sb("passed", [1, ST, NE], at=moe)
        expert_f = sb("expert_f", [1, ST], at=moe)
        expert = sb("expert", [1, ST], I32, at=moe)
        slot_f = sb("slot_f", [T, TOP, NT], at=moe)
        slot = sb("slot", [T, TOP, NT], I32, at=moe)
        acc = sb("acc", [T, 2, CG, D], at=moe)
        sg = sb("sg", [128, 2, NI], at=moe)
        srow = sb("srow", [T, SB, RW], at=moe)
        s_weight = sb("s_weight", [T, ST], at=moe)
        s_dest_f = sb("s_dest_f", [T, ST], at=moe)
        s_dest = sb("s_dest", [T, SB], I32, at=moe)
        shared_only = ExitStack()
        sgs = sb("sgs", [128, 3, CH], at=shared_only)
        hid = sb("hid", [128, 2, len(IC), CH], at=shared_only)
        beats = hid[:].rearrange("p u c n -> p (u c n)")[:, 0:NT * NE * NE].rearrange("p (t e f) -> p t e f", t=NT, e=NE)
        shared_only.close()
        h_hi = sb("h_hi", [D, 2, T], F32R, at=moe)
        h_lo = sb("h_lo", [D, 2, T], F32R, at=moe)
        hid_s = sb("hid_s", [T, 2, NI], at=moe)
        hidT = sb("hidT", [128, 2, len(IC), T], at=moe)
        y_s = sb("y_s", [T, SB, D], at=moe)
        y_in = [h2_hi[:].bitcast(F32).rearrange("p (t d) -> p t d", t=NT),
                h2_lo[:].bitcast(F32).rearrange("p (t d) -> p t d", t=NT)]

        ps = ctx.enter_context(nc.psum_tensor("ps", [128, 8, CH], F32))

        s_in0 = sem("s_in0")
        s_in = sem("s_in")
        s_x = [sem(f"s_x_row{b}") for b in range(B)]
        s_link = sem("s_link")
        s_glink = sem("s_glink")
        s_csilu = sem("s_csilu")
        s_cb = sem("s_cb")
        s_modps = sem("s_modps")
        s_mod = sem("s_mod")
        s_wo = sem("s_wo")
        s_raw = sem("s_raw")
        s_var = sem("s_var")
        s_std = sem("s_std")
        s_seen_act, s_seen_pool, s_seen_dve = sem("s_seen_act"), sem("s_seen_pool"), sem("s_seen_dve")
        s_xn = sem("s_xn")
        s_tp = sem("s_tp")
        s_hT = sem("s_hT")
        s_qk = sem("s_qk")
        s_prod = sem("s_prod")
        s_sum = sem("s_sum")
        s_hi = sem("s_hi")
        s_rest = sem("s_rest")
        s_mid = sem("s_mid")
        s_v = sem("s_v")
        s_v_free = sem("s_v_free")
        s_parts = sem("s_parts")
        s_spill = [sem(f"s_spill{m}") for m in range(2)]
        s_fill = sem("s_fill")
        s_qk_in = [sem(f"s_qk_in{m}") for m in range(3)]
        s_ring = sem("s_ring")
        s_ring_free = sem("s_ring_free")
        s_rowmax = sem("s_rowmax")
        s_mparts = sem("s_mparts")
        s_m_in = [sem(f"s_m_in{m}") for m in range(3)]
        s_scores = sem("s_scores")
        s_exp = sem("s_exp")
        s_mask = sem("s_mask")
        s_pv = sem("s_pv")
        s_outT = sem("s_outT")
        s_v4 = sem("s_v4")
        s_ot = sem("s_ot")
        s_oT = sem("s_oT")
        s_proj = sem("s_proj")
        s_x2 = sem("s_x2")
        s_var2 = sem("s_var2")
        s_std2 = sem("s_std2")
        s_xn2 = sem("s_xn2")
        s_tp2 = sem("s_tp2")
        s_hT2 = sem("s_hT2")
        s_lg = sem("s_lg")
        s_lg_free = sem("s_lg_free")
        s_h2_hi = sem("s_h2_hi")
        s_split2 = sem("s_split2")
        s_max7 = sem("s_max7")
        s_exp7 = sem("s_exp7")
        s_wraw = [sem(f"s_wraw{m}") for m in range(2)]
        s_whi = sem("s_whi")
        s_wlo = sem("s_wlo")
        s_wd = sem("s_wd")
        s_gu = sem("s_gu")
        s_silu = sem("s_silu")
        s_hid = sem("s_hid")
        s_dn = sem("s_dn")
        s_dn_free = sem("s_dn_free")
        s_shared = sem("s_shared")
        s_scaled = sem("s_scaled")
        s_rows = sem("s_rows")
        s_beats = sem("s_beats")
        s_sel = sem("s_sel")
        s_prefix = sem("s_prefix")
        s_slot = sem("s_slot")
        s_expert = sem("s_expert")
        s_pad_out = sem("s_pad_out")
        s_scatter = sem("s_scatter")
        s_srow = [sem(f"s_srow{j}") for j in range(SB)]
        s_rowT = sem("s_rowT")
        s_meta = sem("s_meta")
        s_h_hi = sem("s_h_hi")
        s_h_lo = sem("s_h_lo")
        s_sgu = sem("s_sgu")
        s_ssilu = sem("s_ssilu")
        s_shid = sem("s_shid")
        s_shidT = sem("s_shidT")
        s_hidT = sem("s_hidT")
        s_sdn = sem("s_sdn")
        s_y = sem("s_y")
        s_dest_i = sem("s_dest_i")
        s_y_out = [sem(f"s_y_out{j}") for j in range(SB)]
        s_y_in = [sem(f"s_y_in{n}") for n in range(2 * B)]
        s_y_sum = sem("s_y_sum")
        s_res = sem("s_res")
        s_out = sem("s_out")

        block = ctx.enter_context(nc.Block())

        def quad(i, r):
            return 3 * i + r

        def third(i, r):
            return i + r // 3

        FULL = ring_plan(True, True, True)
        FIRST = ring_plan(False, True, True)
        PRE = [("max", 0, p) for p in range(NM)] + [("shift", 0, None)] + [("max", 1, p) for p in range(EARLY)]
        LAST1 = ring_plan(True, True, False)
        LAST0 = ring_plan(True, False, False)
        R1 = len(PRE) + len(FIRST)
        RL = len(FULL)
        assert RL % RING == 0

        def ring_base(i, r):
            if isinstance(i, int):
                n = quad(i, r)
                if n == 0:
                    return len(PRE)
                return R1 + RL * (min(n, NQ - 2) - 1) + (len(LAST1) if n >= NQ - 1 else 0) \
                    + (len(LAST0) if n >= NQ else 0)
            return quad(i, r) * RL + (R1 - RL)

        def ring_bank(i, r, k):
            if isinstance(i, int):
                return (ring_base(i, r) + k) % RING
            return (R1 + k) % RING

        def plan_of(i, r):
            if isinstance(i, int):
                n = quad(i, r)
                return {0: FIRST, NQ - 2: LAST1, NQ - 1: LAST0}.get(n, FULL)
            return FULL

        def quads(eng, body):
            body(0, 0)
            with eng.Fori(0, 4) as i:
                for r in (1, 2, 3):
                    body(i, r)
            for r in (1, 2, 3):
                body(4, r)

        def slot_steps(eng, first, last, body):
            stop = (ST - SB - 1) // SU
            for s in range(first, SU):
                body(0, s)
            with eng.Fori(1, stop) as i:
                for r in range(SU):
                    body(i, r)
            for s in range(stop * SU, last + 1):
                body(0, s)

        def tile(i, r, lag):
            t = SU * i + (r - lag)
            if isinstance(t, int) and not 0 <= t < ST:
                return None
            return t, (r - lag) % SB, SU // SB * i + (r - lag) // SB

        def needs(eng, semaphore, value):
            if not (isinstance(value, int) and value <= 0):
                eng.wait_ge(semaphore, value)

        @block.sync
        def _(sp):
            for dst, src in ((c_t[:], c_d), (wmod[:], wmod_d.rearrange("k (j f) -> k j f", j=6)),
                             (eye[:], eye_d)):
                sp.dma_start(dst, src).then_inc(s_in0, 16)
            xv = x_d.rearrange("(t p) d -> p t d", p=T)
            for b in range(B):
                sp.dma_start(xs[:, b * TB:(b + 1) * TB, :], xv[:, b * TB:(b + 1) * TB, :]).then_inc(s_x[b], 16)
            for dst, src in ((wq[:], wq_d.rearrange("j k m -> k j m")), (wk[:], wk_d.rearrange("j k m -> k j m")),
                             (wv[:], wv_d), (cos[:], cos_d), (sin[:], sin_d), (wo[:], wo_d), (tri[:], tri_d),
                             (wr[:], wr_d), (rb[:], rb_d[0:1, :].to_broadcast((128, NE))), (cst[:], cst_d)):
                sp.dma_start(dst, src).then_inc(s_in, 16)

            def spill(b, u):
                for p, cut in enumerate((s_hi, s_mid, s_parts)):
                    for w, scr in enumerate((qs_d, ks_d)):
                        sp.wait_ge(cut, (b * 2 + u) * 2 + w + 1)
                        dst = scr[bass.ds(b * NG, NG), p, :, u * CH:(u + 1) * CH]
                        sp.dma_start(dst, qk_parts[:, u, w, p, :]).then_inc(s_spill[u], 16)

            def load_quad(i, r):
                n, m = quad(i, r), r % 3
                q = qs_d[bass.ds(n, 1), :, :, :].rearrange("n p (d h) s -> (n p d) (h s)", h=HQ)
                k = ks_d[bass.ds(n, 1), :, :, :].rearrange("n p (d h) s -> (n p d) (h s)", h=HQ)
                w = NP * DK
                for j in range(NP):
                    sp.dma_start(qa[m][j * w:(j + 1) * w, :], q[0:w, :]).then_inc(s_qk_in[m], 16)
                    mid = (j + 1) * w - j * DK
                    sp.dma_start(ka[m][j * w:mid, :], k[j * DK:w, :]).then_inc(s_qk_in[m], 16)
                    if j:
                        sp.dma_start(ka[m][mid:(j + 1) * w, :], k[0:j * DK, :]).then_inc(s_qk_in[m], 16)

            def load_shift(i, r):
                m = r % 3
                sp.wait_ge(s_mparts, quad(i, r) + 1)
                for p in range(NP):
                    sp.dma_start(qa[m][KR + p:KR + p + 1, :].rearrange("o (a t) -> o a t", t=T),
                                 mparts[m][:, p, :]).then_inc(s_m_in[m], 16)

            UNIT = 16 * 2 * NP
            for u in range(2):
                spill(0, u)
            for u in range(2):
                sp.wait_ge(s_spill[u], UNIT + 16)
            sp.wait_ge(s_fill, 1)
            for u in range(2):
                spill(1, u)
            load_quad(0, 0)
            with sp.Fori(2, B) as b:
                for u in range(2):
                    spill(b, u)
            load_quad(0, 1)
            for u in range(2):
                sp.wait_ge(s_spill[u], B * UNIT + 16)
            load_shift(0, 0)

            pad0, _ = CST["pad"]
            sp.wait_ge(s_in, 16 * 10)
            sp.dma_start(slot_d.rearrange("(t p) c -> p t c", p=T),
                         cst[:, pad0:pad0 + RW].unsqueeze(1).to_broadcast((T, ST, RW))).then_inc(s_pad_out, 16)

            def body(i, r):
                n = quad(i, r)
                if not (isinstance(i, int) and n + 2 >= NQ):
                    if not (isinstance(i, int) and n == 0):
                        sp.wait_ge(s_scores, n * (2 * NS))
                    load_quad(i, r + 2)
                if not (isinstance(i, int) and n + 1 >= NQ):
                    load_shift(i, r + 1)
            quads(sp, body)

            sp.wait_ge(s_ring_free, ring_base(0, NQ) + 1)
            for c, (i0, w) in enumerate(IC):
                sp.dma_start(wd[0:w, :, c, :], sw_d_d[:, i0:i0 + w, :].rearrange("e p h -> p e h")).then_inc(s_wd, 16)
            for e in range(EX):
                if e >= 2:
                    sp.wait_ge(s_wlo, e - 1)
                sp.dma_start(w_raw[:, e % 2, 0, :], sw_g_d[e, :, :]).then_inc(s_wraw[e % 2], 16)
                sp.dma_start(w_raw[:, e % 2, 1, :], sw_u_d[e, :, :]).then_inc(s_wraw[e % 2], 16)

            sp.wait_ge(s_scatter, 16 * TOP * NT)

            def load_rows(i, r):
                at = tile(i, r, -SB - 1)
                if at:
                    t, j, times = at
                    needs(sp, s_rowT, t - SB + 1)
                    needs(sp, s_meta, t - SB + 1)
                    sp.dma_start(srow[:, j, :], slot_d[bass.ds(t * T, T), :]).then_inc(s_srow[j], 16)
            slot_steps(sp, -SB - 1, ST - SB - 2, load_rows)

            yv = y_d[0:TOP * B * S, :].rearrange("(k t p) d -> k p t d", k=TOP, p=T)
            for j in range(SB):
                sp.wait_ge(s_y_out[j], 16 * ((ST + SB - 1 - j) // SB))
            for n in range(2 * B):
                for k in range(TOP):
                    sp.dma_start(y_in[k][:, n * CG:(n + 1) * CG, :], yv[k, :, n * CG:(n + 1) * CG, :]).then_inc(s_y_in[n], 16)
            ov = out_d.rearrange("(t p) d -> p t d", p=T)
            for n in range(2 * B):
                sp.wait_ge(s_res, n + 1)
                sp.dma_start(ov[:, n * CG:(n + 1) * CG, :], xs[:, n * CG:(n + 1) * CG, :]).then_inc(s_out, 16)
            sp.wait_ge(s_out, 16 * 2 * B)

        @block.gpsimd
        def _(pool):
            for m in range(3):
                nc.gpsimd.memset(ka[m][64:KM, :], 1.0)
                last = nc.gpsimd.memset(qa[m][64:KM, :], 0.0)
            last.then_inc(s_fill, 1)
            pool.wait_ge(s_fill, 1)
            for m in range(3):
                nc.gpsimd.memset(v4[m][:], 0.0).then_inc(s_glink, 1)
            pool.wait_ge(s_glink, 3)
            for m in range(3):
                nc.gpsimd.memset(v4[m][:, :, :, DK:DK + 1], 1.0).then_inc(s_glink, 1)
            pool.wait_ge(s_glink, 6)

            def values(i, r):
                m = r % 3
                nc.gpsimd.tensor_copy(v4[m][:, :, :, 0:DK],
                                      v_all[:, bass.ds(quad(i, r), 1), :, :].rearrange("p n k (h d) -> p (n k) h d", h=HQ)
                                      ).then_inc(s_v4, 1)

            with pool.Fori(0, B) as b:
                for u in range(2):
                    for w in range(2):
                        pool.wait_ge(s_mid, (b * 2 + u) * 2 + w + 1)
                        pool.sem_inc(s_seen_pool, 1)
                        nc.gpsimd.tensor_tensor(qk_parts[:, u, w, 2, :], rot[:, u, w, 1, :], qk_parts[:, u, w, 1, :],
                                                ALU.subtract).then_inc(s_parts, 1)

            pool.wait_ge(s_v_free, 2 * B)
            values(0, 0)

            def body(i, r):
                n = quad(i, r)
                if not (isinstance(i, int) and n + 1 >= NQ):
                    if not (isinstance(i, int) and n == 0):
                        pool.wait_ge(s_pv, n * NS - (NS - 1))
                    values(i, r + 1)
                for s, (c, k, q0) in enumerate(STEPS):
                    if k < CG * c:
                        continue
                    pool.wait_ge(s_exp, n * (2 * NS) + 2 * (s + 1))
                    pool.sem_inc(s_seen_pool, 1)
                    p = probs[s % 4][:, :, 0:T]
                    nc.gpsimd.affine_select(out=p, in_=p, compare_op=ALU.is_ge, fill=0.0, base=0,
                                            pattern=[[0, HQ], [1, T]], channel_multiplier=-1).then_inc(s_mask, 1)
            quads(pool, body)

            def second_part(e):
                pool.wait_ge(s_whi, e + 1)
                nc.gpsimd.tensor_tensor(w_lo[:, e, :, :], w_raw[:, e % 2, :, :], w_hi[:, e, :, :].bitcast(F32),
                                        ALU.subtract).then_inc(s_wlo, 1)
            for e in range(EX // 2):
                second_part(e)
            with pool.Fori(0, B) as b:
                for u in range(2):
                    n = b * 2 + u
                    tiles = bass.ds(b * TB + u * CG, CG)
                    pool.wait_ge(s_xn2, n + 1)
                    pool.sem_inc(s_seen_pool, 1)
                    nc.gpsimd.tensor_tensor(rows[:, tiles, 0:D], xn[:, tiles, :],
                                            mod2_rows[:, 1, bass.ds(b, 1), :].to_broadcast((T, CG, D)), ALU.mult).then_inc(s_scaled, 1)
                    pool.wait_ge(s_scaled, n + 1)
                    pool.sem_inc(s_seen_pool, 1)
                    nc.gpsimd.tensor_tensor(rows[:, tiles, 0:D], rows[:, tiles, 0:D],
                                            mod2_rows[:, 0, bass.ds(b, 1), :].to_broadcast((T, CG, D)), ALU.add).then_inc(s_rows, 1)
            for e in range(EX // 2, EX):
                second_part(e)

            pool.wait_ge(s_rows, 2 * B)
            pool.wait_ge(s_pad_out, 16)
            for k in range(TOP):
                pool.wait_ge(s_slot, k + 1)
                for t in range(NT):
                    nc.gpsimd.indirect_dma_start(slot_d, bass.IndirectOffsetOnAxis(ap=slot[:, k, t:t + 1], axis=0),
                                                 rows[:, t, :], None).then_inc(s_scatter, 16)

            pool.wait_ge(s_expert, 1)

            def slot_step(i, r):
                at = tile(i, r, -2)
                if at:
                    t, j, times = at
                    t2 = j % 2
                    pool.wait_ge(s_srow[j], 16 * times + 16)
                    e = pool.value_load(expert[0:1, bass.ds(t, 1)], min_val=1, max_val=NE)
                    nc.gpsimd.tensor_copy(s_weight[:, bass.ds(t, 1)], srow[:, j, bass.ds(D - 1 + e, 1)])
                    nc.gpsimd.tensor_tensor(s_dest_f[:, bass.ds(t, 1)], srow[:, j, bass.ds(D + NE - 1 + e, 1)],
                                            cst[:, bass.ds(CST["spare"][0] + t, 1)], ALU.add).then_inc(s_meta, 1)
                at = tile(i, r, 3)
                if at:
                    t, j, times = at
                    t2 = j % 2
                    needs(pool, s_y_out[j], 16 * times)
                    pool.sem_inc(s_seen_pool, 1)
                    nc.gpsimd.tensor_copy(s_dest[:, j:j + 1], s_dest_f[:, bass.ds(t, 1)]).then_inc(s_dest_i, 1)
                    pool.wait_ge(s_dest_i, t + 1)
                    pool.wait_ge(s_y, t + 1)
                    pool.sem_inc(s_seen_pool, 1)
                    nc.gpsimd.indirect_dma_start(y_d, bass.IndirectOffsetOnAxis(ap=s_dest[:, j:j + 1], axis=0),
                                                 y_s[:, j, :], None).then_inc(s_y_out[j], 16)
            slot_steps(pool, -2, ST + 2, slot_step)

            for n in range(2 * B):
                ts = slice(n * CG, (n + 1) * CG)
                pool.wait_ge(s_y_in[n], 16 * TOP)
                nc.gpsimd.tensor_tensor(y_in[0][:, ts, :], y_in[0][:, ts, :], y_in[1][:, ts, :], ALU.add).then_inc(s_y_sum, 1)

        @block.scalar
        def _(act):
            act.wait_ge(s_in0, 48)
            nc.scalar.activation(c_s[:], c_t[:], ACT.Silu).then_inc(s_csilu, 1)
            act.wait_ge(s_modps, 1)
            for bank, dst in ((1, gate_a[:]), (2, gate_b[:]), (3, mod2_rows[:, 0, :, :]), (4, mod2_rows[:, 1, :, :])):
                nc.scalar.activation(dst, ps[:, bank, :].rearrange("p (b d) -> p b d", b=B), ACT.Copy).then_inc(s_raw, 1)
            act.wait_ge(s_var, 1)
            nc.scalar.activation(rstd[:], rstd[:], ACT.Sqrt).then_inc(s_std, 1)
            act.wait_ge(s_mod, 1)

            def modulate(b, u):
                act.wait_ge(s_tp, b * 2 + u + 1)
                act.sem_inc(s_seen_act, 1)
                nc.scalar.activation(hT[:, u, :], ps[:, u, :], ACT.Identity, scale=mod1[:, 0, bass.ds(b, 1)],
                                     bias=mod1[:, 1, bass.ds(b, 1)]).then_inc(s_hT, 1)

            def project(b, u, more):
                n = b * 2 + u
                for w in range(2):
                    act.wait_ge(s_sum, n * 2 + w + 1)
                    nc.scalar.activation(qk_parts[:, u, w, 0, :], rot[:, u, w, 0, :], ACT.Copy).then_inc(s_hi, 1)
                for w in range(2):
                    act.wait_ge(s_rest, n * 2 + w + 1)
                    nc.scalar.activation(qk_parts[:, u, w, 1, :], rot[:, u, w, 1, :], ACT.Copy).then_inc(s_mid, 1)
                act.wait_ge(s_v, n + 1)
                act.sem_inc(s_seen_act, 1)
                nc.scalar.activation(
                    v_all[:, bass.ds(b * NG, NG), u * CG:(u + 1) * CG, :].rearrange("p g j e -> p j g e"),
                    ps[:, 6 + u, :].rearrange("p (j g e) -> p j g e", j=CG, g=NG), ACT.Copy).then_inc(s_v_free, 1)
                if more:
                    modulate(b + 1, u)

            for u in range(2):
                modulate(0, u)
            with act.Fori(0, B - 1) as b:
                for u in range(2):
                    project(b, u, True)
            for u in range(2):
                project(B - 1, u, False)

            def copy_out(i, r, c):
                n = quad(i, r)
                act.wait_ge(s_pv, n * NS + CG + c * 2 * CG)
                if not (isinstance(i, int) and n == 0):
                    j, q = (i, r) if c else (i, r - 1)
                    if isinstance(i, int):
                        j, q = 0, quad(i, q)
                    at = [x[1:] for x in plan_of(j, q)].index(("norm", -1, 1) if c else ("norm", 0, 0))
                    act.wait_ge(s_ring, ring_base(j, q) + (at + 1))
                nc.scalar.activation(outT[:, c, :], ps[:, 4, :], ACT.Copy).then_inc(s_outT, 1)

            def body(i, r):
                n = quad(i, r)
                first = isinstance(i, int) and n == 0
                for s, (c, k, q0) in enumerate(STEPS):
                    if not (first and s < 4):
                        act.wait_ge(s_pv, n * NS + s - 3)
                    for h in range(2):
                        act.wait_ge(s_scores, n * (2 * NS) + 2 * s + h + 1)
                        nc.scalar.activation(probs[s % 4][:, 2 * h:2 * h + 2, 0:CH - q0], ps[:, 2 * h:2 * h + 2, q0:CH],
                                             ACT.Exp, scale=SCALE).then_inc(s_exp, 1)
                    if s == 1 and not first:
                        copy_out(i, r - 1, 1)
                    if s == 5:
                        copy_out(i, r, 0)
            quads(act, body)
            copy_out(5, 0, 1)

            for u in range(2):
                act.wait_ge(s_ot, u + 1)
                nc.scalar.activation(oT[:, u, :], ps[:, u, :], ACT.Copy).then_inc(s_oT, 1)

            def first_part(e):
                act.wait_ge(s_wraw[e % 2], 32 * (e // 2 + 1))
                nc.scalar.activation(w_hi[:, e, :, :], w_raw[:, e % 2, :, :], ACT.Copy).then_inc(s_whi, 1)
            act.wait_ge(s_var2, 1)
            nc.scalar.activation(rstd[:], rstd[:], ACT.Sqrt).then_inc(s_std2, 1)
            for e in range(EX // 2):
                first_part(e)
            with act.Fori(0, B) as b:
                for u in range(2):
                    n = b * 2 + u
                    act.wait_ge(s_tp2, n + 1)
                    act.wait_ge(s_lg_free, n + 1)
                    act.sem_inc(s_seen_act, 1)
                    nc.scalar.activation(hT[:, u, :], ps[:, 4 + u, :], ACT.Identity, scale=mod2[:, 0, bass.ds(b, 1)],
                                         bias=mod2[:, 1, bass.ds(b, 1)]).then_inc(s_hT2, 1)
                    nc.scalar.activation(h2_hi[:, bass.ds(n * CH, CH)], ps[:, 4 + u, :], ACT.Identity,
                                         scale=mod2[:, 0, bass.ds(b, 1)], bias=mod2[:, 1, bass.ds(b, 1)]).then_inc(s_h2_hi, 1)
            act.wait_ge(s_max7, 1)
            nc.scalar.activation(prob[:], logit[:], ACT.Exp).then_inc(s_exp7, 1)
            for e in range(EX // 2, EX):
                first_part(e)

            with act.Fori(0, B) as b:
                for u in range(2):
                    for c, (i0, w) in enumerate(IC):
                        g = (b * 2 + u) * len(IC) + c
                        act.wait_ge(s_gu, g + 1)
                        act.wait_ge(s_hid, g + 1)
                        nc.scalar.activation(sgs[0:w, c, :], ps[0:w, 2 * c, :], ACT.Silu).then_inc(s_silu, 1)

            def slot_step(i, r):
                at = tile(i, r, -1)
                if at:
                    t, j, _ = at
                    t2 = j % 2
                    act.wait_ge(s_rowT, t + 1)
                    needs(act, s_sgu, t - 1)
                    nc.scalar.activation(h_hi[:, t2, :], ps[:, 0, 0:T], ACT.Copy).then_inc(s_h_hi, 1)
                at = tile(i, r, 0)
                if at:
                    t, j, _ = at
                    t2 = j % 2
                    act.wait_ge(s_sgu, t + 1)
                    needs(act, s_shid, t - 1)
                    nc.scalar.activation(sg[:, t2, :], ps[:, 1 + 2 * t2, 0:NI], ACT.Silu).then_inc(s_ssilu, 1)
                at = tile(i, r, 2)
                if at:
                    t, j, times = at
                    t2 = j % 2
                    act.wait_ge(s_sdn, t + 1)
                    act.wait_ge(s_meta, t + 1)
                    needs(act, s_y_out[j], 16 * times)
                    act.sem_inc(s_seen_act, 1)
                    nc.scalar.activation(y_s[:, j, :], ps[:, 6, 0:D], ACT.Copy, scale=s_weight[:, bass.ds(t, 1)]).then_inc(s_y, 1)
                at = tile(i, r, 1)
                if at:
                    t, j, _ = at
                    t2 = j % 2
                    act.wait_ge(s_shidT, t + 1)
                    needs(act, s_sdn, t - 1)
                    nc.scalar.activation(hidT[:, t2, 0:2, :], ps[:, 5, 0:2 * T].rearrange("p (c t) -> p c t", c=2), ACT.Copy)
                    w = IC[2][1]
                    nc.scalar.activation(hidT[0:w, t2, 2, :], ps[0:w, 5, 2 * T:3 * T], ACT.Copy).then_inc(s_hidT, 1)
            slot_steps(act, -1, ST + 1, slot_step)

        @block.vector
        def _(dve):
            chain = [0]

            def link(ins):
                chain[0] += 1
                ins.then_inc(s_link, 1)
                dve.wait_ge(s_link, chain[0])

            V = nc.vector
            dve.sem_inc(s_prod, 2)
            dve.sem_inc(s_hT, 2)
            dve.sem_inc(s_lg_free, 2)
            dve.sem_inc(s_hid, len(IC))
            dve.sem_inc(s_dn_free, 1)
            for u in range(2):
                dve.sem_inc(s_spill[u], 16)

            def tile_stats(t0, count):
                for j in range(count):
                    V.bn_stats(stats[:, bass.ds(t0 + j, 1), :].rearrange("p o s -> p (o s)"),
                               xs[:, bass.ds(t0 + j, 1), :].rearrange("p o s -> p (o s)"))

            def layernorm_scale(done, std):
                m0, q0, m1, q1 = stats[:, :, 1], stats[:, :, 2], stats[:, :, 4], stats[:, :, 5]
                link(V.drain())
                link(V.tensor_tensor(mean[:], m0, m1, ALU.add))
                link(V.tensor_tensor(part_a[:], m0, m1, ALU.subtract))
                link(V.tensor_tensor(part_b[:], q0, q1, ALU.add))
                link(V.tensor_scalar(mean[:], mean[:], 0.5, None, ALU.mult))
                link(V.tensor_tensor(part_a[:], part_a[:], part_a[:], ALU.mult))
                link(V.tensor_scalar(part_b[:], part_b[:], 1.0 / D, EPS, ALU.mult, ALU.add))
                V.scalar_tensor_tensor(rstd[:], part_a[:], 0.25, part_b[:], ALU.mult, ALU.add).then_inc(done, 1)
                dve.wait_ge(std, 1)
                link(V.reciprocal(rstd[:], rstd[:]))

            dve.wait_ge(s_csilu, 1)
            V.tensor_copy(c_b[:], c_s[:].unsqueeze(2).to_broadcast((D, B, 128))).then_inc(s_cb, 1)
            for b in range(B):
                dve.wait_ge(s_x[b], 16)
                tile_stats(b * TB, TB)
            layernorm_scale(s_var, s_std)
            dve.wait_ge(s_modps, 1)
            mps = ps[:, 0, 0:4 * B].rearrange("p (j b) -> p j b", b=B)
            for m, j in ((mod1, 0), (mod2, 2)):
                link(V.tensor_scalar(m[:, 0, :], mps[:, j + 1, :], 1.0, None, ALU.add))
                link(V.tensor_copy(m[:, 1, :], mps[:, j, :]))
            dve.sem_inc(s_mod, 1)

            def normalise(done):
                with dve.Fori(0, B) as b:
                    for j in range(TB):
                        t = b * TB + j
                        last = V.tensor_scalar(xn[:, bass.ds(t, 1), :].rearrange("p o d -> p (o d)"),
                                               xs[:, bass.ds(t, 1), :].rearrange("p o d -> p (o d)"),
                                               mean[:, bass.ds(t, 1)], rstd[:, bass.ds(t, 1)],
                                               ALU.subtract, ALU.mult)
                        if j % CG == CG - 1:
                            last.then_inc(done, 1)
            normalise(s_xn)
            dve.wait_ge(s_in, 16 * 10)

            with dve.Fori(0, B) as b:
                for u in range(2):
                    n = b * 2 + u
                    dve.wait_ge(s_spill[u], b * (16 * 2 * NP) + 16)
                    part = [[qk_parts[:, u, w, p, :] for p in range(NP)] for w in range(2)]
                    ra = [rot[:, u, w, 0, :] for w in range(2)]
                    rb_ = [rot[:, u, w, 1, :] for w in range(2)]

                    def products(w):
                        dve.wait_ge(s_qk, n * 2 + w + 1)
                        V.tensor_tensor(ra[w], ps[:, 2 + 2 * w, :], cos[:, u * CH:(u + 1) * CH], ALU.mult)
                        V.tensor_tensor(rb_[w], ps[:, 3 + 2 * w, :], sin[:, u * CH:(u + 1) * CH],
                                        ALU.mult).then_inc(s_prod, 1)

                    def rotated(w):
                        dve.wait_ge(s_prod, n * 2 + w + 3)
                        V.tensor_tensor(ra[w], ra[w], rb_[w], ALU.add).then_inc(s_sum, 1)

                    def rest(w):
                        dve.wait_ge(s_hi, n * 2 + w + 1)
                        V.tensor_tensor(rb_[w], ra[w], part[w][0], ALU.subtract).then_inc(s_rest, 1)

                    products(0)
                    products(1)
                    rotated(0)
                    rotated(1)
                    rest(0)
                    rest(1)

            dve.wait_ge(s_raw, 4)
            for g in (gate_a, gate_b):
                row = g[:].rearrange("p b d -> p (b d)")
                link(V.tensor_scalar(junk[:, 0, :], row, 0.0, 2.0, ALU.is_ge, ALU.mult))
                link(V.tensor_scalar(junk[:, 1, :], row, -1.0, 0.25, ALU.mult, ALU.max))
                link(V.tensor_tensor(junk[:, 1, :], row, junk[:, 1, :], ALU.max))
                link(V.scalar_tensor_tensor(row, junk[:, 0, :], -1.0, junk[:, 1, :], ALU.add, ALU.mult))
            link(V.tensor_scalar(mod2_rows[:, 1, :, :], mod2_rows[:, 1, :, :], 1.0, None, ALU.add))
            link(V.tensor_tensor(wo_gated[:], wo[:].unsqueeze(1).to_broadcast((D, B, D)), gate_a[:], ALU.mult))
            dve.sem_inc(s_wo, 1)

            def shift_parts(m, bank, before):
                part = [mparts[m][:, p, :] for p in range(NP)]
                neg = ps[0:HQ * TB, bank, 0:T]
                V.tensor_scalar(part[0], neg, -1.0, None, ALU.mult).then_inc(s_link, 1)
                dve.wait_ge(s_link, before + 1)
                V.scalar_tensor_tensor(mrest[:], neg, -1.0, part[0], ALU.mult, ALU.subtract).then_inc(s_link, 1)
                dve.wait_ge(s_link, before + 2)
                dve.sem_inc(s_ring_free, 1)
                V.tensor_copy(part[1], mrest[:]).then_inc(s_link, 1)
                dve.wait_ge(s_link, before + 3)
                V.tensor_tensor(part[2], mrest[:], part[1], ALU.subtract).then_inc(s_mparts, 1)

            def bank_maxima(m, bank, what):
                h, parts = PIECES[what]
                at = 0
                for q, k0, w, diag in parts:
                    src = ps[:, bank, at:at + w]
                    if diag:
                        last = V.tensor_tensor_reduce(out=junk[:, bank - 5, at:at + w], in0=src, in1=tri[:, CH - w:CH],
                                                      scale=1.0, scalar=LOW, op0=ALU.add, op1=ALU.max,
                                                      accum_out=rowmax[m][:, h, q:q + 1])
                    else:
                        last = V.reduce_max(leftmax[m][:, h, q - CG:q - CG + 1], src, AX.X)
                    at += w
                return last

            aux = chain[0]
            AUX = 7

            def ring_item(i, r, k, kind, off, what, before):
                bank = 5 + ring_bank(i, r, k)
                m = (r + off) % 3
                if kind == "max":
                    dve.sem_inc(s_seen_dve, 1)
                    bank_maxima(m, bank, what).then_inc(s_ring_free, 1)
                elif kind == "turn":
                    V.tensor_copy(oT[:, what % 2, :], ps[:, bank, :]).then_inc(s_ring_free, 1)
                elif kind == "project":
                    xt = xs[:, what * CG:(what + 1) * CG, :]
                    V.tensor_tensor(xt, xt, ps[:, bank, :].rearrange("p (j d) -> p j d", j=CG), ALU.add).then_inc(s_ring_free, 1)
                    dve.wait_ge(s_ring_free, ring_base(i, r) + (k + 1))
                    tile_stats(what * CG, CG)
                elif kind == "shift":
                    shift_parts(m, bank, before)
                    return 3
                else:
                    c = what
                    src = ps[:, bank, :].rearrange("p (j h w) -> p j h w", j=CG, h=HQ)
                    V.reciprocal(recip[:], src[:, :, :, DK]).then_inc(s_link, 1)
                    dve.wait_ge(s_link, before + 1)
                    dst = o_quads[:, c * CG:(c + 1) * CG, bass.ds(quad(i, r + off), 1), :]
                    V.tensor_tensor(dst.rearrange("p j n (h d) -> p (j n) h d", h=HQ), src[:, :, :, 0:DK],
                                    recip[:].unsqueeze(3).to_broadcast((T, CG, HQ, DK)), ALU.mult).then_inc(s_ring_free, 1)
                    dve.sem_inc(s_link, 1)
                    return 2
                return 0

            def full_max(m):
                V.tensor_tensor(rowmax[m][:, :, CG:TB], rowmax[m][:, :, CG:TB], leftmax[m][:], ALU.max).then_inc(s_rowmax, 1)

            for k, (kind, off, what) in enumerate(PRE):
                dve.wait_ge(s_ring, k + 1)
                if kind == "max":
                    bank_maxima(off % 3, 5 + k % RING, what).then_inc(s_ring_free, 1)
                    if what == NM - 1:
                        dve.wait_ge(s_ring_free, k + 1)
                        full_max(off % 3)
                else:
                    shift_parts(off % 3, 5 + k % RING, aux)
            l0 = aux + 3

            def body(i, r):
                n = quad(i, r)
                plan = plan_of(i, r)
                links = 0
                first = isinstance(i, int) and n == 0
                lbase = l0 if first else n * AUX + (l0 - 2)
                rbase = ring_base(i, r)
                for k, (s, kind, off, what) in enumerate(plan):
                    if k and kind == "norm" and plan[k - 1][1] == "norm":
                        dve.wait_ge(s_ring_free, rbase + k)
                    dve.wait_ge(s_ring, rbase + (k + 1))
                    links += ring_item(i, r, k, kind, off, what, lbase + links)
                    if kind == "max" and what == NM - 1:
                        dve.wait_ge(s_ring_free, rbase + (k + 1))
                        full_max((r + off) % 3)
            quads(dve, body)
            endbase = ring_base(5, 1)
            dve.wait_ge(s_ring_free, endbase)
            dve.wait_ge(s_ring, endbase + 1)
            lend = l0 - 2 + NQ * AUX - 3
            ring_item(5, 1, 0, "norm", -1, 1, lend)
            chain[0] = lend + 2

            def tile_pair(b, u):
                return b * TB + u * CG

            dve.wait_ge(s_ring_free, ring_base(0, NQ) + 1)
            b = B - 1
            for u in range(2):
                dve.wait_ge(s_proj, u + 1)
                xt = xs[:, bass.ds(tile_pair(b, u), CG), :]
                V.tensor_tensor(xt, xt, ps[:, 2 + u, :].rearrange("p (j d) -> p j d", j=CG),
                                ALU.add).then_inc(s_x2, 1)
                dve.wait_ge(s_x2, u + 1)
                tile_stats(tile_pair(b, u), CG)
            layernorm_scale(s_var2, s_std2)
            normalise(s_xn2)

            with dve.Fori(0, B) as b:
                for u in range(2):
                    n = b * 2 + u
                    dve.wait_ge(s_h2_hi, n + 1)
                    cols = bass.ds(n * CH, CH)
                    V.tensor_tensor(h2_lo[:, cols], hT[:, u, :], h2_hi[:, cols].bitcast(F32), ALU.subtract).then_inc(s_split2, 1)
                    dve.wait_ge(s_lg, n + 1)
                    V.tensor_tensor(logit[:, bass.ds(tile_pair(b, u), CG), :],
                                    ps[:, 6 + u, 0:CG * NE].rearrange("p (j e) -> p j e", j=CG),
                                    rb[:].unsqueeze(1).to_broadcast((T, CG, NE)), ALU.add).then_inc(s_lg_free, 1)

            dve.wait_ge(s_lg_free, 2 + 2 * B)
            link(V.tensor_reduce(rsum[:], logit[:], AX.X, ALU.max))
            V.tensor_tensor(logit[:], logit[:], rsum[:].unsqueeze(2).to_broadcast((T, NT, NE)), ALU.subtract).then_inc(s_max7, 1)
            dve.wait_ge(s_exp7, 1)
            link(V.reduce_sum(rsum[:], prob[:], AX.X))
            link(V.reciprocal(rsum[:], rsum[:]))
            link(V.tensor_tensor(prob[:], prob[:], rsum[:].unsqueeze(2).to_broadcast((T, NT, NE)), ALU.mult))
            V.memset(beats[:], 0.0).then_inc(s_beats, 1)
            dve.wait_ge(s_beats, 1)
            for j in range(NE):
                pj = prob[:, :, j:j + 1]
                if j:
                    last = V.tensor_tensor(beats[:, :, 0:j, j], pj.to_broadcast((T, NT, j)), prob[:, :, 0:j], ALU.is_gt)
                if j < NE - 1:
                    last = V.tensor_tensor(beats[:, :, j + 1:NE, j], pj.to_broadcast((T, NT, NE - 1 - j)),
                                           prob[:, :, j + 1:NE], ALU.is_ge)
            link(last)
            link(V.reduce_sum(rank[:], beats[:], AX.X))
            V.tensor_scalar(sel[:], rank[:], TOP - 0.5, None, ALU.is_lt).then_inc(s_sel, 1)

            dve.wait_ge(s_sel, 1)
            link(V.tensor_tensor(prob[:], prob[:], sel[:], ALU.mult))
            link(V.reduce_sum(rsum[:], prob[:], AX.X))
            link(V.reciprocal(rsum[:], rsum[:]))
            V.tensor_tensor(rows[:, :, D:D + NE], prob[:], rsum[:].unsqueeze(2).to_broadcast((T, NT, NE)), ALU.mult)

            def table(name, p=128):
                at, w = CST[name]
                return cst[0:p, at:at + w]
            V.scalar_tensor_tensor(rows[:, :, D + NE:RW], rank[:], float(B * S),
                                   table("token").unsqueeze(2).to_broadcast((T, NT, NE)), ALU.mult, ALU.add)

            dve.wait_ge(s_prefix, 1)
            before = ps[:, 2, 0:NT * NE].rearrange("p (t e) -> p t e", t=NT)
            total = ps[:, 2, NT * NE:2 * NT * NE].rearrange("p (t e) -> p t e", t=NT)
            V.tensor_copy(tot[:], total)
            link(V.tensor_copy(scan[:, 0, :, :], total))
            cur, step = 0, 1
            while step < NT:
                V.tensor_copy(scan[:, 1 - cur, 0:step, :], scan[:, cur, 0:step, :])
                link(V.tensor_tensor(scan[:, 1 - cur, step:NT, :], scan[:, cur, step:NT, :],
                                     scan[:, cur, 0:NT - step, :], ALU.add))
                cur, step = 1 - cur, 2 * step
            incl = scan[:, cur, :, :]
            link(V.tensor_tensor(reached[:], incl[:, NT - 1, :].unsqueeze(2).to_broadcast((T, NE, NT)),
                                 table("steps").unsqueeze(1).to_broadcast((T, NE, NT)), ALU.is_gt))
            link(V.reduce_sum(tcount[:], reached[:], AX.X))
            link(V.tensor_copy(tend[:, 0, :], tcount[:]))
            cur_e, step = 0, 1
            while step < NE:
                V.tensor_copy(tend[:, 1 - cur_e, 0:step], tend[:, cur_e, 0:step])
                link(V.tensor_tensor(tend[:, 1 - cur_e, step:NE], tend[:, cur_e, step:NE],
                                     tend[:, cur_e, 0:NE - step], ALU.add))
                cur_e, step = 1 - cur_e, 2 * step
            end = tend[:, cur_e, :]
            link(V.tensor_tensor(tbase[:], end, tcount[:], ALU.subtract))
            link(V.tensor_scalar(tbase[:], tbase[:], float(T), None, ALU.mult))
            link(V.tensor_tensor(tot[:], incl, tot[:], ALU.subtract))
            link(V.tensor_tensor(tot[:], tot[:], before, ALU.add))
            link(V.tensor_tensor(tot[:], tot[:], tbase[:].unsqueeze(1).to_broadcast((T, NT, NE)), ALU.add))
            link(V.tensor_tensor(rows[:, :, D + NE:RW], rows[:, :, D + NE:RW], tot[:], ALU.subtract))
            for k in range(TOP):
                link(V.tensor_scalar(sel[:], rank[:], float(k), None, ALU.is_equal))
                link(V.tensor_tensor(chosen[:], sel[:], tot[:], ALU.mult))
                link(V.reduce_sum(slot_f[:, k, :], chosen[:], AX.X))
                V.tensor_copy(slot[:, k, :], slot_f[:, k, :]).then_inc(s_slot, 1)
            link(V.tensor_tensor(passed[:], table("tiles", 1).unsqueeze(2).to_broadcast((1, ST, NE)),
                                 end[0:1, :].unsqueeze(1).to_broadcast((1, ST, NE)), ALU.is_ge))
            link(V.reduce_sum(expert_f[:], passed[:], AX.X))
            V.tensor_scalar(expert[:], expert_f[:], float(NE - 1), 1.0, ALU.min, ALU.add).then_inc(s_expert, 1)

            base4 = chain[0]
            with dve.Fori(0, B) as b:
                for u in range(2):
                    n = b * 2 + u
                    for c, (i0, w) in enumerate(IC):
                        dve.wait_ge(s_silu, n * len(IC) + c + 1)
                        V.tensor_tensor(hid[0:w, u, c, :], sgs[0:w, c, :], ps[0:w, 2 * c + 1, :], ALU.mult).then_inc(s_hid, 1)
                    dve.wait_ge(s_dn, n + 1)
                    V.tensor_tensor(acc[:, u, :, :], ps[:, 6, :].rearrange("p (j d) -> p j d", j=CG),
                                    gate_b[:, bass.ds(b, 1), :].to_broadcast((T, CG, D)), ALU.mult).then_inc(s_dn_free, 1)
                    dve.wait_ge(s_dn_free, n + 2)
                    xt = xs[:, bass.ds(tile_pair(b, u), CG), :]
                    V.tensor_tensor(xt, xt, acc[:, u, :, :], ALU.add).then_inc(s_shared, 1)

            def slot_step(i, r):
                at = tile(i, r, -1)
                if at:
                    t, j, _ = at
                    t2 = j % 2
                    dve.wait_ge(s_h_hi, t + 1)
                    V.tensor_tensor(h_lo[:, t2, :], ps[:, 0, 0:T], h_hi[:, t2, :].bitcast(F32), ALU.subtract).then_inc(s_h_lo, 1)
                at = tile(i, r, 0)
                if at:
                    t, j, _ = at
                    t2 = j % 2
                    dve.wait_ge(s_ssilu, t + 1)
                    needs(dve, s_shidT, t - 1)
                    V.tensor_tensor(hid_s[:, t2, :], sg[:, t2, :], ps[:, 2 + 2 * t2, 0:NI], ALU.mult).then_inc(s_shid, 1)
            slot_steps(dve, -1, ST + 1, slot_step)

            dve.wait_ge(s_shared, 2 * B)
            for n in range(2 * B):
                b, ts = n // 2, slice(n * CG, (n + 1) * CG)
                dve.wait_ge(s_y_sum, n + 1)
                link(V.tensor_tensor(acc[:, n % 2, :, :], y_in[0][:, ts, :], gate_b[:, b:b + 1, :].to_broadcast((T, CG, D)),
                                     ALU.mult))
                V.tensor_tensor(xs[:, ts, :], xs[:, ts, :], acc[:, n % 2, :, :], ALU.add).then_inc(s_res, 1)

        @block.tensor
        def _(pe):
            MM = nc.tensor.matmul
            pe.wait_ge(s_in0, 48)
            pe.wait_ge(s_csilu, 1)
            for k, j in enumerate((0, 1, 3, 4)):
                MM(ps[:, 0, k * B:(k + 1) * B], wmod[:, j, :], c_s[:], start=True, stop=True)
            pe.wait_ge(s_cb, 1)
            for bank, j in ((1, 2), (2, 5), (3, 3), (4, 4)):
                for b in range(B):
                    last = MM(ps[:, bank, b * D:(b + 1) * D], c_b[:, b, :], wmod[:, j, :], start=True, stop=True)
            last.then_inc(s_modps, 1)
            pe.wait_ge(s_mod, 1)
            pe.wait_ge(s_raw, 4)
            pe.wait_ge(s_in, 16 * 10)

            def turn(n):
                u = n % 2
                pe.wait_ge(s_xn, n + 1)
                pe.wait_ge(s_hT, n + 1)
                for j in range(CG):
                    last = nc.tensor.transpose(ps[:, u, j * T:(j + 1) * T], xn[:, n * CG + j, :], eye[:])
                last.then_inc(s_tp, 1)

            turn(0)
            turn(1)
            for n in range(2 * B):
                u = n % 2
                pe.wait_ge(s_hT, n + 3)
                for w, mat in enumerate((wq, wk)):
                    pe.wait_ge(s_prod, n * 2 + w + 1)
                    for j in range(2):
                        last = MM(ps[:, 2 + 2 * w + j, :], mat[:, j, :], hT[:, u, :], start=True, stop=True)
                    last.then_inc(s_qk, 1)
                for j in range(CG):
                    last = MM(ps[:, 6 + u, j * D:(j + 1) * D], hT[:, u, j * T:(j + 1) * T], wv[:], start=True, stop=True)
                last.then_inc(s_v, 1)
                if n + 2 < 2 * B:
                    turn(n + 2)

            def row_scores(m, bank, what):
                h, parts = PIECES[what]
                at = 0
                for q, k0, w, diag in parts:
                    last = MM(ps[:, bank, at:at + w], qa[m][0:KR, h * S + q * T:h * S + (q + 1) * T],
                              ka[m][0:KR, h * S + k0:h * S + k0 + w], start=True, stop=True)
                    at += w
                return last

            pe.wait_ge(s_wo, 1)

            def ring_write(i, r, bank, kind, off, what):
                m = (r + off) % 3
                if kind == "max":
                    if what == 0:
                        pe.wait_ge(s_qk_in[m], (third(i, r + off) + 1) * ((3 * NP - 1) * 16))
                    last = row_scores(m, bank, what)
                elif kind == "turn":
                    b, u = what // 2, what % 2
                    for j in range(CG):
                        last = nc.tensor.transpose(ps[:, bank, j * T:(j + 1) * T], o_rows[:, u * CG + j, b, :], eye[:])
                elif kind == "project":
                    b, u = what // 2, what % 2
                    turned = [x[1:] for x in plan_of(i, r)].index(("turn", 0, what))
                    pe.wait_ge(s_ring_free, ring_base(i, r) + (turned + 1))
                    for j in range(CG):
                        last = MM(ps[:, bank, j * D:(j + 1) * D], oT[:, u, j * T:(j + 1) * T], wo_gated[:, b, :],
                                  start=True, stop=True)
                elif kind == "shift":
                    pe.wait_ge(s_rowmax, quad(i, r + off) + 1)
                    last = nc.tensor.transpose(ps[0:HQ * TB, bank, 0:T],
                                               rowmax[m][:].rearrange("p h q -> p (h q)"), eye[:])
                else:
                    pe.wait_ge(s_outT, 2 * quad(i, r + off) + what + 1)
                    for j in range(CG):
                        last = nc.tensor.transpose(ps[:, bank, j * T:(j + 1) * T], outT[:, what, j * T:(j + 1) * T], eye[:])
                last.then_inc(s_ring, 1)

            pe.wait_ge(s_v_free, 2 * B)
            for k, (kind, off, what) in enumerate(PRE):
                if k >= RING:
                    pe.wait_ge(s_ring_free, k - RING + 1)
                ring_write(0, 0, 5 + k % RING, kind, off, what)

            def values_product(i, r, s):
                c, k, q0 = STEPS[s]
                n, m = quad(i, r), r % 3
                pe.wait_ge(s_exp, n * (2 * NS) + 2 * s + 2)
                if k >= CG * c:
                    diag = s if c == 0 else s - NS + 2 * CG
                    pe.wait_ge(s_mask, n * (2 * CG) + diag + 1)
                if s == 0:
                    pe.wait_ge(s_v4, n + 1)
                if k == 0 and not (isinstance(i, int) and n == 0 and c == 0):
                    pe.wait_ge(s_outT, 2 * n + c)
                for h in range(HQ):
                    last = MM(ps[VW * h:VW * (h + 1), 4, q0:CH], v4[m][:, k, h, :], probs[s % 4][:, h, 0:CH - q0],
                              start=(k == 0), stop=(k == CG * (c + 1) - 1))
                last.then_inc(s_pv, 1)

            def body(i, r):
                n, m = quad(i, r), r % 3
                first = isinstance(i, int) and n == 0
                plan = plan_of(i, r)
                rbase = ring_base(i, r)
                pe.wait_ge(s_m_in[m], (third(i, r) + 1) * (16 * NP))
                ks = [0]

                def ring_entries(slot):
                    while ks[0] < len(plan) and plan[ks[0]][0] <= slot:
                        k = ks[0]
                        _, kind, off, what = plan[k]
                        pe.wait_ge(s_ring_free, rbase + (k + 1 - RING))
                        ring_write(i, r, 5 + ring_bank(i, r, k), kind, off, what)
                        ks[0] += 1

                for s, (c, kb, q0) in enumerate(STEPS):
                    for h in range(HQ):
                        if h % 2 == 0 and not (first and s == 0):
                            pe.wait_ge(s_exp, n * (2 * NS) + 2 * s + h // 2 - 1)
                        last = MM(ps[:, h, q0:CH], ka[m][0:KM, h * S + kb * T:h * S + (kb + 1) * T],
                                  qa[m][0:KM, h * S + c * CH + q0:h * S + (c + 1) * CH], start=True, stop=True)
                        if h % 2:
                            last.then_inc(s_scores, 1)
                            ring_entries(s * SLOTS + h // 2)
                    if s >= 2:
                        values_product(i, r, s - 2)
                    elif not first:
                        values_product(i, r - 1, NS - 2 + s)
                    ring_entries(s * SLOTS + 2)
            quads(pe, body)
            values_product(5, 0, NS - 2)
            values_product(5, 0, NS - 1)
            endbase = ring_base(5, 1)
            pe.wait_ge(s_ring_free, endbase + 1 - RING)
            ring_write(5, 1, 5 + endbase % RING, "norm", -1, 1)
            pe.wait_ge(s_ring_free, ring_base(0, NQ) + 1)

            b = B - 1
            for u in range(2):
                for j in range(CG):
                    last = nc.tensor.transpose(ps[:, u, j * T:(j + 1) * T],
                                               o_rows[:, u * CG + j, b, :], eye[:])
                last.then_inc(s_ot, 1)
            for u in range(2):
                pe.wait_ge(s_oT, u + 1)
                for j in range(CG):
                    last = MM(ps[:, 2 + u, j * D:(j + 1) * D], oT[:, u, j * T:(j + 1) * T], wo_gated[:, b, :], start=True, stop=True)
                last.then_inc(s_proj, 1)

            def turn_normalised(n):
                u = n % 2
                pe.wait_ge(s_xn2, n + 1)
                needs(pe, s_h2_hi, n - 1)
                for j in range(CG):
                    last = nc.tensor.transpose(ps[:, 4 + u, j * T:(j + 1) * T], xn[:, n * CG + j, :], eye[:])
                last.then_inc(s_tp2, 1)

            turn_normalised(0)
            turn_normalised(1)
            for n in range(2 * B):
                u = n % 2
                pe.wait_ge(s_hT2, n + 1)
                pe.wait_ge(s_lg_free, n + 1)
                for j in range(CG):
                    last = MM(ps[:, 6 + u, j * NE:(j + 1) * NE], hT[:, u, j * T:(j + 1) * T], wr[:], start=True, stop=True)
                last.then_inc(s_lg, 1)
                if n + 2 < 2 * B:
                    turn_normalised(n + 2)

            pe.wait_ge(s_sel, 1)
            for name, at in (("before", 0), ("ones", 1)):
                c0, w = CST[name]
                last = MM(ps[:, 2, at * NT * NE:(at + 1) * NT * NE], cst[:, c0:c0 + w],
                          sel[:].rearrange("p t e -> p (t e)"), start=True, stop=True)
            last.then_inc(s_prefix, 1)

            pe.wait_ge(s_expert, 1)
            pe.wait_ge(s_split2, 2 * B)
            pe.wait_ge(s_wlo, 1)
            pe.wait_ge(s_wd, 16 * len(IC))

            def gate_up(b, u):
                n = b * 2 + u
                cols = bass.ds(n * CH, CH)
                for c, (i0, w) in enumerate(IC):
                    pe.wait_ge(s_hid, n * len(IC) + c + 1)
                    for g in range(2):
                        trio = ((w_hi, h2_hi), (w_lo, h2_hi), (w_hi, h2_lo))
                        for k, (wt, ht) in enumerate(trio):
                            last = MM(ps[0:w, 2 * c + g, :], wt[:, 0, g, i0:i0 + w], ht[:, cols],
                                      start=(k == 0), stop=(k == 2))
                    last.then_inc(s_gu, 1)

            def down(n, u):
                pe.wait_ge(s_hid, (n + 2) * len(IC))
                pe.wait_ge(s_dn_free, n + 1)
                for j in range(CG):
                    for c, (i0, w) in enumerate(IC):
                        last = MM(ps[:, 6, j * D:(j + 1) * D], hid[0:w, u, c, j * T:(j + 1) * T],
                                  wd[0:w, 0, c, :], start=(c == 0), stop=(c == len(IC) - 1))
                last.then_inc(s_dn, 1)

            with pe.Fori(0, B) as b:
                for u in range(2):
                    gate_up(b, u)
                    down(b * 2 + u, u)

            pe.wait_ge(s_shared, 2 * B)
            pe.wait_ge(s_wlo, EX)

            known = {}

            def expert_of(i, t, r):
                if r in known and r >= 0 and known[r][0] is i:
                    return known[r][1]
                known[r] = i, load_expert(t)
                return known[r][1]

            def load_expert(t):
                return pe.value_load(expert[0:1, bass.ds(t, 1)], min_val=1, max_val=NE)

            def slot_step(i, r):
                at = tile(i, r, -1)
                if at:
                    t, j, times = at
                    t2 = j % 2
                    pe.wait_ge(s_srow[j], 16 * times + 16)
                    needs(pe, s_h_lo, t)
                    nc.tensor.transpose(ps[:, 0, 0:T], srow[:, j, 0:D], eye[:]).then_inc(s_rowT, 1)
                at = tile(i, r, 0)
                if at:
                    t, j, _ = at
                    t2 = j % 2
                    e = expert_of(i, t, r)
                    if isinstance(t, int) and t == ST - 1:
                        pe.wait_ge(s_h_lo, t + 1)
                    for k, (ht, wt) in enumerate(((h_hi, w_hi), (h_hi, w_lo), (h_lo, w_hi))):
                        for g in range(2):
                            last = MM(ps[:, 1 + 2 * t2 + g, 0:NI], ht[:, t2, :], wt[:, bass.ds(e, 1), g, :],
                                      start=(k == 0), stop=(k == 2))
                    last.then_inc(s_sgu, 1)
                at = tile(i, r, 2)
                if at:
                    t, j, _ = at
                    t2 = j % 2
                    e = expert_of(i, t, r - 2)
                    pe.wait_ge(s_hidT, t + 1)
                    needs(pe, s_y, t)
                    for c, (i0, w) in enumerate(IC):
                        last = MM(ps[:, 6, 0:D], hidT[0:w, t2, c, :], wd[0:w, bass.ds(e, 1), c, :],
                                  start=(c == 0), stop=(c == len(IC) - 1))
                    last.then_inc(s_sdn, 1)
                at = tile(i, r, 1)
                if at:
                    t, j, _ = at
                    t2 = j % 2
                    pe.wait_ge(s_shid, t + 1)
                    for c, (i0, w) in enumerate(IC):
                        last = nc.tensor.transpose(ps[0:w, 5, c * T:(c + 1) * T], hid_s[:, t2, i0:i0 + w], eye[:])
                    last.then_inc(s_shidT, 1)
            slot_steps(pe, -1, ST + 1, slot_step)


_INS = ["x", "wq", "wk", "wv", "wo", "gate", "up", "down", "wr", "rb", "c", "wmod", "cos", "sin", "eye", "tri", "cst"]


def kernel(L0_attn_x, L0_attn_W_q, L0_attn_W_k, L0_attn_W_v, L0_attn_W_o, L0_ffn_sg, L0_ffn_su, L0_ffn_sd,
           L0_ffn_rg, L0_ffn_ru, L0_ffn_rd, L0_ffn_wr, L0_ffn_rb, L0_c, L0_wmod):
    import concourse.bacc as bacc
    from concourse.bass_utils import run_bass_kernel_spmd

    def rows(w, swap):
        w = np.asarray(w).reshape(NG, HQ, DK, D)
        if swap:
            w = w[:, :, [d ^ 1 for d in range(DK)], :]
        return w.transpose(0, 2, 1, 3).reshape(D, D).T

    def both(w):
        return np.stack([rows(w, False), rows(w, True)])

    freq = np.float32(10000.0) ** (np.float32(-2.0) * np.arange(DK // 2, dtype=np.float32) / np.float32(DK))
    ang = np.arange(S, dtype=np.float32)[:, None] * freq[None, :].astype(np.float32)
    dim = (np.arange(D) // HQ) % DK
    cos = np.cos(ang)[:, dim // 2].T
    sin = np.sin(ang)[:, dim // 2].T * np.where(dim % 2 == 0, -1.0, 1.0)[:, None]
    tri = np.zeros((T, CH), np.float32)
    tri[:, CH - T:] = np.where(np.arange(T)[None, :] > np.arange(T)[:, None], LOW, 0.0)

    cst = {"before": np.arange(T)[:, None] < np.arange(T)[None, :], "ones": np.ones((T, T)),
           "steps": np.tile(T * np.arange(NT), (T, 1)), "tiles": np.tile(np.arange(ST), (T, 1)),
           "token": np.arange(T)[:, None] + T * np.arange(NT)[None, :] - TOP * B * S,
           "pad": np.zeros((T, RW)),
           "spare": TOP * B * S + np.arange(T)[:, None] + T * np.arange(ST)[None, :]}
    cst = np.concatenate([cst[name] for name in CST], axis=1).astype(np.float32)

    def experts(shared, routed):
        return np.concatenate([np.asarray(shared)[None], np.asarray(routed)])

    vals = [
        np.asarray(L0_attn_x).reshape(B * S, D), both(L0_attn_W_q), both(L0_attn_W_k),
        np.asarray(L0_attn_W_v).T, np.asarray(L0_attn_W_o).T,
        experts(L0_ffn_sg, L0_ffn_rg).transpose(0, 2, 1), experts(L0_ffn_su, L0_ffn_ru).transpose(0, 2, 1),
        experts(L0_ffn_sd, L0_ffn_rd).transpose(0, 2, 1), np.asarray(L0_ffn_wr).T,
        np.asarray(L0_ffn_rb).reshape(1, NE), np.asarray(L0_c).T, np.asarray(L0_wmod),
        cos.astype(np.float32), sin.astype(np.float32), np.eye(128, dtype=np.float32), tri, cst,
    ]
    nc = bacc.Bacc("TRN2", target_bir_lowering=False, num_devices=1)
    arrays, args = {}, []
    for name, a in zip(_INS, vals):
        a = np.ascontiguousarray(a)
        arrays[f"in_{name}"] = a
        args.append(nc.dram_tensor(f"in_{name}", a.shape, mybir.dt.from_np(a.dtype), kind="ExternalInput").ap())
    out = nc.dram_tensor("out", (B * S, D), F32, kind="ExternalOutput").ap()
    adaln_block(nc, *args, out)
    r = run_bass_kernel_spmd(nc, [arrays], core_ids=[0])
    return r.results[0]["out"].reshape(B, S, D)
```
